# Optimizing a Trainium2 kernel written in Bass

```python
import numpy as np
import jax
import jax.numpy as jnp

def _softmax(x, axis=-1):
    return jax.nn.softmax(x, axis=axis)

def _gelu(x):
    return jax.nn.gelu(x, approximate=True)

def _silu(x):
    return jax.nn.silu(x)

def _sigmoid(x):
    return jax.nn.sigmoid(x)

def _layernorm(x, axis=-1, eps=1e-05):
    m = jnp.mean(x, axis=axis, keepdims=True)
    v = jnp.var(x, axis=axis, keepdims=True)
    return (x - m) / jnp.sqrt(v + eps)

def _scatter_add(tgt, idx, src, axis=0):
    return tgt.at[idx].add(src)

def _segment_sum(src, seg, n):
    return jax.ops.segment_sum(src, seg, n)
kernel_name = 'mk_early_fusion_d1_tok_img1024_r4_94aa29'

def setup_inputs(seed: int=0):
    np.random.seed(seed)
    _w = jnp.asarray

    def _rec_inputs():
        import jax
        import jax.numpy as jnp
        _rk = jax.random.key(seed)
        x = -4.65018e-05 + 0.999886 * jax.random.normal(jax.random.fold_in(_rk, 1), (8, 3, 128, 128), jnp.float32)
        txt = 0.419162 + 1.15059 * jax.random.normal(jax.random.fold_in(_rk, 2), (8, 77, 256), jnp.float32)
        return (x, txt)
    x, txt = _rec_inputs()

    def _L0_tok_setup():
        import jax, jax.numpy as jnp
        import numpy as np
        IMG_H = 128
        IMG_W = 128
        C = 3
        PH = 16
        PW = 16
        HID = 256
        NH = IMG_H // PH
        NW = IMG_W // PW
        PD = C * PH * PW
        BATCH = 64

        def sinusoidal_pos_embed(embed_dim, grid_size_x, grid_size_y):
            gh = jnp.arange(grid_size_y)
            gw = jnp.arange(grid_size_x)
            grid = jnp.stack(jnp.meshgrid(gh, gw, indexing='ij'), axis=0)
            h_pos = grid[0].reshape(-1).astype(jnp.float32)
            w_pos = grid[1].reshape(-1).astype(jnp.float32)
            quarter = embed_dim // 4
            factor = 10000.0 ** (jnp.arange(quarter, dtype=jnp.float32) / quarter)
            h = h_pos[:, None] / factor
            w = w_pos[:, None] / factor
            return jnp.concatenate([jnp.sin(h), jnp.cos(h), jnp.sin(w), jnp.cos(w)], axis=-1)
        key = jax.random.key(seed)
        k1, k2 = jax.random.split(key, 2)
        x = jax.random.normal(k1, (BATCH, C, IMG_H, IMG_W), dtype=jnp.float32)
        Wp = jax.random.normal(k2, (HID, PD), dtype=jnp.float32) * (1.0 / np.sqrt(PD))
        b = jnp.zeros((HID,), dtype=jnp.float32)
        return {'x': x, 'Wp': Wp, 'b': b}
    _L0_tok_all = _L0_tok_setup()
    _L0_tok_in = {k: v for k, v in _L0_tok_all.items() if k in ('Wp', 'b')}
    del _L0_tok_all

    def _L0_attn_setup():
        import jax, jax.numpy as jnp
        import numpy as np
        B, N, DIM, H = (4, 1024, 256, 16)
        HD = DIM // H
        SCALE = HD ** (-0.5)

        def _heads(t, bsz, ntok):
            return t.reshape(bsz, ntok, H, HD).transpose(0, 2, 1, 3)

        def _fwd(x, q_w1, q_b1, q_w2, q_b2, k_w1, k_b1, k_w2, k_b2, v_w, v_b, g_w, g_b, p_w, p_b):
            bsz, ntok, dim = x.shape
            gelu = lambda t: jax.nn.gelu(t, approximate=False)
            q = _heads(jax.nn.softplus(gelu(x @ q_w1.T + q_b1) @ q_w2.T + q_b2), bsz, ntok)
            k = _heads(jax.nn.softplus(gelu(x @ k_w1.T + k_b1) @ k_w2.T + k_b2), bsz, ntok)
            v = _heads(gelu(x @ v_w.T + v_b), bsz, ntok)
            g = _heads(gelu(x @ g_w.T + g_b), bsz, ntok)
            z = jnp.einsum('bhcn,bhc->bhn', q, k.sum(axis=-1)) * SCALE
            z = 1.0 / (z + dim)
            A = jnp.einsum('bhcn,bhcm->bhnm', q, k)
            out = jnp.einsum('bhnm,bhdm->bhdn', A, v) * SCALE
            out = (out + v) * z[:, :, None, :]
            out = out.reshape(bsz, ntok, dim)
            out = out * g.reshape(bsz, ntok, dim)
            return out @ p_w.T + p_b
        key = jax.random.key(seed)
        ks = jax.random.split(key, 16)
        w = lambda k: jax.random.normal(k, (DIM, DIM), jnp.float32) * 0.02
        b = lambda k: jax.random.normal(k, (DIM,), jnp.float32) * 0.02
        return {'x': jax.random.normal(ks[0], (B, N, DIM), jnp.float32), 'q_w1': w(ks[1]), 'q_b1': b(ks[2]), 'q_w2': w(ks[3]), 'q_b2': b(ks[4]), 'k_w1': w(ks[5]), 'k_b1': b(ks[6]), 'k_w2': w(ks[7]), 'k_b2': b(ks[8]), 'v_w': w(ks[9]), 'v_b': b(ks[10]), 'g_w': w(ks[11]), 'g_b': b(ks[12]), 'p_w': w(ks[13]), 'p_b': b(ks[14])}
    _L0_attn_all = _L0_attn_setup()
    _L0_attn_in = {k: v for k, v in _L0_attn_all.items() if k in ('q_w1', 'q_b1', 'q_w2', 'q_b2', 'k_w1', 'k_b1', 'k_w2', 'k_b2', 'v_w', 'v_b', 'g_w', 'g_b', 'p_w', 'p_b')}
    del _L0_attn_all

    def _L0_ffn_setup():
        import jax, jax.numpy as jnp
        import numpy as np
        B, T, C = (4, 512, 256)
        E = 8
        K = 2
        H = 352
        HS = 352 * 2
        key = jax.random.key(seed)
        k = jax.random.split(key, 8)
        s = 0.02
        return {'x': jax.random.normal(k[0], (B, T, C), jnp.float32), 'Wg': jax.random.normal(k[1], (C, E), jnp.float32) * s, 'W1': jax.random.normal(k[2], (E, C, H), jnp.float32) * s, 'W2': jax.random.normal(k[3], (E, C, H), jnp.float32) * s, 'W3': jax.random.normal(k[4], (E, H, C), jnp.float32) * s, 'Ws1': jax.random.normal(k[5], (C, HS), jnp.float32) * s, 'Ws2': jax.random.normal(k[6], (C, HS), jnp.float32) * s, 'Ws3': jax.random.normal(k[7], (HS, C), jnp.float32) * s}
    _L0_ffn_all = _L0_ffn_setup()
    _L0_ffn_in = {k: v for k, v in _L0_ffn_all.items() if k in ('Wg', 'W1', 'W2', 'W3', 'Ws1', 'Ws2', 'Ws3')}
    del _L0_ffn_all
    return {'x': x, 'txt': txt, 'L0_tok_Wp': _L0_tok_in['Wp'], 'L0_tok_b': _L0_tok_in['b'], 'L0_attn_q_w1': _L0_attn_in['q_w1'], 'L0_attn_q_b1': _L0_attn_in['q_b1'], 'L0_attn_q_w2': _L0_attn_in['q_w2'], 'L0_attn_q_b2': _L0_attn_in['q_b2'], 'L0_attn_k_w1': _L0_attn_in['k_w1'], 'L0_attn_k_b1': _L0_attn_in['k_b1'], 'L0_attn_k_w2': _L0_attn_in['k_w2'], 'L0_attn_k_b2': _L0_attn_in['k_b2'], 'L0_attn_v_w': _L0_attn_in['v_w'], 'L0_attn_v_b': _L0_attn_in['v_b'], 'L0_attn_g_w': _L0_attn_in['g_w'], 'L0_attn_g_b': _L0_attn_in['g_b'], 'L0_attn_p_w': _L0_attn_in['p_w'], 'L0_attn_p_b': _L0_attn_in['p_b'], 'L0_ffn_Wg': _L0_ffn_in['Wg'], 'L0_ffn_W1': _L0_ffn_in['W1'], 'L0_ffn_W2': _L0_ffn_in['W2'], 'L0_ffn_W3': _L0_ffn_in['W3'], 'L0_ffn_Ws1': _L0_ffn_in['Ws1'], 'L0_ffn_Ws2': _L0_ffn_in['Ws2'], 'L0_ffn_Ws3': _L0_ffn_in['Ws3']}

def reference(x, txt, L0_tok_Wp, L0_tok_b, L0_attn_q_w1, L0_attn_q_b1, L0_attn_q_w2, L0_attn_q_b2, L0_attn_k_w1, L0_attn_k_b1, L0_attn_k_w2, L0_attn_k_b2, L0_attn_v_w, L0_attn_v_b, L0_attn_g_w, L0_attn_g_b, L0_attn_p_w, L0_attn_p_b, L0_ffn_Wg, L0_ffn_W1, L0_ffn_W2, L0_ffn_W3, L0_ffn_Ws1, L0_ffn_Ws2, L0_ffn_Ws3):
    import jax
    import jax.numpy as jnp

    def _L0_tok_ref(x, Wp, b):
        import jax, jax.numpy as jnp
        import numpy as np
        IMG_H = 128
        IMG_W = 128
        C = 3
        PH = 16
        PW = 16
        HID = 256
        NH = IMG_H // PH
        NW = IMG_W // PW
        PD = C * PH * PW
        BATCH = 64

        def sinusoidal_pos_embed(embed_dim, grid_size_x, grid_size_y):
            gh = jnp.arange(grid_size_y)
            gw = jnp.arange(grid_size_x)
            grid = jnp.stack(jnp.meshgrid(gh, gw, indexing='ij'), axis=0)
            h_pos = grid[0].reshape(-1).astype(jnp.float32)
            w_pos = grid[1].reshape(-1).astype(jnp.float32)
            quarter = embed_dim // 4
            factor = 10000.0 ** (jnp.arange(quarter, dtype=jnp.float32) / quarter)
            h = h_pos[:, None] / factor
            w = w_pos[:, None] / factor
            return jnp.concatenate([jnp.sin(h), jnp.cos(h), jnp.sin(w), jnp.cos(w)], axis=-1)
        B = x.shape[0]
        p = x.reshape(B, C, NH, PH, NW, PW)
        p = p.transpose(0, 2, 4, 3, 5, 1)
        p = p.reshape(B, NH * NW, PH * PW * C)
        out = jnp.einsum('bnd,hd->bnh', p, Wp) + b
        pos = sinusoidal_pos_embed(HID, NW, NH)
        return out + pos

    def _L0_attn_ref(x, q_w1, q_b1, q_w2, q_b2, k_w1, k_b1, k_w2, k_b2, v_w, v_b, g_w, g_b, p_w, p_b):
        import jax, jax.numpy as jnp
        import numpy as np
        B, N, DIM, H = (4, 1024, 256, 16)
        HD = DIM // H
        SCALE = HD ** (-0.5)

        def _heads(t, bsz, ntok):
            return t.reshape(bsz, ntok, H, HD).transpose(0, 2, 1, 3)

        def _fwd(x, q_w1, q_b1, q_w2, q_b2, k_w1, k_b1, k_w2, k_b2, v_w, v_b, g_w, g_b, p_w, p_b):
            bsz, ntok, dim = x.shape
            gelu = lambda t: jax.nn.gelu(t, approximate=False)
            q = _heads(jax.nn.softplus(gelu(x @ q_w1.T + q_b1) @ q_w2.T + q_b2), bsz, ntok)
            k = _heads(jax.nn.softplus(gelu(x @ k_w1.T + k_b1) @ k_w2.T + k_b2), bsz, ntok)
            v = _heads(gelu(x @ v_w.T + v_b), bsz, ntok)
            g = _heads(gelu(x @ g_w.T + g_b), bsz, ntok)
            z = jnp.einsum('bhcn,bhc->bhn', q, k.sum(axis=-1)) * SCALE
            z = 1.0 / (z + dim)
            A = jnp.einsum('bhcn,bhcm->bhnm', q, k)
            out = jnp.einsum('bhnm,bhdm->bhdn', A, v) * SCALE
            out = (out + v) * z[:, :, None, :]
            out = out.reshape(bsz, ntok, dim)
            out = out * g.reshape(bsz, ntok, dim)
            return out @ p_w.T + p_b
        return _fwd(x, q_w1, q_b1, q_w2, q_b2, k_w1, k_b1, k_w2, k_b2, v_w, v_b, g_w, g_b, p_w, p_b)

    def _L0_ffn_ref(x, Wg, W1, W2, W3, Ws1, Ws2, Ws3):
        import jax, jax.numpy as jnp
        import numpy as np
        B, T, C = (4, 512, 256)
        E = 8
        K = 2
        H = 352
        HS = 352 * 2
        b, t, c = x.shape
        xf = x.reshape(-1, c)
        n = xf.shape[0]
        router = xf @ Wg
        top_logits, idx = jax.lax.top_k(router, K)
        probs = jax.nn.softmax(top_logits.astype(jnp.float32), axis=-1).astype(x.dtype)
        w = jnp.zeros((n, E), x.dtype).at[jnp.arange(n)[:, None], idx].add(probs)
        h = jax.nn.silu(jnp.einsum('tc,ech->eth', xf, W1)) * jnp.einsum('tc,ech->eth', xf, W2)
        y = jnp.einsum('eth,ehc,te->tc', h, W3, w)
        y = y.reshape(b, t, c)
        hs = jax.nn.silu(xf @ Ws1) * (xf @ Ws2)
        y = y + (hs @ Ws3).reshape(b, t, c)
        return y
    h = _L0_tok_ref(x, L0_tok_Wp, L0_tok_b)
    h = jnp.concatenate([h, txt], axis=1)
    h = h + _L0_attn_ref(_layernorm(h, axis=-1), L0_attn_q_w1, L0_attn_q_b1, L0_attn_q_w2, L0_attn_q_b2, L0_attn_k_w1, L0_attn_k_b1, L0_attn_k_w2, L0_attn_k_b2, L0_attn_v_w, L0_attn_v_b, L0_attn_g_w, L0_attn_g_b, L0_attn_p_w, L0_attn_p_b)
    h = h + _L0_ffn_ref(_layernorm(h, axis=-1), L0_ffn_Wg, L0_ffn_W1, L0_ffn_W2, L0_ffn_W3, L0_ffn_Ws1, L0_ffn_Ws2, L0_ffn_Ws3)
    return h

_drawn_inputs = setup_inputs


def setup_inputs(seed=0):
    import zlib

    import numpy as np

    out = dict(_drawn_inputs(seed))
    spreads = {'L0_tok_b': (0.0, 0.1)}
    factors = {'L0_attn_q_w1': 8.0,
     'L0_attn_q_b1': 22.277,
     'L0_attn_q_w2': 8.0,
     'L0_attn_q_b2': 31.859,
     'L0_attn_k_w1': 8.0,
     'L0_attn_k_b1': 8.0,
     'L0_attn_k_w2': 8.0,
     'L0_attn_k_b2': 22.394,
     'L0_attn_v_w': 8.0,
     'L0_attn_v_b': 8.0,
     'L0_attn_g_w': 8.0,
     'L0_attn_g_b': 8.0,
     'L0_attn_p_w': 8.0,
     'L0_attn_p_b': 3.545,
     'L0_ffn_Wg': 5.79,
     'L0_ffn_W1': 4.945,
     'L0_ffn_W2': 4.886,
     'L0_ffn_W3': 4.897,
     'L0_ffn_Ws1': 8.0,
     'L0_ffn_Ws2': 8.0,
     'L0_ffn_Ws3': 8.0}
    for name, (base, spread) in spreads.items():
        noise = np.random.default_rng([zlib.crc32(name.encode()), seed]).standard_normal(out[name].shape)
        drawn = base * np.exp(spread * noise) if base else spread * noise
        out[name] = jnp.asarray(drawn.astype(out[name].dtype))
    for name, factor in factors.items():
        out[name] = (out[name] * factor).astype(out[name].dtype)
    return out
```

```python
from contextlib import ExitStack

import concourse.bass as bass
from concourse import mybir

F32 = mybir.dt.float32
U32 = mybir.dt.uint32
ALU = mybir.AluOpType
ACT = mybir.ActivationFunctionType
AX_X = mybir.AxisListType.X

P = 128
B, CH, IMG = 8, 3, 128
PATCH = 16
NP = (IMG // PATCH) ** 2
NT = 77
N = NP + NT
T = B * N
C = 256
KC = C // P
PD = CH * PATCH * PATCH
KP = PD // P
HEADS, HD = 16, 16
SCALE = float(HD) ** -0.5
EPS = 1e-5
E = 8
H = 352
HS = 704
KH = -(-H // P)
KS = -(-HS // P)
NCH = 3
CW = T // NCH
TI = B // 2
TA = TI + B
XS = 8
TF = -(-T // P)
LAST = T - (TF - 1) * P
SLOTS = (2 * T + E * (P - 1)) // P
ROW = C + 4
NOBODY = 4096.0
BIG = 3.0e38


def rows_of(i):
    return P if i < TF - 1 else LAST


def fused_layer(nc, x, txt, Wp, tok_b, q_w1, q_b1, q_w2, q_b2, k_w1, k_b1, k_w2, k_b2, v_w, v_b,
                g_w, g_b, p_w, p_b, Wg, W1, W2, W3, Ws1, Ws2, Ws3, pos, out):
    h_dram = nc.dram_tensor("h_dram", [T, C], F32, kind="Internal").ap()
    mix_dram = nc.dram_tensor("mix_dram", [B, HEADS * N * HD], F32, kind="Internal").ap()
    slot_dram = nc.dram_tensor("slot_dram", [SLOTS * P, ROW], F32, kind="Internal").ap()
    out2d = out.rearrange("b t c -> (b t) c")

    with ExitStack() as ctx:
        at = [-(-nc.sbuf_base // 32) * 32]

        def place(name, shape, dt=F32, where=None):
            size = 4
            for n in shape[1:]:
                size *= n
            size = -(-size // 32) * 32
            off = at[0] if where is None else where[0]
            t = nc.alloc_sbuf_tensor_at(name, shape, dt, offset=off)
            if where is None:
                at[0] += size
            else:
                where[0] += size
                assert where[0] <= where[1], (name, where)
            return t

        def sem(name):
            return ctx.enter_context(nc.semaphore(name))

        e0 = at[0]
        w12 = place("w12", [P, E, KC, 2 * H])
        w3 = place("w3", [P, E, KH, C])
        under = [e0, at[0]]
        xst = place("xst", [P, CH, PATCH * IMG // 2], where=under)
        xrs = place("xrs", [P, CH, PATCH * IMG // 2], where=under)
        wpn = place("wpn", [P, KC, PD], where=under)
        wpT = place("wpT", [P, KP, C], where=under)
        patchT = place("patchT", [P, KP, B * NP], where=under)
        wnat = place("wnat", [P, 7, KC, C], where=under)
        w0 = at[0]
        wT = place("wT", [P, 7, KC, C])
        xs = place("xs", [P, XS, C], where=[w0, w0 + 4 * KC * C * 4])
        QW1, KW1, VW, GW, QW2, KW2, PW = range(7)
        a0 = at[0]
        xT = place("xT", [P, KC, T])
        q1T = place("q1T", [P, KC, T])
        k1T = place("k1T", [P, KC, T])
        vT = place("vT", [P, KC, T])
        over = [a0, at[0]]
        h2 = place("h2", [P, TF, C], where=over)
        xn2 = place("xn2", [P, TF, ROW], where=over)
        x2T = place("x2T", [P, KC, T], where=over)
        sil = place("sil", [P, 2, CW], where=over)
        lg = place("lg", [P, TF, E], where=over)
        lg2 = place("lg2", [P, TF, E], where=over)
        eq = place("eq", [P, TF, E], where=over)
        oh1 = place("oh1", [P, TF, E], where=over)
        oh2 = place("oh2", [P, TF, E], where=over)
        both = place("both", [P, TF, E], where=over)
        m1 = place("m1", [P, TF], where=over)
        m2 = place("m2", [P, TF], where=over)
        mx1 = place("mx1", [P, TF], where=over)
        mx2 = place("mx2", [P, TF], where=over)
        dif = place("dif", [P, TF], where=over)
        ex = place("ex", [P, TF], where=over)
        exs = place("exs", [P, TF], where=over)
        cnt = place("cnt", [P, E], where=over)
        cmpt = place("cmpt", [P, E, TF], where=over)
        ntl = place("ntl", [P, E], where=over)
        cume = place("cume", [P, E, E], where=over)
        base = place("base", [P, E], where=over)
        upto = place("upto", [P, E], where=over)
        cmps = place("cmps", [P, SLOTS, E], where=over)
        esl = place("esl", [P, SLOTS], where=over)
        esu = place("esu", [P, SLOTS], U32, where=over)
        adr = place("adr", [P, TF, E], where=over)
        prd = place("prd", [P, 2, TF, E], where=over)
        posf = place("posf", [P, 2, TF], where=over)
        posu = place("posu", [P, 2, TF], U32, where=over)
        g0 = at[0]
        g = place("g", [P, TA, C])
        qk = place("qk", [P, 2, 3, 2 * C])
        spy = place("spy", [P, 2, 2 * C])
        spa = place("spa", [P, 2, 2 * C])
        mm2 = place("mm2", [P, 2, C])
        mz = place("mz", [P, 2, C])
        mm3 = place("mm3", [P, 2, C])
        ogi = place("ogi", [P, 2, C])
        ogt = place("ogt", [P, 2, C])
        over = [g0, at[0]]
        hsT = place("hsT", [P, KS, T], where=over)
        sl_x = place("sl_x", [P, 2, C], where=over)
        sl_xT = place("sl_xT", [P, 2, C], where=over)
        sl_s = place("sl_s", [P, 2, H], where=over)
        sl_h = place("sl_h", [P, 2, H], where=over)
        sl_hT = place("sl_hT", [P, 2, KH * P], where=over)
        sl_y = place("sl_y", [P, 2, C], where=over)
        n0 = at[0]
        xn = place("xn", [P, TA, C])
        hI = place("hI", [P, TI, C])
        tx = place("tx", [P, B, C])
        at[0] += 2048
        over = [n0, at[0]]
        ws12 = place("ws12", [P, KC, 2 * HS], where=over)
        ws3 = place("ws3", [P, KS, C], where=over)
        hb = place("hb", [P, TF, C], where=over)
        xsT = place("xsT", [P, 2, C])
        ident = place("ident", [P, P])
        ones = place("ones", [P, P])
        before = place("before", [P, P])
        blocks = place("blocks", [P, KC, P])
        ident2 = place("ident2", [P, KC, P])
        posb = place("posb", [P, C])
        tokb = place("tokb", [P, C])
        gb = place("gb", [P, C])
        qkb = place("qkb", [P, 2 * C])
        pb = place("pb", [P, C])
        cb = place("cb", [P, 3, KC])
        wg = place("wg", [P, KC, E])
        eps = place("eps", [P, 1])
        empty = place("empty", [P, ROW])
        st = place("st", [P, TA, 6])
        mv = place("mv", [P, TA, 2])
        rs = place("rs", [P, TA])
        rs2 = place("rs2", [P, TA])
        e_up = place("e_up", [P, E])
        e_dn = place("e_dn", [P, E])
        e_lt = place("e_lt", [P, E, E])
        tile_at = place("tile_at", [P, TF])
        slot_no = place("slot_no", [P, SLOTS])
        tok_no = place("tok_no", [P, TF])
        tail = place("tail", [P, SLOTS, ROW - C])
        dg = place("dg", [P, SLOTS])
        own = place("own", [P, SLOTS])
        gate = place("gate", [P, SLOTS])
        idx = place("idx", [P, SLOTS], U32)
        assert at[0] <= nc.sbuf_usable_end, at[0]

        ps = ctx.enter_context(nc.psum_tensor("ps", [P, 8, 512], F32))

        ld_wp, ld_x, ld_tx, ld_wn = sem("ld_wp"), sem("ld_x"), sem("ld_tx"), sem("ld_wn")
        ld_b, ld_ws, ld_we = sem("ld_b"), sem("ld_ws"), sem("ld_we")
        ld_xs = [sem(f"ld_xs{i}") for i in range(TF)]
        ld_hb = sem("ld_hb")
        ld_tail = sem("ld_tail")
        h_out, slot_zero = sem("h_out"), sem("slot_zero")
        mix_out = [sem(f"mix_out{b}") for b in range(B)]
        slot_out, out_init = sem("slot_out"), sem("out_init")
        sl_ld = [sem(f"sl_ld{i}") for i in range(2)]
        sl_add = sem("sl_add")
        k_set, k_ready, k_empty, w3_z = sem("k_set"), sem("k_ready"), sem("k_empty"), sem("w3_z")
        wp_t, wp_c, x_t, x_c = sem("wp_t"), sem("wp_c"), sem("x_t"), sem("x_c")
        xr_a, xr_d = sem("xr_a"), sem("xr_d")
        posb_r, emb, hi_r = sem("posb_r"), sem("emb"), sem("hi_r")
        w_t, w_c = sem("w_t"), sem("w_c")
        st_r, mv_r, sd_r, rs_r, xn_r, xn_t, xn_c = (sem(n) for n in ("st_r", "mv_r", "sd_r", "rs_r", "xn_r", "xn_t", "xn_c"))
        p1, p1_c, pg, pg_b, pg_c = (sem(n) for n in ("p1", "p1_c", "pg", "pg_b", "pg_c"))
        sp, sp_y, sp_a, sp_e, sp_l, sp_q = (sem(n) for n in ("sp", "sp_y", "sp_a", "sp_e", "sp_l", "sp_q"))
        at_a, at_m, at_m2, at_z, at_zb, at_r, at_m3, at_o, at_g = (
            sem(n) for n in ("at_a", "at_m", "at_m2", "at_z", "at_zb", "at_r", "at_m3", "at_o", "at_g"))
        hb_r, xs_t, xs_c, y_p, h2_r, st2, mv2, sd2, rs2_r, n2, n2_t, n2_c, r_l, lg_r, lg_z = (
            sem(n) for n in ("hb_r", "xs_t", "xs_c", "y_p", "h2_r", "st2", "mv2", "sd2", "rs2_r", "n2",
                             "n2_t", "n2_c", "r_l", "lg_r", "lg_z"))
        rt, rt_both, rt_pre, rt_dif, rt_ex, rt_done, rt_row = (
            sem(n) for n in ("rt", "rt_both", "rt_pre", "rt_dif", "rt_ex", "rt_done", "rt_row"))
        s_up, s_sil, s_h, s_dn, s_o = (sem(n) for n in ("s_up", "s_sil", "s_h", "s_dn", "s_o"))
        sl_tx, sl_xc, sl_a, sl_b, sl_si, sl_hr, sl_th, sl_hc, sl_yp, sl_yr, sl_d, sl_g = (
            sem(n) for n in ("sl_tx", "sl_xc", "sl_a", "sl_b", "sl_si", "sl_hr", "sl_th", "sl_hc",
                             "sl_yp", "sl_yr", "sl_d", "sl_g"))

        block = ctx.enter_context(nc.Block())

        def cols(u):
            if u < TI:
                return P, slice(u * P, (u + 1) * P)
            return NT, slice(B * NP + (u - TI) * NT, B * NP + (u - TI + 1) * NT)

        def tile_of(gp, j):
            return gp if j == 0 else TI + 2 * gp + j - 1

        def last_batch(i):
            return (i * P + rows_of(i) - 1) // N

        def by_row(t, c):
            return t[:, c, :].rearrange("p (r w k) -> p w r k", w=8, k=PATCH)

        def by_patch(t, c):
            return t[:, c, :].rearrange("p (w r k) -> p w r k", w=8, k=PATCH)

        CONSTS = 12
        BIASES = 10
        PAIR = (0, 2, 4)
        DOWN = (0, 1, 2, 3)

        def load_rows(q, i, mix_rows):
            n = rows_of(i)
            for b in range((i * P) // N, last_batch(i) + 1):
                q.wait_ge(mix_out[b], 32)
            if i >= XS:
                q.wait_ge(xs_t, i - XS + 1)
            q.dma_start(xs[0:n, i % XS, :], mix_rows[i * P:i * P + n, :]).then_inc(ld_xs[i], 16)

        @block.sync
        def _(sp_):
            sp_.dma_start(wpn[:, :, :], Wp.rearrange("(k p) d -> p k d", p=P)).then_inc(ld_wp, 16)
            for hf in range(2):
                for b in range(B):
                    sp_.dma_start(xst[hf * 64 + 8 * b:hf * 64 + 8 * b + 8, :, :],
                                  x[b].rearrange("c (n h r) w -> h n c (r w)", h=2, r=PATCH // 2)[hf]).then_inc(ld_x, 16)
            sp_.dma_start(tx[0:NT, :, :], txt.rearrange("b t c -> t b c")).then_inc(ld_tx, 16)
            for n, w in enumerate((q_w1, k_w1, v_w, g_w, q_w2, k_w2, p_w)):
                sp_.dma_start(wnat[:, n, :, :], w.rearrange("(k p) c -> p k c", p=P)).then_inc(ld_wn, 16)
            sp_.dma_start(wg[:, :, :], Wg.rearrange("(k p) e -> p k e", p=P)).then_inc(ld_wn, 16)
            hv = h_dram.rearrange("(b t) c -> b t c", t=N)
            sp_.dma_start(hv[:, NP:N, :].rearrange("b t c -> b (t c)"), txt.rearrange("b t c -> b (t c)")).then_inc(h_out, 16)
            for i in range(TI):
                sp_.wait_ge(hi_r, i + 1)
                for j in range(2):
                    sp_.dma_start(hv[2 * i + j, 0:NP, :], hI[j * NP:(j + 1) * NP, i, :]).then_inc(h_out, 16)
            sp_.wait_ge(xn_t, 6)
            sp_.wait_ge(h_out, 16 * (1 + B))
            for n, w in enumerate((Ws1, Ws2)):
                sp_.dma_start(ws12[:, :, n * HS:(n + 1) * HS], w.rearrange("(k p) h -> p k h", p=P)).then_inc(ld_ws, 16)
            full = HS // P
            sp_.dma_start(ws3[:, 0:full, :], Ws3[0:full * P, :].rearrange("(k p) c -> p k c", p=P)).then_inc(ld_ws, 16)
            sp_.dma_start(ws3[0:HS - full * P, full, :], Ws3[full * P:HS, :]).then_inc(ld_ws, 16)
            sp_.wait_ge(xn_t, 6)
            sp_.dma_start(hb[:, 0:TF - 1, :], h_dram[0:(TF - 1) * P, :].rearrange("(i p) c -> p i c", p=P)).then_inc(ld_hb, 16)
            sp_.dma_start(hb[0:LAST, TF - 1, :], h_dram[(TF - 1) * P:T, :]).then_inc(ld_hb, 16)
            sp_.wait_ge(emb, TI)
            sp_.wait_ge(w_t, 7)
            full = H // P
            for e in range(E):
                sp_.dma_start(w12[:, e, :, 0:H], W1[e].rearrange("(k p) h -> p k h", p=P)).then_inc(ld_we, 16)
                sp_.dma_start(w12[:, e, :, H:2 * H], W2[e].rearrange("(k p) h -> p k h", p=P)).then_inc(ld_we, 16)
                sp_.dma_start(w3[:, e, 0:full, :], W3[e, 0:full * P, :].rearrange("(k p) c -> p k c", p=P)).then_inc(ld_we, 16)
                sp_.dma_start(w3[KH * P - H:P, e, full, :], W3[e, full * P:H, :]).then_inc(ld_we, 16)
            mix_rows = mix_dram.rearrange("b (t c) -> (b t) c", c=C)
            loaded = 0
            for b in range(B):
                v = mix_dram[b].rearrange("(h d n) -> d h n", h=HEADS, n=HD)
                r = (b % 2) * NP
                sp_.wait_ge(at_g, 2 * b + 2)
                sp_.dma_start(v[0:NP], ogi[r:r + NP, b % 2, :].rearrange("p (h n) -> p h n", n=HD)).then_inc(mix_out[b], 16)
                sp_.dma_start(v[NP:N], ogt[0:NT, b % 2, :].rearrange("p (h n) -> p h n", n=HD)).then_inc(mix_out[b], 16)
                if b == 0:
                    continue
                while last_batch(loaded) < b:
                    load_rows(sp_, loaded, mix_rows)
                    loaded += 1
            while loaded < TF:
                load_rows(sp_, loaded, mix_rows)
                loaded += 1
            for i in range(TF):
                sp_.wait_ge(s_o, i + 1)
                sp_.dma_start(out2d[i * P:i * P + rows_of(i), :], h2[0:rows_of(i), i, :]).then_inc(out_init, 16)
                if i == 4:
                    sp_.wait_ge(slot_out, 2 * TF * 16)
                    for s in range(2):
                        sp_.dma_start(sl_x[:, s, :], slot_dram[s * P:(s + 1) * P, 0:C]).then_inc(sl_ld[s], 16)
                    sp_.dma_start(tail[:, :, :], slot_dram[:, C:ROW].rearrange("(s p) c -> p s c", p=P)).then_inc(ld_tail, 16)

            def slot_load(s, j):
                sp_.wait_ge(sl_tx, s - 1)
                sp_.dma_start(sl_x[:, j, :], slot_dram[bass.ds(s * P, P), 0:C]).then_inc(sl_ld[j], 16)

            with sp_.Fori(1, SLOTS // 2) as i:
                slot_load(2 * i, 0)
                slot_load(2 * i + 1, 1)
            slot_load(SLOTS - 1, 0)
            sp_.wait_ge(out_init, TF * 16)
            sp_.wait_ge(sl_add, SLOTS * 16)

        @block.gpsimd
        def _(pool):
            pool.memset(ident[:, :], 0.0).then_inc(k_set, 1)
            pool.memset(ident2[:, :, :], 0.0).then_inc(k_set, 1)
            pool.memset(blocks[:, :, :], SCALE).then_inc(k_set, 1)
            pool.memset(before[:, :], 1.0).then_inc(k_set, 1)
            pool.memset(e_lt[:, :, :], 1.0).then_inc(k_set, 1)
            pool.memset(empty[:, :], 0.0).then_inc(k_set, 1)
            pool.memset(ones[:, :], 1.0).then_inc(k_ready, 1)
            pool.memset(eps[:, :], EPS).then_inc(k_ready, 1)
            pool.wait_ge(k_set, 6)
            pool.affine_select(out=ident[:, :], in_=ident[:, :], compare_op=ALU.not_equal, fill=1.0, base=0,
                               pattern=[[-1, P]], channel_multiplier=1).then_inc(k_ready, 1)
            pool.affine_select(out=ident2[:, :, :], in_=ident2[:, :, :], compare_op=ALU.not_equal, fill=1.0, base=0,
                               pattern=[[0, KC], [-1, P]], channel_multiplier=1).then_inc(k_ready, 1)
            pool.affine_select(out=before[:, :], in_=before[:, :], compare_op=ALU.is_gt, fill=0.0, base=0,
                               pattern=[[1, P]], channel_multiplier=-1).then_inc(k_ready, 1)
            pool.affine_select(out=e_lt[:, :, :], in_=e_lt[:, :, :], compare_op=ALU.is_gt, fill=0.0, base=0,
                               pattern=[[1, E], [-1, E]], channel_multiplier=0).then_inc(k_ready, 1)
            bl = blocks[:, :, :].rearrange("p k (b n) -> p (k b) n", n=HD)
            pool.affine_select(out=bl, in_=bl, compare_op=ALU.is_ge, fill=0.0, base=0,
                               pattern=[[0, KC], [-HD, P // HD], [0, HD]], channel_multiplier=1).then_inc(k_set, 1)
            pool.wait_ge(k_set, 7)
            pool.affine_select(out=bl, in_=bl, compare_op=ALU.is_ge, fill=0.0, base=HD - 1,
                               pattern=[[0, KC], [HD, P // HD], [0, HD]], channel_multiplier=-1).then_inc(k_ready, 1)
            io = dict(allow_small_or_imprecise_dtypes=True)
            pool.iota(e_up[:, :], pattern=[[1, E]], base=0, channel_multiplier=0, **io).then_inc(k_ready, 1)
            pool.iota(e_dn[:, :], pattern=[[-1, E]], base=E, channel_multiplier=0, **io).then_inc(k_ready, 1)
            pool.iota(tile_at[:, :], pattern=[[P, TF]], base=0, channel_multiplier=0, **io).then_inc(k_ready, 1)
            pool.iota(slot_no[:, :], pattern=[[1, SLOTS]], base=0, channel_multiplier=0, **io).then_inc(k_ready, 1)
            pool.iota(tok_no[:, :], pattern=[[P, TF]], base=0, channel_multiplier=1, **io).then_inc(k_ready, 1)
            pool.wait_ge(emb, TI)
            pool.wait_ge(w_t, 7)
            pool.memset(w3[0:KH * P - H, :, KH - 1, :], 0.0).then_inc(w3_z, 1)
            pool.memset(empty[:, C:C + 1], NOBODY).then_inc(k_empty, 1)
            pool.wait_ge(k_empty, 1)
            pool.wait_ge(ld_we, 16 * 4 * E)
            pool.dma_start(slot_dram.rearrange("(s p) c -> p s c", p=P),
                           empty[:, :].unsqueeze(1).broadcast_to([P, SLOTS, ROW])).then_inc(slot_zero, 16)
            pool.wait_ge(ld_hb, 32)
            pool.wait_ge(ld_b, 16 * BIASES)
            for i in range(TF):
                n = rows_of(i)
                pool.tensor_tensor(hb[0:n, i, :], hb[0:n, i, :], pb[0:n, :], ALU.add).then_inc(hb_r, 1)
            pool.wait_ge(slot_zero, 16)
            pool.wait_ge(rt_done, 1)
            for i in range(TF):
                n = rows_of(i)
                for j in range(2):
                    pool.indirect_dma_start(
                        out=slot_dram, out_offset=bass.IndirectOffsetOnAxis(ap=posu[0:n, j, i:i + 1], axis=0),
                        in_=xn2[0:n, i, :], in_offset=None).then_inc(slot_out, 16)

            pool.wait_ge(out_init, TF * 16)
            pool.wait_ge(sl_g, 2)
            for s in range(SLOTS):
                pool.wait_ge(sl_yr, s + 1)
                if s:
                    pool.wait_ge(sl_add, 16 * s)
                pool.indirect_dma_start(
                    out=out2d, out_offset=bass.IndirectOffsetOnAxis(ap=idx[:, s:s + 1], axis=0),
                    in_=sl_y[:, s % 2, :], in_offset=None, bounds_check=T - 1, oob_is_err=False,
                    compute_op=ALU.add).then_inc(sl_add, 16)
            pool.wait_ge(sl_add, SLOTS * 16)

        @block.scalar
        def _(act):
            row = lambda a: a.partition_broadcast(P)
            for j in range(2):
                act.dma_start(posb[j * NP:(j + 1) * NP, :], pos).then_inc(ld_b, 16)
            act.dma_start(tokb[:, :], row(tok_b)).then_inc(ld_b, 16)
            for n, w in enumerate((q_b1, k_b1, v_b)):
                act.dma_start(cb[:, n, :], w.rearrange("(k p) -> p k", p=P), allow_slow_non_contiguous=True).then_inc(ld_b, 16)
            act.dma_start(gb[:, :], row(g_b)).then_inc(ld_b, 16)
            act.dma_start(qkb[:, 0:C], row(q_b2)).then_inc(ld_b, 16)
            act.dma_start(qkb[:, C:2 * C], row(k_b2)).then_inc(ld_b, 16)
            act.dma_start(pb[:, :], row(p_b)).then_inc(ld_b, 16)

            act.wait_ge(ld_x, 32 * B)
            act.activation(by_patch(xrs, 1), by_row(xst, 1), ACT.Copy).then_inc(xr_a, 1)
            for f in range(3):
                act.wait_ge(wp_t, f + 1)
                act.activation(wpT[:, 2 * f:2 * f + 2, :], ps[:, f, :].rearrange("p (a c) -> p a c", a=2), ACT.Copy).then_inc(wp_c, 1)
            act.wait_ge(k_ready, CONSTS)
            act.wait_ge(mv_r, B)
            act.activation(rs[:, TI:TA], mv[:, TI:TA, 1], ACT.Sqrt, bias=eps[:, 0:1]).then_inc(sd_r, 1)
            for f in range(7):
                act.wait_ge(w_t, f + 1)
                act.activation(wT[:, f, :, :], ps[:, 4 + f % 4, :].rearrange("p (a c) -> p a c", a=2), ACT.Copy).then_inc(w_c, 1)
            act.wait_ge(mv_r, TA)
            act.activation(rs[:, 0:TI], mv[:, 0:TI, 1], ACT.Sqrt, bias=eps[:, 0:1]).then_inc(sd_r, 1)
            for f in range(6):
                act.wait_ge(xn_t, f + 1)
                w = 2 * NT if f < 4 else 2 * P
                c0 = B * NP + f * w if f < 4 else (f - 4) * w
                act.activation(xT[:, :, c0:c0 + w], ps[:, f % 4, :].rearrange("p (k c) -> p k c", k=KC)[:, :, 0:w], ACT.Copy).then_inc(xn_c, 1)
            n = 0
            for w, dst in enumerate((q1T, k1T, vT)):
                for c in range(NCH):
                    for m in range(KC):
                        act.wait_ge(p1, n + 1)
                        act.activation(dst[:, m, c * CW:(c + 1) * CW], ps[:, 4 + n % 4, 0:CW], ACT.Gelu,
                                       bias=cb[:, w, m:m + 1]).then_inc(p1_c, 1)
                        n += 1
            for u in range(TA):
                act.wait_ge(pg_b, u + 1)
                r, _c = cols(u)
                act.activation(g[0:r, u, :], g[0:r, u, :], ACT.Gelu).then_inc(pg_c, 1)

            def soft(v):
                r, _c = cols(tile_of(v // 3, v % 3))
                act.wait_ge(sp_y, v + 1)
                if v >= 2:
                    act.wait_ge(sp_q, v - 1)
                act.activation(spa[0:r, v % 2, :], spy[0:r, v % 2, :], ACT.Abs).then_inc(sp_a, 1)
                act.wait_ge(sp_a, v + 1)
                act.activation(spa[0:r, v % 2, :], spa[0:r, v % 2, :], ACT.Exp, scale=-1.0).then_inc(sp_e, 1)
                act.wait_ge(sp_e, v + 1)
                act.activation(spa[0:r, v % 2, :], spa[0:r, v % 2, :], ACT.Ln, bias=1.0).then_inc(sp_l, 1)

            act.preload_act_table_set("natural_log_exp_and_others")
            for v in range(3):
                soft(v)
            for gp in range(TI):
                if gp + 1 < TI:
                    soft(3 * gp + 3)
                for b in (2 * gp, 2 * gp + 1):
                    act.wait_ge(at_z, b + 1)
                    act.activation(mz[:, b % 2, :], ps[:, 2 + b % 2, 0:C], ACT.Copy, bias=float(C - 1)).then_inc(at_zb, 1)
                if gp + 1 < TI:
                    soft(3 * gp + 4)
                    soft(3 * gp + 5)

            for k in range(TF + 3):
                if k < TF:
                    act.wait_ge(xs_t, k + 1)
                    if k >= 2:
                        act.wait_ge(y_p, k - 1)
                    act.activation(xsT[:, k % 2, :], ps[:, k % 2, 0:C], ACT.Copy).then_inc(xs_c, 1)
                i = k - 1
                if 0 <= i < TF:
                    act.wait_ge(mv2, i + 1)
                    act.activation(rs[:, i:i + 1], mv[:, i, 1:2], ACT.Sqrt, bias=eps[:, 0:1]).then_inc(sd2, 1)
                i = k - 3
                if 0 <= i < TF:
                    n = rows_of(i)
                    act.wait_ge(n2_t, i + 1)
                    act.activation(x2T[:, :, i * P:i * P + n], ps[:, 4 + i % 2, 0:C].rearrange("p (k c) -> p k c", k=KC)[:, :, 0:n],
                                   ACT.Copy).then_inc(n2_c, 1)
            act.wait_ge(rt_dif, 1)
            act.activation(ex[:, :], dif[:, :], ACT.Exp).then_inc(rt_ex, 1)

            for v in range(KS * NCH):
                m = P if v // NCH < KS - 1 else HS - (KS - 1) * P
                act.wait_ge(s_up, v + 1)
                if v >= 2:
                    act.wait_ge(s_h, v - 1)
                act.activation(sil[0:m, v % 2, :], ps[0:m, PAIR[v % 3], 0:CW], ACT.Silu).then_inc(s_sil, 1)

            def x_copy(s, j):
                act.wait_ge(sl_tx, s + 1)
                act.activation(sl_xT[:, j, :].rearrange("p (k c) -> p k c", k=KC), ps[:, 4 * j:4 * j + 2, 384:512],
                               ACT.Copy).then_inc(sl_xc, 1)

            def silu(s, j):
                act.wait_ge(sl_a, s + 1)
                act.activation(sl_s[:, j, :], ps[:, 4 * j, 0:H], ACT.Silu).then_inc(sl_si, 1)

            def gated(s, j, first=False):
                act.wait_ge(sl_yp, s + 1)
                if not first:
                    act.wait_ge(sl_add, 16 * (s - 1))
                act.activation(sl_y[:, j, :], ps[:, 4 * j + 3, 0:C], ACT.Copy, scale=gate[:, bass.ds(s, 1)]).then_inc(sl_yr, 1)

            act.wait_ge(s_dn, TF)
            act.wait_ge(s_o, TF)
            act.wait_ge(sl_g, 2)
            x_copy(0, 0)
            x_copy(1, 1)
            silu(0, 0)
            x_copy(2, 0)
            silu(1, 1)
            gated(0, 0, True)
            x_copy(3, 1)
            silu(2, 0)
            gated(1, 1, True)

            def act_body(s, j):
                x_copy(s + 2, j)
                silu(s + 1, 1 - j)
                gated(s, j)

            with act.Fori(1, SLOTS // 2 - 1) as i:
                act_body(2 * i, 0)
                act_body(2 * i + 1, 1)
            act_body(SLOTS - 3, 0)
            silu(SLOTS - 1, 0)
            gated(SLOTS - 2, 1)
            gated(SLOTS - 1, 0)

        @block.vector
        def _(dve):
            dve.wait_ge(ld_x, 32 * B)
            for c in (0, 2):
                dve.tensor_copy(by_patch(xrs, c), by_row(xst, c)).then_inc(xr_d, 1)
            dve.memset(mv[:, :, :], 0.0).then_inc(st_r, 1)
            dve.wait_ge(st_r, 1)
            dve.wait_ge(ld_tx, 16)
            for b in range(B):
                dve.bn_stats(st[0:NT, TI + b, :], tx[0:NT, b, :]).then_inc(st_r, 1)
            for b in range(B):
                dve.wait_ge(st_r, b + 2)
                dve.bn_aggr(mv[0:NT, TI + b, :], st[0:NT, TI + b, :]).then_inc(mv_r, 1)
            for f in range(KP):
                dve.wait_ge(x_t, f + 1)
                c, w0 = f // 2, (f % 2) * 4
                dve.tensor_copy(patchT[:, 2 * c:2 * c + 2, :].rearrange("p h (q w) -> p h q w", w=8)[:, :, :, w0:w0 + 4],
                                ps[:, 4 + f % 4, :].rearrange("p (w h q) -> p h q w", w=4, h=2)).then_inc(x_c, 1)
            dve.wait_ge(ld_b, 16 * BIASES)
            dve.tensor_tensor(posb[:, :], posb[:, :], tokb[:, :], ALU.add).then_inc(posb_r, 1)
            dve.wait_ge(posb_r, 1)
            dve.wait_ge(sd_r, 1)
            dve.reciprocal(rs2[:, TI:TA], rs[:, TI:TA]).then_inc(rs_r, 1)
            dve.wait_ge(rs_r, 1)
            for u in range(TI, TA):
                dve.tensor_scalar(xn[0:NT, u, :], tx[0:NT, u - TI, :], mv[0:NT, u, 0:1], rs2[0:NT, u:u + 1],
                                  ALU.subtract, ALU.mult).then_inc(xn_r, 1)
            for i in range(TI):
                dve.wait_ge(emb, i + 1)
                dve.tensor_tensor(hI[:, i, :], ps[:, i, 0:C], posb[:, :], ALU.add).then_inc(hi_r, 1)
                dve.wait_ge(hi_r, i + 1)
                dve.bn_stats(st[:, i, :], hI[:, i, :]).then_inc(st_r, 1)
                dve.wait_ge(st_r, 2 + B + i)
                dve.bn_aggr(mv[:, i, :], st[:, i, :]).then_inc(mv_r, 1)
            dve.wait_ge(sd_r, 2)
            dve.reciprocal(rs2[:, 0:TI], rs[:, 0:TI]).then_inc(rs_r, 1)
            dve.wait_ge(rs_r, 2)
            for u in range(TI):
                dve.tensor_scalar(xn[:, u, :], hI[:, u, :], mv[:, u, 0:1], rs2[:, u:u + 1],
                                  ALU.subtract, ALU.mult).then_inc(xn_r, 1)
            for u in range(TA):
                r, _c = cols(u)
                dve.wait_ge(pg, u + 1)
                dve.tensor_tensor(g[0:r, u, :], ps[0:r, u % 4, 0:C], gb[0:r, :], ALU.add).then_inc(pg_b, 1)

            def soft_in(v):
                r, _c = cols(tile_of(v // 3, v % 3))
                dve.wait_ge(sp, v + 1)
                dve.tensor_tensor(spy[0:r, v % 2, :], ps[0:r, 4 + v % 2, :], qkb[0:r, :], ALU.add).then_inc(sp_y, 1)

            def soft_out(v):
                r, _c = cols(tile_of(v // 3, v % 3))
                dve.wait_ge(sp_l, v + 1)
                if v >= 6:
                    dve.wait_ge(at_a, 2 * (v // 3 - 1))
                dve.scalar_tensor_tensor(out=qk[0:r, (v // 3) % 2, v % 3, :], in0=spy[0:r, v % 2, :], scalar=0.0,
                                         in1=spa[0:r, v % 2, :], op0=ALU.max, op1=ALU.add).then_inc(sp_q, 1)

            def masked(b):
                j = b % 2
                dve.wait_ge(at_a, b + 1)
                if b >= 2:
                    dve.wait_ge(at_z, b - 1)
                dve.tensor_tensor(mm2[:, j, :], ps[:, j, 0:C], blocks[:, :, :].rearrange("p k c -> p (k c)"), ALU.mult).then_inc(at_m, 1)
                dve.wait_ge(at_m, b + 1)
                dve.tensor_tensor(mm2[:, j, :], mm2[:, j, :], ident2[:, :, :].rearrange("p k c -> p (k c)"), ALU.add).then_inc(at_m2, 1)

            def scaled(b):
                j = b % 2
                dve.wait_ge(at_zb, b + 1)
                dve.reciprocal(mz[:, j, :], mz[:, j, :]).then_inc(at_r, 1)
                dve.wait_ge(at_r, b + 1)
                if b >= 2:
                    dve.wait_ge(at_o, b - 1)
                dve.tensor_tensor(mm3[:, j, :], mm2[:, j, :], mz[:, j, :], ALU.mult).then_inc(at_m3, 1)

            def gate_mix(b):
                j, r = b % 2, (b % 2) * NP
                dve.wait_ge(at_o, b + 1)
                if b == 0:
                    dve.wait_ge(pg_c, TA)
                if b >= 2:
                    dve.wait_ge(mix_out[b - 2], 32)
                dve.tensor_tensor(ogi[r:r + NP, j, :], ps[r:r + NP, 6 + j, 0:C], g[r:r + NP, b // 2, :], ALU.mult).then_inc(at_g, 1)
                dve.tensor_tensor(ogt[0:NT, j, :], ps[0:NT, 6 + j, C:2 * C], g[0:NT, TI + b, :], ALU.mult).then_inc(at_g, 1)

            soft_in(0)
            soft_in(1)
            soft_out(0)
            soft_in(2)
            soft_out(1)
            soft_out(2)
            for gp in range(TI):
                more = gp + 1 < TI
                masked(2 * gp)
                masked(2 * gp + 1)
                if more:
                    soft_in(3 * gp + 3)
                    soft_out(3 * gp + 3)
                scaled(2 * gp)
                scaled(2 * gp + 1)
                if more:
                    soft_in(3 * gp + 4)
                    soft_in(3 * gp + 5)
                gate_mix(2 * gp)
                gate_mix(2 * gp + 1)
                if more:
                    soft_out(3 * gp + 4)
                    soft_out(3 * gp + 5)

            dve.wait_ge(at_o, B)
            dve.memset(lg[:, :, :], 0.0).then_inc(lg_z, 1)
            for i in range(TF + 3):
                if i < TF:
                    n = rows_of(i)
                    dve.wait_ge(y_p, i + 1)
                    dve.wait_ge(hb_r, i + 1)
                    dve.tensor_tensor(h2[0:n, i, :], ps[0:n, 2 + i % 2, 0:C], hb[0:n, i, :], ALU.add).then_inc(h2_r, 1)
                    dve.wait_ge(h2_r, i + 1)
                    dve.bn_stats(st[0:n, i, :], h2[0:n, i, :]).then_inc(st2, 1)
                    dve.wait_ge(st2, i + 1)
                    dve.bn_aggr(mv[0:n, i, :], st[0:n, i, :]).then_inc(mv2, 1)
                k = i - 1
                if 0 <= k < TF:
                    n = rows_of(k)
                    dve.wait_ge(sd2, k + 1)
                    dve.reciprocal(rs2[:, k:k + 1], rs[:, k:k + 1]).then_inc(rs2_r, 1)
                    dve.wait_ge(rs2_r, k + 1)
                    dve.tensor_scalar(xn2[0:n, k, 0:C], h2[0:n, k, :], mv[0:n, k, 0:1], rs2[0:n, k:k + 1],
                                      ALU.subtract, ALU.mult).then_inc(n2, 1)
            dve.wait_ge(lg_z, 1)
            dve.wait_ge(r_l, TF)
            full = (TF - 1) * E
            dve.tensor_copy(lg[:, 0:TF - 1, :], ps[:, 6, 0:full].rearrange("p (t e) -> p t e", e=E)).then_inc(lg_r, 1)
            dve.tensor_copy(lg[0:LAST, TF - 1, :], ps[0:LAST, 6, full:full + E]).then_inc(lg_r, 1)
            dve.wait_ge(lg_r, 2)

            steps = [0]

            def then(ins, s=rt):
                steps[0] += 1
                ins.then_inc(rt, 1)
                dve.wait_ge(rt, steps[0])

            def wide(a):
                return a[:, :].unsqueeze(2).broadcast_to([P, TF, E])

            def per_tile(a):
                return a[:, :].unsqueeze(1).broadcast_to([P, TF, E])

            def best(l, mval, mx, oh):
                then(dve.tensor_reduce(mval[:, :], l[:, :, :], AX_X, ALU.max))
                then(dve.tensor_tensor(eq[:, :, :], l[:, :, :], wide(mval), ALU.is_equal))
                then(dve.tensor_tensor(eq[:, :, :], eq[:, :, :], per_tile(e_dn), ALU.mult))
                then(dve.tensor_reduce(mx[:, :], eq[:, :, :], AX_X, ALU.max))
                then(dve.tensor_tensor(oh[:, :, :], eq[:, :, :], wide(mx), ALU.is_equal))

            dve.wait_ge(k_ready, CONSTS)
            best(lg, m1, mx1, oh1)
            then(dve.scalar_tensor_tensor(out=lg2[:, :, :].rearrange("p t e -> p (t e)"),
                                          in0=oh1[:, :, :].rearrange("p t e -> p (t e)"), scalar=-BIG,
                                          in1=lg[:, :, :].rearrange("p t e -> p (t e)"), op0=ALU.mult, op1=ALU.add))
            best(lg2, m2, mx2, oh2)
            dve.tensor_tensor(both[:, :, :], oh1[:, :, :], oh2[:, :, :], ALU.add).then_inc(rt_both, 1)
            dve.tensor_tensor(dif[:, :], m2[:, :], m1[:, :], ALU.subtract).then_inc(rt_dif, 1)

            def shared_h(v):
                m, c = v // NCH, v % NCH
                r = P if m < KS - 1 else HS - m * P
                dve.wait_ge(s_sil, v + 1)
                dve.tensor_tensor(hsT[0:r, m, c * CW:(c + 1) * CW], sil[0:r, v % 2, :], ps[0:r, PAIR[v % 3] + 1, 0:CW],
                                  ALU.mult).then_inc(s_h, 1)

            for v in range(4):
                shared_h(v)
            dve.wait_ge(rt_ex, 1)
            then(dve.tensor_scalar(exs[:, :], ex[:, :], 1.0, None, ALU.add))
            then(dve.reciprocal(xn2[:, :, C + 1], exs[:, :]))
            then(dve.tensor_tensor(xn2[:, :, C + 2], ex[:, :], xn2[:, :, C + 1], ALU.mult))
            then(dve.tensor_scalar(xn2[:, :, C + 3], mx1[:, :], -1.0, float(E), ALU.mult, ALU.add))
            then(dve.tensor_copy(xn2[:, :, C], tok_no[:, :]))
            dve.wait_ge(rt_pre, 1)
            pre = ps[:, 7, 0:(TF + 1) * E].rearrange("p (t e) -> p t e", e=E)
            then(dve.tensor_copy(cnt[:, :], pre[:, TF, :]))
            then(dve.tensor_tensor(cmpt[:, :, :], cnt[:, :].unsqueeze(2).broadcast_to([P, E, TF]),
                                   tile_at[:, :].unsqueeze(1).broadcast_to([P, E, TF]), ALU.is_gt))
            then(dve.tensor_reduce(ntl[:, :], cmpt[:, :, :], AX_X, ALU.add))
            then(dve.tensor_tensor(cume[:, :, :], e_lt[:, :, :], ntl[:, :].unsqueeze(1).broadcast_to([P, E, E]), ALU.mult))
            then(dve.tensor_reduce(base[:, :], cume[:, :, :], AX_X, ALU.add))
            then(dve.tensor_tensor(upto[:, :], base[:, :], ntl[:, :], ALU.add))
            then(dve.tensor_scalar(base[:, :], base[:, :], float(P), None, ALU.mult))
            then(dve.tensor_tensor(adr[:, :, :], pre[:, 0:TF, :], per_tile(base), ALU.add))
            then(dve.tensor_tensor(prd[:, 0, :, :], adr[:, :, :], oh1[:, :, :], ALU.mult))
            then(dve.tensor_tensor(prd[:, 1, :, :], adr[:, :, :], oh2[:, :, :], ALU.mult))
            then(dve.tensor_reduce(posf[:, :, :], prd[:, :, :, :], AX_X, ALU.add))
            then(dve.tensor_copy(posu[:, :, :], posf[:, :, :]))
            then(dve.tensor_tensor(cmps[:, :, :], upto[:, :].unsqueeze(1).broadcast_to([P, SLOTS, E]),
                                   slot_no[:, :].unsqueeze(2).broadcast_to([P, SLOTS, E]), ALU.is_le))
            then(dve.tensor_reduce(esl[:, :], cmps[:, :, :], AX_X, ALU.add))
            then(dve.tensor_scalar(esl[:, :], esl[:, :], float(E - 1), None, ALU.min))
            dve.tensor_copy(esu[:, :], esl[:, :]).then_inc(rt_done, 1)
            for v in range(4, KS * NCH):
                shared_h(v)
            for i in range(TF):
                n = rows_of(i)
                dve.wait_ge(s_dn, i + 1)
                dve.tensor_tensor(h2[0:n, i, :], ps[0:n, DOWN[i % 4], 0:C], h2[0:n, i, :], ALU.add).then_inc(s_o, 1)

            dve.wait_ge(ld_tail, 16)
            dve.tensor_copy(idx[:, :], tail[:, :, 0]).then_inc(sl_g, 1)
            dve.tensor_tensor(dg[:, :], tail[:, :, 1], tail[:, :, 2], ALU.subtract).then_inc(sl_d, 1)
            dve.tensor_tensor(own[:, :], tail[:, :, 3], esl[:, :], ALU.is_equal).then_inc(sl_d, 1)
            dve.wait_ge(sl_d, 2)
            dve.tensor_tensor(dg[:, :], dg[:, :], own[:, :], ALU.mult).then_inc(sl_d, 1)
            dve.wait_ge(sl_d, 3)
            dve.tensor_tensor(gate[:, :], dg[:, :], tail[:, :, 2], ALU.add).then_inc(sl_g, 1)

            def h_copy(s, j):
                dve.wait_ge(sl_th, s + 1)
                dve.tensor_copy(sl_hT[:, j, :], ps[:, 4 * j + 2, 0:KH * P]).then_inc(sl_hc, 1)

            def h_prod(s, j):
                dve.wait_ge(sl_si, s + 1)
                dve.wait_ge(sl_b, s + 1)
                dve.tensor_tensor(sl_h[:, j, :], sl_s[:, j, :], ps[:, 4 * j + 1, 0:H], ALU.mult).then_inc(sl_hr, 1)

            h_prod(0, 0)
            h_copy(0, 0)
            h_prod(1, 1)
            h_copy(1, 1)
            h_prod(2, 0)

            def dve_body(s, j):
                h_copy(s, j)
                h_prod(s + 1, 1 - j)

            with dve.Fori(1, SLOTS // 2) as i:
                dve_body(2 * i, 0)
                dve_body(2 * i + 1, 1)
            h_copy(SLOTS - 1, 0)

        @block.tensor
        def _(pe):
            pe.wait_ge(k_ready, CONSTS)
            pe.wait_ge(ld_wp, 16)
            for f in range(3):
                for kt in (2 * f, 2 * f + 1):
                    c0 = (kt % 2) * (PD // 2) + kt // 2
                    for k in range(KC):
                        ins = pe.transpose(ps[:, f, (kt % 2) * C + k * P:(kt % 2) * C + (k + 1) * P],
                                           wpn[:, k, c0:c0 + 3 * (P - 1) + 1:3], ident[:, :])
                ins.then_inc(wp_t, 1)
            pe.wait_ge(xr_d, 2)
            pe.wait_ge(xr_a, 1)
            for f in range(KP):
                if f >= 4:
                    pe.wait_ge(x_c, f - 3)
                for w in range(4):
                    c0 = ((f % 2) * 4 + w) * P
                    ins = pe.transpose(ps[:, 4 + f % 4, w * P:(w + 1) * P], xrs[:, f // 2, c0:c0 + P], ident[:, :])
                ins.then_inc(x_t, 1)
            pe.wait_ge(x_c, KP)
            pe.wait_ge(wp_c, 3)
            for i in range(TI):
                for kt in range(KP):
                    ins = pe.matmul(ps[:, i, 0:C], patchT[:, kt, i * P:(i + 1) * P], wpT[:, kt, :],
                                    start=(kt == 0), stop=(kt == KP - 1))
                ins.then_inc(emb, 1)
            pe.wait_ge(ld_wn, 16 * 8)
            for f in range(7):
                if f >= 4:
                    pe.wait_ge(w_c, f - 3)
                for k in range(KC):
                    for m in range(KC):
                        ins = pe.transpose(ps[:, 4 + f % 4, k * C + m * P:k * C + (m + 1) * P],
                                           wnat[:, f, m, k * P:(k + 1) * P], ident[:, :])
                ins.then_inc(w_t, 1)
            pe.wait_ge(hi_r, TI)
            for f in range(6):
                r, u0, s = (NT, TI + 2 * f, 2 * f + 2) if f < 4 else (P, 2 * (f - 4), B + 2 * (f - 4) + 2)
                pe.wait_ge(xn_r, s)
                if f >= 4:
                    pe.wait_ge(xn_c, f - 3)
                for k in range(KC):
                    for j in range(2):
                        ins = pe.transpose(ps[:, f % 4, k * C + j * r:k * C + (j + 1) * r],
                                           xn[0:r, u0 + j, k * P:(k + 1) * P], ident[0:r, 0:r])
                ins.then_inc(xn_t, 1)
            pe.wait_ge(xn_c, 6)
            pe.wait_ge(w_c, 7)
            n = 0
            for w in (QW1, KW1, VW):
                for c in range(NCH):
                    for m in range(KC):
                        if n >= 4:
                            pe.wait_ge(p1_c, n - 3)
                        for k in range(KC):
                            ins = pe.matmul(ps[:, 4 + n % 4, 0:CW], wT[:, w, k, m * P:(m + 1) * P],
                                            xT[:, k, c * CW:(c + 1) * CW], start=(k == 0), stop=(k == KC - 1))
                        ins.then_inc(p1, 1)
                        n += 1
            for u in range(TA):
                r, cs = cols(u)
                if u >= 4:
                    pe.wait_ge(pg_b, u - 3)
                for k in range(KC):
                    ins = pe.matmul(ps[0:r, u % 4, 0:C], xT[:, k, cs], wT[:, GW, k, :], start=(k == 0), stop=(k == KC - 1))
                ins.then_inc(pg, 1)

            def layer2(v):
                u = tile_of(v // 3, v % 3)
                r, cs = cols(u)
                if v >= 2:
                    pe.wait_ge(sp_y, v - 1)
                    pe.wait_ge(sp_q, v - 1)
                for n, (src, w) in enumerate(((q1T, QW2), (k1T, KW2))):
                    for k in range(KC):
                        ins = pe.matmul(ps[0:r, 4 + v % 2, n * C:(n + 1) * C], src[:, k, cs], wT[:, w, k, :],
                                        start=(k == 0), stop=(k == KC - 1))
                ins.then_inc(sp, 1)

            def gram(b):
                s, r = (b // 2) % 2, (b % 2) * NP
                pe.wait_ge(sp_q, 3 * (b // 2) + 3)
                if b >= 2:
                    pe.wait_ge(at_m, b - 1)
                for m in range(KC):
                    qc, kc = slice(m * P, (m + 1) * P), slice(C + m * P, C + (m + 1) * P)
                    pe.matmul(ps[:, b % 2, qc], qk[r:r + NP, s, 0, kc], qk[r:r + NP, s, 0, qc], start=True, stop=False)
                    ins = pe.matmul(ps[:, b % 2, qc], qk[0:NT, s, 1 + b % 2, kc], qk[0:NT, s, 1 + b % 2, qc],
                                    start=False, stop=True)
                ins.then_inc(at_a, 1)

            def sums(b):
                pe.wait_ge(at_m2, b + 1)
                if b >= 2:
                    pe.wait_ge(at_zb, b - 1)
                pe.matmul(ps[:, 2 + b % 2, 0:C], ones[:, :], mm2[:, b % 2, :], start=True, stop=True).then_inc(at_z, 1)

            def mixed(b):
                r = (b % 2) * NP
                pe.wait_ge(at_m3, b + 1)
                if b >= 2:
                    pe.wait_ge(at_g, 2 * (b - 1))
                for m in range(KC):
                    cs = slice(m * P, (m + 1) * P)
                    pe.matmul(ps[r:r + NP, 6 + b % 2, cs], vT[:, m, b * NP:(b + 1) * NP], mm3[:, b % 2, cs], start=True, stop=True)
                for m in range(KC):
                    cs = slice(m * P, (m + 1) * P)
                    ins = pe.matmul(ps[0:NT, 6 + b % 2, C + m * P:C + (m + 1) * P], vT[:, m, cols(TI + b)[1]],
                                    mm3[:, b % 2, cs], start=True, stop=True)
                ins.then_inc(at_o, 1)

            pe.wait_ge(p1_c, 18)
            for v in range(3):
                layer2(v)
            pe.wait_ge(pg_b, TA)
            for gp in range(TI):
                more = gp + 1 < TI
                gram(2 * gp)
                gram(2 * gp + 1)
                if more:
                    layer2(3 * gp + 3)
                sums(2 * gp)
                sums(2 * gp + 1)
                if more:
                    layer2(3 * gp + 4)
                    layer2(3 * gp + 5)
                mixed(2 * gp)
                mixed(2 * gp + 1)

            pe.wait_ge(at_m, B)
            pe.wait_ge(at_zb, B)
            pe.wait_ge(at_g, 2 * B)
            pe.wait_ge(sp_y, 3 * TI)
            for k in range(TF + 4):
                if k < TF:
                    n = rows_of(k)
                    pe.wait_ge(ld_xs[k], 16)
                    if k >= 2:
                        pe.wait_ge(xs_c, k - 1)
                    for c in range(KC):
                        ins = pe.transpose(ps[:, k % 2, c * P:c * P + n], xs[0:n, k % XS, c * P:(c + 1) * P], ident[0:n, 0:n])
                    if n < P:
                        for c in range(KC):
                            ins = pe.transpose(ps[:, k % 2, c * P + n:(c + 1) * P], xs[0:P - n, k % XS, c * P:(c + 1) * P], ident[0:P - n, 0:P - n])
                    ins.then_inc(xs_t, 1)
                i = k - 1
                if 0 <= i < TF:
                    n = rows_of(i)
                    pe.wait_ge(xs_c, i + 1)
                    if i >= 2:
                        pe.wait_ge(h2_r, i - 1)
                    for c in range(KC):
                        ins = pe.matmul(ps[0:n, 2 + i % 2, 0:C], xsT[:, i % 2, c * P:c * P + n], wT[:, PW, c, :],
                                        start=(c == 0), stop=(c == KC - 1))
                    ins.then_inc(y_p, 1)
                i = k - 3
                if 0 <= i < TF:
                    n = rows_of(i)
                    pe.wait_ge(n2, i + 1)
                    if i >= 2:
                        pe.wait_ge(n2_c, i - 1)
                    for c in range(KC):
                        ins = pe.transpose(ps[:, 4 + i % 2, c * P:c * P + n], xn2[0:n, i, c * P:(c + 1) * P], ident[0:n, 0:n])
                    ins.then_inc(n2_t, 1)
                i = k - 4
                if 0 <= i < TF:
                    n = rows_of(i)
                    pe.wait_ge(n2_c, i + 1)
                    for c in range(KC):
                        ins = pe.matmul(ps[0:n, 6, i * E:(i + 1) * E], x2T[:, c, i * P:i * P + n], wg[:, c, :],
                                        start=(c == 0), stop=(c == KC - 1))
                    ins.then_inc(r_l, 1)

            def shared_up(v):
                m, c = v // NCH, v % NCH
                r = P if m < KS - 1 else HS - m * P
                if v >= 3:
                    pe.wait_ge(s_h, v - 2)
                for n in range(2):
                    for k in range(KC):
                        ins = pe.matmul(ps[0:r, PAIR[v % 3] + n, 0:CW], ws12[:, k, n * HS + m * P:n * HS + m * P + r],
                                        x2T[:, k, c * CW:(c + 1) * CW], start=(k == 0), stop=(k == KC - 1))
                ins.then_inc(s_up, 1)

            pe.wait_ge(ld_ws, 16 * 4)
            pe.wait_ge(h2_r, TF)
            for v in range(3):
                shared_up(v)
            pe.wait_ge(rt_both, 1)
            full = (TF - 1) * E
            flat = both[:, :, :].rearrange("p t e -> p (t e)")
            pe.matmul(ps[:, 7, 0:full], before[:, :], flat[:, 0:full], start=True, stop=False, skip_group_check=True)
            pe.matmul(ps[:, 7, full:full + E], before[0:LAST, :], flat[0:LAST, full:full + E], start=False, stop=False, skip_group_check=True)
            for t in range(TF):
                n = rows_of(t)
                ins = pe.matmul(ps[:, 7, (t + 1) * E:(TF + 1) * E], ones[0:n, :],
                                both[0:n, t, :].unsqueeze(1).broadcast_to([n, TF - t, E]),
                                start=False, stop=(t == TF - 1), skip_group_check=True)
            ins.then_inc(rt_pre, 1)
            for v in range(3, KS * NCH):
                shared_up(v)
            pe.wait_ge(s_h, KS * NCH)
            for i in range(TF):
                n = rows_of(i)
                if i >= 4:
                    pe.wait_ge(s_o, i - 3)
                for k in range(KS):
                    r = P if k < KS - 1 else HS - k * P
                    ins = pe.matmul(ps[0:n, DOWN[i % 4], 0:C], hsT[0:r, k, i * P:i * P + n], ws3[0:r, k, :],
                                    start=(k == 0), stop=(k == KS - 1))
                ins.then_inc(s_dn, 1)

            def x_turn(s, j, i):
                pe.wait_ge(sl_ld[j], 16 * (i + 1))
                for k in range(KC):
                    ins = pe.transpose(ps[:, 4 * j + k, 384:512], sl_x[:, j, k * P:(k + 1) * P], ident[:, :])
                ins.then_inc(sl_tx, 1)

            def up(s, j, e):
                pe.wait_ge(sl_xc, s + 1)
                for n, done in ((0, sl_a), (1, sl_b)):
                    for k in range(KC):
                        ins = pe.matmul(ps[:, 4 * j + n, 0:H], sl_xT[:, j, k * P:(k + 1) * P],
                                        w12f[:, bass.ds(e * (KC * 2 * H) + k * 2 * H + n * H, H)], start=(k == 0), stop=(k == KC - 1))
                    ins.then_inc(done, 1)

            def h_turn(s, j):
                pe.wait_ge(sl_hr, s + 1)
                for k in range(KH):
                    c0 = min(k * P, H - P)
                    ins = pe.transpose(ps[:, 4 * j + 2, k * P:(k + 1) * P], sl_h[:, j, c0:c0 + P], ident[:, :])
                ins.then_inc(sl_th, 1)

            def down(s, j, e, first=False):
                pe.wait_ge(sl_hc, s + 1)
                if not first:
                    pe.wait_ge(sl_yr, s - 1)
                for k in range(KH):
                    ins = pe.matmul(ps[:, 4 * j + 3, 0:C], sl_hT[:, j, k * P:(k + 1) * P],
                                    w3f[:, bass.ds(e * (KH * C) + k * C, C)], start=(k == 0), stop=(k == KH - 1))
                ins.then_inc(sl_yp, 1)

            w12f = w12[:, :, :, :].rearrange("p e k h -> p (e k h)")
            w3f = w3[:, :, :, :].rearrange("p e k c -> p (e k c)")

            def expert(s):
                return pe.value_load(esu[0:1, bass.ds(s, 1)], min_val=0, max_val=E - 1)

            pe.wait_ge(ld_we, 16 * 4 * E)
            pe.wait_ge(w3_z, 1)
            pe.wait_ge(rt_done, 1)
            pe.wait_ge(s_o, TF)
            x_turn(0, 0, 0)
            x_turn(1, 1, 0)
            up(0, 0, expert(0))

            def pe_body(s, j, i, first=False, turn=True, more=True):
                h_turn(s, j)
                if turn:
                    x_turn(s + 2, j, i + 1)
                if more:
                    up(s + 1, 1 - j, expert(s + 1))
                down(s, j, expert(s), first)

            pe_body(0, 0, 0, True)
            pe_body(1, 1, 0, True)
            with pe.Fori(1, SLOTS // 2 - 1) as i:
                pe_body(2 * i, 0, i)
                pe_body(2 * i + 1, 1, i)
            i = SLOTS // 2 - 1
            pe_body(2 * i, 0, i)
            pe_body(2 * i + 1, 1, i, turn=False)
            pe_body(2 * i + 2, 0, i + 1, turn=False, more=False)


_INS = ['x', 'txt', 'L0_tok_Wp', 'L0_tok_b', 'L0_attn_q_w1', 'L0_attn_q_b1', 'L0_attn_q_w2', 'L0_attn_q_b2',
        'L0_attn_k_w1', 'L0_attn_k_b1', 'L0_attn_k_w2', 'L0_attn_k_b2', 'L0_attn_v_w', 'L0_attn_v_b',
        'L0_attn_g_w', 'L0_attn_g_b', 'L0_attn_p_w', 'L0_attn_p_b', 'L0_ffn_Wg', 'L0_ffn_W1', 'L0_ffn_W2',
        'L0_ffn_W3', 'L0_ffn_Ws1', 'L0_ffn_Ws2', 'L0_ffn_Ws3']


def position_table():
    import numpy as np
    side, quarter = IMG // PATCH, C // 4
    gh, gw = np.meshgrid(np.arange(side), np.arange(side), indexing="ij")
    factor = np.float32(10000.0) ** (np.arange(quarter, dtype=np.float32) / np.float32(quarter))
    h = gh.reshape(-1).astype(np.float32)[:, None] / factor
    w = gw.reshape(-1).astype(np.float32)[:, None] / factor
    return np.concatenate([np.sin(h), np.cos(h), np.sin(w), np.cos(w)], axis=-1).astype(np.float32)


def kernel(**inputs):
    import numpy as _np
    import concourse.bacc as _bacc
    from concourse import mybir as _mybir
    from concourse.bass_utils import run_bass_kernel_spmd as _run

    nc = _bacc.Bacc("TRN2", target_bir_lowering=False, num_devices=1)
    arrays, args = {}, []
    for name, a in [(n, inputs[n]) for n in _INS] + [("pos", position_table())]:
        a = _np.ascontiguousarray(a)
        arrays[f"in_{name}_dram"] = a
        args.append(nc.dram_tensor(f"in_{name}_dram", a.shape, _mybir.dt.from_np(a.dtype), kind="ExternalInput").ap())
    args.append(nc.dram_tensor("out_0_dram", (B, N, C), _mybir.dt.float32, kind="ExternalOutput").ap())
    fused_layer(nc, *args)
    r = _run(nc, [arrays], core_ids=[0])
    return r.results[0]["out_0_dram"]
```

```python
from contextlib import ExitStack

import concourse.bass as bass
from concourse import mybir

F32 = mybir.dt.float32
F32R = mybir.dt.float32r
U32 = mybir.dt.uint32
ALU = mybir.AluOpType
ACT = mybir.ActivationFunctionType
AX_X = mybir.AxisListType.X

P = 128
B, CH, IMG = 8, 3, 128
PATCH = 16
NP = (IMG // PATCH) ** 2
NT = 77
N = NP + NT
T = B * N
C = 256
KC = C // P
PD = CH * PATCH * PATCH
KP = PD // P
HEADS, HD = 16, 16
SCALE = float(HD) ** -0.5
EPS = 1e-5
E = 8
H = 352
HS = 704
KH = -(-H // P)
KS = -(-HS // P)
NCH = 3
CW = T // NCH
XT = KC * T + P - NT + 1
SW = 384
TI = B // 2
TA = TI + B
XS = 8
TF = -(-T // P)
LAST = T - (TF - 1) * P
SLOTS = (2 * T + E * (P - 1)) // P
ROW = C + 4
NOBODY = 4096.0
BIG = 3.0e38


def rows_of(i):
    return P if i < TF - 1 else LAST


def fused_layer(nc, x, txt, Wp, tok_b, q_w1, q_b1, q_w2, q_b2, k_w1, k_b1, k_w2, k_b2, v_w, v_b,
                g_w, g_b, p_w, p_b, Wg, W1, W2, W3, Ws1, Ws2, Ws3, pos, out):
    h_dram = nc.dram_tensor("h_dram", [T, C], F32, kind="Internal").ap()
    mix_dram = nc.dram_tensor("mix_dram", [B, HEADS * N * HD], F32, kind="Internal").ap()
    slot_dram = nc.dram_tensor("slot_dram", [SLOTS * P, ROW], F32, kind="Internal").ap()
    out2d = out.rearrange("b t c -> (b t) c")

    with ExitStack() as ctx:
        at = [-(-nc.sbuf_base // 32) * 32]

        def place(name, shape, dt=F32, where=None):
            size = 4
            for n in shape[1:]:
                size *= n
            size = -(-size // 32) * 32
            off = at[0] if where is None else where[0]
            t = nc.alloc_sbuf_tensor_at(name, shape, dt, offset=off)
            if where is None:
                at[0] += size
            else:
                where[0] += size
                assert where[0] <= where[1], (name, where)
            return t

        def sem(name):
            return ctx.enter_context(nc.semaphore(name))

        e0 = at[0]
        w12 = place("w12", [P, E, KC, 2 * H])
        w3 = place("w3", [P, E, KH, C])
        under = [e0, at[0]]
        xst = place("xst", [P, CH, PATCH * IMG // 2], where=under)
        xrs = place("xrs", [P, CH, PATCH * IMG // 2], where=under)
        wpn = place("wpn", [P, KC, PD], where=under)
        wpT = place("wpT", [P, KP, C], where=under)
        patchT = place("patchT", [P, KP, B * NP], where=under)
        wnat = place("wnat", [P, 7, KC, C], where=under)
        QW1, KW1, VW, GW, QW2, KW2 = range(6)
        w12l = nc.alloc_sbuf_tensor_at("w12l", [P, E, KC, 2 * H], F32R, offset=e0)
        w3l = nc.alloc_sbuf_tensor_at("w3l", [P, E, KH, C], F32R, offset=e0 + E * KC * 2 * H * 4)
        w30 = e0 + E * KC * 2 * H * 4
        over = [w30, at[0]]
        xTl = place("xTl", [P, XT], F32R, where=over)
        k1Tl = place("k1Tl", [P, XT], F32R, where=over)
        over[0] = max(over[0], under[0])
        wTl2 = place("wTl2", [P, 2, KC, C], F32R, where=over)
        a0 = at[0]
        xTh = place("xTh", [P, XT], F32R)
        q1Th = place("q1Th", [P, XT], F32R)
        k1Th = place("k1Th", [P, XT], F32R)
        vT = place("vT", [P, KC, T])
        over = [a0, at[0]]
        w3h = nc.alloc_sbuf_tensor_at("w3h", [P, E, KH, C], F32R, offset=a0)
        ws12 = place("ws12", [P, KC, 2 * HS], where=over)
        x2T = place("x2T", [P, KC, T], where=over)
        sil = place("sil", [P, 2, SW], where=over)
        lg = place("lg", [P, TF, E], where=over)
        lg2 = place("lg2", [P, TF, E], where=over)
        eq = place("eq", [P, TF, E], where=over)
        oh1 = place("oh1", [P, TF, E], where=over)
        oh2 = place("oh2", [P, TF, E], where=over)
        both = place("both", [P, TF, E], where=over)
        assert over[0] >= a0 + E * KH * C * 4
        xn2 = place("xn2", [P, TF, ROW], where=over)
        m1 = place("m1", [P, TF], where=over)
        m2 = place("m2", [P, TF], where=over)
        mx1 = place("mx1", [P, TF], where=over)
        mx2 = place("mx2", [P, TF], where=over)
        dif = place("dif", [P, TF], where=over)
        ex = place("ex", [P, TF], where=over)
        exs = place("exs", [P, TF], where=over)
        cnt = place("cnt", [P, E], where=over)
        cmpt = place("cmpt", [P, E, TF], where=over)
        ntl = place("ntl", [P, E], where=over)
        cume = place("cume", [P, E, E], where=over)
        base = place("base", [P, E], where=over)
        upto = place("upto", [P, E], where=over)
        g0 = at[0]
        g = place("g", [P, TA, C])
        qk = place("qk", [P, 2, 3, 2 * C])
        spy = place("spy", [P, 3, 2 * C])
        q1s = place("q1s", [P, 4, CW], where=[at[0], at[0] + 3 * 2 * C * 4])
        spa = place("spa", [P, 3, 2 * C])
        l0 = at[0]
        wTl1 = nc.alloc_sbuf_tensor_at("wTl1", [P, 4, KC, C], F32R, offset=l0)
        mm2 = place("mm2", [P, 2, C])
        zs = place("zs", [P, 2, KC])
        zr = place("zr", [P, 2, KC])
        mm3 = place("mm3", [P, 2, C])
        ogi = place("ogi", [P, 2, C])
        ogt = place("ogt", [P, 2, C])
        assert l0 + 4 * KC * C * 4 <= at[0]
        over = [g0, at[0]]
        w12h = place("w12h", [P, E, KC, 2 * H], F32R, where=over)
        n0 = at[0]
        xn = place("xn", [P, TA, C])
        hI = place("hI", [P, TI, C])
        tx = place("tx", [P, B, C])
        over = [n0, at[0]]
        ws3 = place("ws3", [P, KS, C], where=over)
        hb = place("hb", [P, TF, C], where=over)
        hs0 = over[0]
        at[0] += 32
        q1Tl = nc.alloc_sbuf_tensor_at("q1Tl", [P, XT], F32R, offset=hs0)
        assert hs0 + XT * 4 <= at[0]
        w0 = at[0]
        wTh = place("wTh", [P, 6, KC, C], F32R)
        pwT = place("pwT", [P, KC, C])
        xs = place("xs", [P, XS, C], where=[w0, w0 + 4 * KC * C * 4])
        qkb = place("qkb", [P, 2 * C])
        posb = place("posb", [P, C])
        tokb = place("tokb", [P, C])
        hsT = place("hsT", [P, NCH, KS, SW], where=[hs0, at[0]])
        assert hs0 + KS * SW * 4 <= w0
        over = [hs0, at[0]]
        sl_xTh = place("sl_xTh", [P, 2, C], F32R, where=over)
        sl_xTl = place("sl_xTl", [P, 2, C], F32R, where=over)
        assert over[0] <= hs0 + KS * SW * 4
        sl_s = place("sl_s", [P, 2, H], where=over)
        sl_h = place("sl_h", [P, 2, H], where=over)
        sl_hTh = place("sl_hTh", [P, 2, KH * P], F32R, where=over)
        sl_hTl = place("sl_hTl", [P, 2, KH * P], F32R, where=over)
        sl_y = place("sl_y", [P, 2, C], where=over)
        sl_x = place("sl_x", [P, 2, C])
        xsT = place("xsT", [P, 2, C])
        ident = place("ident", [P, P])
        ones = place("ones", [P, P])
        before = place("before", [P, P])
        blocks = place("blocks", [P, KC, P])
        ident2 = place("ident2", [P, KC, P])
        gb = place("gb", [P, C])
        pb = place("pb", [P, C])
        cb = place("cb", [P, 3, KC])
        wg = place("wg", [P, KC, E])
        eps = place("eps", [P, 1])
        empty = place("empty", [P, ROW])
        st = place("st", [P, TA, 6])
        mv = place("mv", [P, TA, 2])
        rs = place("rs", [P, TA])
        rs2 = place("rs2", [P, TA])
        e_up = place("e_up", [P, E])
        e_dn = place("e_dn", [P, E])
        e_lt = place("e_lt", [P, E, E])
        tile_at = place("tile_at", [P, TF])
        slot_no = place("slot_no", [P, SLOTS])
        tok_no = place("tok_no", [P, TF])
        tail = place("tail", [P, SLOTS, ROW - C])
        dg = place("dg", [P, SLOTS])
        own = place("own", [P, SLOTS])
        gate = place("gate", [P, SLOTS])
        idx = place("idx", [P, SLOTS], U32)
        cmps = place("cmps", [P, SLOTS, E])
        adr = place("adr", [P, TF, E])
        prd = place("prd", [P, 2, TF, E])
        posf = place("posf", [P, 2, TF])
        posu = place("posu", [P, 2, TF], U32)
        esl = place("esl", [P, SLOTS])
        esu = place("esu", [P, SLOTS], U32)
        assert at[0] <= nc.sbuf_usable_end, at[0]

        ps = ctx.enter_context(nc.psum_tensor("ps", [P, 8, 512], F32))

        ld_wp, ld_tx, ld_wn = sem("ld_wp"), sem("ld_tx"), sem("ld_wn")
        ld_x = [sem(f"ld_x{c}") for c in range(CH)]
        ld_b, ld_ws, ld_we = sem("ld_b"), sem("ld_ws"), sem("ld_we")
        ld_xs = [sem(f"ld_xs{i}") for i in range(TF)]
        ld_hb = sem("ld_hb")
        ld_tail = sem("ld_tail")
        h_out, slot_zero = sem("h_out"), sem("slot_zero")
        mix_out = [sem(f"mix_out{b}") for b in range(B)]
        slot_out, out_init = sem("slot_out"), sem("out_init")
        sl_ld = [sem(f"sl_ld{i}") for i in range(2)]
        sl_add = sem("sl_add")
        k_set, k_ready, k_empty, w3_z = sem("k_set"), sem("k_ready"), sem("k_empty"), sem("w3_z")
        wp_t, wp_c, x_t, x_c = sem("wp_t"), sem("wp_c"), sem("x_t"), sem("x_c")
        xr_a, xr_d = sem("xr_a"), sem("xr_d")
        posb_r, emb, hi_r = sem("posb_r"), sem("emb"), sem("hi_r")
        w_t, w_c, w_l = sem("w_t"), sem("w_c"), sem("w_l")
        st_r, mv_r, sd_r, rs_r, xn_r, xn_t, xn_c, xn_l, pads = (
            sem(n) for n in ("st_r", "mv_r", "sd_r", "rs_r", "xn_r", "xn_t", "xn_c", "xn_l", "pads"))
        p1, p1_c, p1_h, p1_l, pg, pg_b, pg_c = (sem(n) for n in ("p1", "p1_c", "p1_h", "p1_l", "pg", "pg_b", "pg_c"))
        sp, sp_y, sp_a, sp_e, sp_l, sp_q = (sem(n) for n in ("sp", "sp_y", "sp_a", "sp_e", "sp_l", "sp_q"))
        at_a, at_m, at_m2, at_z, at_zs, at_r, at_zb, at_m3, at_o, at_g = (
            sem(n) for n in ("at_a", "at_m", "at_m2", "at_z", "at_zs", "at_r", "at_zb", "at_m3", "at_o", "at_g"))
        hb_r, xs_t, xs_c, y_p, h2_r, st2, mv2, sd2, rs2_r, n2, n2_t, n2_c, r_l, lg_r, lg_z = (
            sem(n) for n in ("hb_r", "xs_t", "xs_c", "y_p", "h2_r", "st2", "mv2", "sd2", "rs2_r", "n2",
                             "n2_t", "n2_c", "r_l", "lg_r", "lg_z"))
        rt, rt_both, rt_pre, rt_dif, rt_ex, rt_done, rt_row = (
            sem(n) for n in ("rt", "rt_both", "rt_pre", "rt_dif", "rt_ex", "rt_done", "rt_row"))
        we_h, we_l = sem("we_h"), sem("we_l")
        s_up, s_sil, s_h, s_dn, s_o = (sem(n) for n in ("s_up", "s_sil", "s_h", "s_dn", "s_o"))
        sl_tx, sl_xh, sl_xl, sl_a, sl_b, sl_si, sl_hr, sl_th, sl_hh, sl_hl, sl_yp, sl_yr, sl_d, sl_g = (
            sem(n) for n in ("sl_tx", "sl_xh", "sl_xl", "sl_a", "sl_b", "sl_si", "sl_hr", "sl_th", "sl_hh", "sl_hl",
                             "sl_yp", "sl_yr", "sl_d", "sl_g"))

        block = ctx.enter_context(nc.Block())

        def cols(u):
            if u < TI:
                return P, slice(u * P, (u + 1) * P)
            return NT, slice(B * NP + (u - TI) * NT, B * NP + (u - TI + 1) * NT)

        def tile_of(gp, j):
            return gp if j == 0 else TI + 2 * gp + j - 1

        def last_batch(i):
            return (i * P + rows_of(i) - 1) // N

        def by_row(t, c):
            return t[:, c, :].rearrange("p (r w k) -> p w r k", w=8, k=PATCH)

        def by_patch(t, c):
            return t[:, c, :].rearrange("p (w r k) -> p w r k", w=8, k=PATCH)

        CONSTS = 12
        P1 = [(c, w, m) for c in range(NCH - 1, -1, -1) for w in range(3) for m in range(KC)]
        IMAGES_AT = 3
        SPLITS = [n for n, (_c, w, _m) in enumerate(P1) if w < 2]
        BIASES = 10
        PAIR = (0, 2)
        UPS = [(m, c) for c in range(NCH) for m in range(KS)]
        GROUPS = [(2 * k, 2 * k + 1) for k in range(TF // 2)] + [(TF - 1,)]
        TURN2 = (5, 6)
        RANKS = P
        SPLIT0 = len(UPS) - E
        EARLY = 2 * (TI - 1)
        DOWN = (4, 5, 6, 7)

        def chunk(c):
            return slice(c * SW, min((c + 1) * SW, T))

        def wl(w):
            return wTl1[:, w, :, :] if w < QW2 else wTl2[:, w - QW2, :, :]

        def turned(f):
            w = 2 * NT if f < 4 else 2 * P
            c0 = B * NP + f * w if f < 4 else (f - 4) * w
            return c0, w

        def parts(x):
            return x[:, 0:KC * T].rearrange("p (k t) -> p k t", k=KC)

        def rows_in(s):
            return s.stop - s.start

        def load_rows(q, i, mix_rows):
            n = rows_of(i)
            for b in range((i * P) // N, last_batch(i) + 1):
                q.wait_ge(mix_out[b], 32)
            if i >= XS:
                q.wait_ge(xs_t, i - XS + 1)
            q.dma_start(xs[0:n, i % XS, :], mix_rows[i * P:i * P + n, :]).then_inc(ld_xs[i], 16)

        def load_x(q, hf):
            for c in (0, 2, 1):
                q.dma_start(xst[hf * 64:(hf + 1) * 64, c, :],
                            x[:, c].rearrange("b (n h r) w -> h b n (r w)", h=2, r=PATCH // 2)[hf]).then_inc(ld_x[c], 16)

        @block.sync
        def _(sp_):
            load_x(sp_, 0)
            sp_.dma_start(tx[0:NT, :, :], txt.rearrange("b t c -> t b c")).then_inc(ld_tx, 16)
            for n, w in enumerate((q_w1, k_w1, v_w, g_w, q_w2, k_w2, p_w)):
                sp_.dma_start(wnat[:, n, :, :], w.rearrange("(k p) c -> p k c", p=P)).then_inc(ld_wn, 16)
            sp_.dma_start(wg[:, :, :], Wg.rearrange("(k p) e -> p k e", p=P)).then_inc(ld_wn, 16)
            hv = h_dram.rearrange("(b t) c -> b t c", t=N)
            sp_.dma_start(hv[:, NP:N, :].rearrange("b t c -> b (t c)"), txt.rearrange("b t c -> b (t c)")).then_inc(h_out, 16)
            for i in range(TI):
                sp_.wait_ge(hi_r, i + 1)
                for j in range(2):
                    sp_.dma_start(hv[2 * i + j, 0:NP, :], hI[j * NP:(j + 1) * NP, i, :]).then_inc(h_out, 16)
            sp_.wait_ge(xn_t, 6)
            sp_.wait_ge(h_out, 16 * (1 + B))
            full = HS // P
            sp_.dma_start(ws3[:, 0:full, :], Ws3[0:full * P, :].rearrange("(k p) c -> p k c", p=P)).then_inc(ld_ws, 16)
            sp_.dma_start(ws3[0:HS - full * P, full, :], Ws3[full * P:HS, :]).then_inc(ld_ws, 16)
            sp_.wait_ge(xn_t, 6)
            sp_.dma_start(hb[:, 0:TF - 1, :], h_dram[0:(TF - 1) * P, :].rearrange("(i p) c -> p i c", p=P)).then_inc(ld_hb, 16)
            sp_.dma_start(hb[0:LAST, TF - 1, :], h_dram[(TF - 1) * P:T, :]).then_inc(ld_hb, 16)
            sp_.wait_ge(emb, TI)
            sp_.wait_ge(w_t, 7)
            for e in range(E):
                sp_.dma_start(w12[:, e, :, 0:H], W1[e].rearrange("(k p) h -> p k h", p=P)).then_inc(ld_we, 16)
                sp_.dma_start(w12[:, e, :, H:2 * H], W2[e].rearrange("(k p) h -> p k h", p=P)).then_inc(ld_we, 16)
            mix_rows = mix_dram.rearrange("b (t c) -> (b t) c", c=C)
            loaded = 0
            for b in range(B):
                v = mix_dram[b].rearrange("(h d n) -> d h n", h=HEADS, n=HD)
                r = (b % 2) * NP
                if b == B - 2:
                    sp_.wait_ge(sp, 3 * TI)
                    for n, w in enumerate((Ws1, Ws2)):
                        sp_.dma_start(ws12[:, :, n * HS:(n + 1) * HS], w.rearrange("(k p) h -> p k h", p=P)).then_inc(ld_ws, 16)
                    full = H // P
                    for e in range(E):
                        sp_.dma_start(w3[:, e, 0:full, :], W3[e, 0:full * P, :].rearrange("(k p) c -> p k c", p=P)).then_inc(ld_we, 16)
                        sp_.dma_start(w3[KH * P - H:P, e, full, :], W3[e, full * P:H, :]).then_inc(ld_we, 16)
                sp_.wait_ge(at_g, 2 * b + 2)
                sp_.dma_start(v[0:NP], ogi[r:r + NP, b % 2, :].rearrange("p (h n) -> p h n", n=HD)).then_inc(mix_out[b], 16)
                sp_.dma_start(v[NP:N], ogt[0:NT, b % 2, :].rearrange("p (h n) -> p h n", n=HD)).then_inc(mix_out[b], 16)
                while b % 2 and loaded < TF and last_batch(loaded) <= b:
                    load_rows(sp_, loaded, mix_rows)
                    loaded += 1
            for i in range(TF):
                sp_.wait_ge(s_o, i + 1)
                sp_.dma_start(out2d[i * P:i * P + rows_of(i), :], hb[0:rows_of(i), i, :]).then_inc(out_init, 16)
                if i == 4:
                    sp_.wait_ge(slot_out, 2 * TF * 16)
                    for s in range(2):
                        sp_.dma_start(sl_x[:, s, :], slot_dram[s * P:(s + 1) * P, 0:C]).then_inc(sl_ld[s], 16)
                    sp_.dma_start(tail[:, :, :], slot_dram[:, C:ROW].rearrange("(s p) c -> p s c", p=P)).then_inc(ld_tail, 16)

            def slot_load(s, j):
                sp_.wait_ge(sl_tx, s - 1)
                sp_.dma_start(sl_x[:, j, :], slot_dram[bass.ds(s * P, P), 0:C]).then_inc(sl_ld[j], 16)

            with sp_.Fori(1, SLOTS // 2) as i:
                slot_load(2 * i, 0)
                slot_load(2 * i + 1, 1)
            slot_load(SLOTS - 1, 0)
            sp_.wait_ge(out_init, TF * 16)
            sp_.wait_ge(sl_add, SLOTS * 16)

        @block.gpsimd
        def _(pool):
            pool.memset(ident[:, :], 0.0).then_inc(k_set, 1)
            pool.memset(ident2[:, :, :], 0.0).then_inc(k_set, 1)
            pool.memset(blocks[:, :, :], SCALE).then_inc(k_set, 1)
            pool.memset(before[:, :], 1.0).then_inc(k_set, 1)
            pool.memset(e_lt[:, :, :], 1.0).then_inc(k_set, 1)
            pool.memset(empty[:, :], 0.0).then_inc(k_set, 1)
            pool.memset(ones[:, :], 1.0).then_inc(k_ready, 1)
            pool.memset(eps[:, :], EPS).then_inc(k_ready, 1)
            pool.wait_ge(k_set, 6)
            pool.affine_select(out=ident[:, :], in_=ident[:, :], compare_op=ALU.not_equal, fill=1.0, base=0,
                               pattern=[[-1, P]], channel_multiplier=1).then_inc(k_ready, 1)
            pool.affine_select(out=ident2[:, :, :], in_=ident2[:, :, :], compare_op=ALU.not_equal, fill=1.0, base=0,
                               pattern=[[0, KC], [-1, P]], channel_multiplier=1).then_inc(k_ready, 1)
            pool.affine_select(out=before[:, :], in_=before[:, :], compare_op=ALU.is_gt, fill=0.0, base=0,
                               pattern=[[1, P]], channel_multiplier=-1).then_inc(k_ready, 1)
            pool.affine_select(out=e_lt[:, :, :], in_=e_lt[:, :, :], compare_op=ALU.is_gt, fill=0.0, base=0,
                               pattern=[[1, E], [-1, E]], channel_multiplier=0).then_inc(k_ready, 1)
            bl = blocks[:, :, :].rearrange("p k (b n) -> p (k b) n", n=HD)
            pool.affine_select(out=bl, in_=bl, compare_op=ALU.is_ge, fill=0.0, base=0,
                               pattern=[[0, KC], [-HD, P // HD], [0, HD]], channel_multiplier=1).then_inc(k_set, 1)
            pool.wait_ge(k_set, 7)
            pool.affine_select(out=bl, in_=bl, compare_op=ALU.is_ge, fill=0.0, base=HD - 1,
                               pattern=[[0, KC], [HD, P // HD], [0, HD]], channel_multiplier=-1).then_inc(k_ready, 1)
            for x in (xTh, q1Th, k1Th):
                pool.memset(x[:, KC * T:XT].bitcast(F32), 0.0).then_inc(pads, 1)
            io = dict(allow_small_or_imprecise_dtypes=True)
            pool.iota(e_up[:, :], pattern=[[1, E]], base=0, channel_multiplier=0, **io).then_inc(k_ready, 1)
            pool.iota(e_dn[:, :], pattern=[[-1, E]], base=E, channel_multiplier=0, **io).then_inc(k_ready, 1)
            pool.iota(tile_at[:, :], pattern=[[P, TF]], base=0, channel_multiplier=0, **io).then_inc(k_ready, 1)
            pool.iota(slot_no[:, :], pattern=[[1, SLOTS]], base=0, channel_multiplier=0, **io).then_inc(k_ready, 1)
            pool.iota(tok_no[:, :], pattern=[[P, TF]], base=0, channel_multiplier=1, **io).then_inc(k_ready, 1)
            row = lambda a: a.partition_broadcast(P)
            for j in range(2):
                pool.dma_start(posb[j * NP:(j + 1) * NP, :], pos).then_inc(ld_b, 16)
            pool.dma_start(tokb[:, :], row(tok_b)).then_inc(ld_b, 16)
            for n, w in enumerate((q_b1, k_b1, v_b)):
                pool.dma_start(cb[:, n, :], w.rearrange("(k p) -> p k", p=P), allow_slow_non_contiguous=True).then_inc(ld_b, 16)
            pool.dma_start(gb[:, :], row(g_b)).then_inc(ld_b, 16)
            pool.dma_start(qkb[:, 0:C], row(q_b2)).then_inc(ld_b, 16)
            pool.dma_start(qkb[:, C:2 * C], row(k_b2)).then_inc(ld_b, 16)
            pool.dma_start(pb[:, :], row(p_b)).then_inc(ld_b, 16)
            pool.memset(empty[:, C:C + 1], NOBODY).then_inc(k_empty, 1)
            pool.wait_ge(k_empty, 1)
            pool.wait_ge(ld_we, 16 * 2 * E)
            pool.dma_start(slot_dram.rearrange("(s p) c -> p s c", p=P),
                           empty[:, :].unsqueeze(1).broadcast_to([P, SLOTS, ROW])).then_inc(slot_zero, 16)
            pool.wait_ge(ld_hb, 32)
            pool.wait_ge(ld_b, 16 * BIASES)
            for i in range(TF):
                n = rows_of(i)
                pool.tensor_tensor(hb[0:n, i, :], hb[0:n, i, :], pb[0:n, :], ALU.add).then_inc(hb_r, 1)
            pool.wait_ge(sp, 3 * TI)
            pool.memset(w3[0:KH * P - H, :, KH - 1, :], 0.0).then_inc(w3_z, 1)
            pool.wait_ge(slot_zero, 16)
            pool.wait_ge(rt_done, 1)
            for i in range(TF):
                n = rows_of(i)
                for j in range(2):
                    pool.indirect_dma_start(
                        out=slot_dram, out_offset=bass.IndirectOffsetOnAxis(ap=posu[0:n, j, i:i + 1], axis=0),
                        in_=xn2[0:n, i, :], in_offset=None).then_inc(slot_out, 16)

            pool.wait_ge(out_init, TF * 16)
            pool.wait_ge(sl_g, 2)
            for s in range(SLOTS):
                pool.wait_ge(sl_yr, s + 1)
                if s:
                    pool.wait_ge(sl_add, 16 * s)
                pool.indirect_dma_start(
                    out=out2d, out_offset=bass.IndirectOffsetOnAxis(ap=idx[:, s:s + 1], axis=0),
                    in_=sl_y[:, s % 2, :], in_offset=None, bounds_check=T - 1, oob_is_err=False,
                    compute_op=ALU.add).then_inc(sl_add, 16)
            pool.wait_ge(sl_add, SLOTS * 16)

        @block.scalar
        def _(act):
            act.dma_start(wpn[:, :, :], Wp.rearrange("(k p) d -> p k d", p=P)).then_inc(ld_wp, 16)
            load_x(act, 1)

            for f in range(3):
                act.wait_ge(wp_t, f + 1)
                act.activation(wpT[:, 2 * f:2 * f + 2, :], ps[:, f, :].rearrange("p (a c) -> p a c", a=2), ACT.Copy).then_inc(wp_c, 1)
            act.wait_ge(ld_x[1], 32)
            act.activation(by_patch(xrs, 1), by_row(xst, 1), ACT.Copy).then_inc(xr_a, 1)
            act.wait_ge(k_ready, CONSTS)
            act.wait_ge(mv_r, B)
            act.activation(rs[:, TI:TA], mv[:, TI:TA, 1], ACT.Sqrt, bias=eps[:, 0:1]).then_inc(sd_r, 1)
            def weight_copy(f):
                act.wait_ge(w_t, f + 1)
                act.activation(wTh[:, f, :, :] if f < 6 else pwT[:, :, :],
                               ps[:, 4 + (f + 2) % 4, :].rearrange("p (a c) -> p a c", a=2), ACT.Copy).then_inc(w_c, 1)

            def xn_copy(f):
                act.wait_ge(xn_t, f + 1)
                c0, w = turned(f)
                act.activation(parts(xTh)[:, :, c0:c0 + w], ps[:, f % 4, :].rearrange("p (k c) -> p k c", k=KC)[:, :, 0:w],
                               ACT.Copy).then_inc(xn_c, 1)

            for f in range(4):
                weight_copy(f)
            for f in range(3):
                xn_copy(f)
            weight_copy(4)
            xn_copy(3)
            weight_copy(5)
            weight_copy(6)
            act.wait_ge(mv_r, TA)
            act.activation(rs[:, 0:TI], mv[:, 0:TI, 1], ACT.Sqrt, bias=eps[:, 0:1]).then_inc(sd_r, 1)

            def soft(v):
                r, _c = cols(tile_of(v // 3, v % 3))
                act.wait_ge(sp_y, v + 1)
                if v >= 3:
                    act.wait_ge(sp_q, v - 2)
                act.activation(spa[0:r, v % 3, :], spy[0:r, v % 3, :], ACT.Abs).then_inc(sp_a, 1)
                act.wait_ge(sp_a, v + 1)
                act.activation(spa[0:r, v % 3, :], spa[0:r, v % 3, :], ACT.Exp, scale=-1.0).then_inc(sp_e, 1)
                act.wait_ge(sp_e, v + 1)
                act.activation(spa[0:r, v % 3, :], spa[0:r, v % 3, :], ACT.Ln, bias=1.0).then_inc(sp_l, 1)

            def mix_copy(k):
                act.wait_ge(xs_t, k + 1)
                if k >= 1:
                    act.wait_ge(y_p, k)
                n = len(GROUPS[k])
                act.activation(xsT[:, 0:n, :], ps[:, 6, 0:n * C].rearrange("p (a c) -> p a c", c=C), ACT.Copy).then_inc(xs_c, 1)

            for n, (c, w, m) in enumerate(P1):
                if n == 0:
                    act.wait_ge(ld_b, 16 * BIASES)
                if n == IMAGES_AT:
                    xn_copy(4)
                    xn_copy(5)
                act.wait_ge(p1, n + 1)
                if w < 2:
                    i = SPLITS.index(n)
                    if i >= 4:
                        act.wait_ge(p1_l, i - 3)
                    y = q1s[:, i % 4, :]
                else:
                    y = vT[:, m, c * CW:(c + 1) * CW]
                act.activation(y, ps[:, 4 + n % 4, 0:CW], ACT.Gelu, bias=cb[:, w, m:m + 1]).then_inc(p1_c, 1)
            act.preload_act_table_set("natural_log_exp_and_others")
            for v in range(3):
                soft(v)
            for u in range(TA):
                act.wait_ge(pg_b, u + 1)
                r, _c = cols(u)
                act.activation(g[0:r, u, :], g[0:r, u, :], ACT.Gelu).then_inc(pg_c, 1)

            act.preload_act_table_set("natural_log_exp_and_others")
            for gp in range(TI):
                more = gp + 1 < TI
                if more:
                    soft(3 * gp + 3)
                    soft(3 * gp + 4)
                if gp >= 1:
                    mix_copy(gp - 1)
                if more:
                    soft(3 * gp + 5)

            def deviations(i0, i1):
                act.wait_ge(mv2, i1)
                act.activation(rs[:, i0:i1], mv[:, i0:i1, 1], ACT.Sqrt, bias=eps[:, 0:1]).then_inc(sd2, 1)

            def x2_copy(i):
                n = rows_of(i)
                act.wait_ge(n2_t, i + 1)
                act.activation(x2T[:, :, i * P:i * P + n], ps[:, TURN2[i % 2], 0:C].rearrange("p (k c) -> p k c", k=KC)[:, :, 0:n],
                               ACT.Copy).then_inc(n2_c, 1)

            def silu_up(v):
                m = P if UPS[v][0] < KS - 1 else HS - (KS - 1) * P
                w = rows_in(chunk(UPS[v][1]))
                act.wait_ge(s_up, v + 1)
                if v >= 2:
                    act.wait_ge(s_h, v - 1)
                act.activation(sil[0:m, v % 2, 0:w], ps[0:m, PAIR[v % 2], 0:w], ACT.Silu).then_inc(s_sil, 1)

            def high12(e):
                act.activation(w12h[:, e, :, :], w12[:, e, :, :], ACT.Copy).then_inc(we_h, 1)

            def high3(e):
                act.activation(w3h[:, e, :, :], w3[:, e, :, :], ACT.Copy).then_inc(we_h, 1)

            deviations(0, EARLY)
            for i in range(EARLY):
                x2_copy(i)
            silu_up(0)
            silu_up(1)
            mix_copy(TI - 1)
            silu_up(2)
            mix_copy(TI)
            silu_up(3)
            deviations(EARLY, TF)
            for v in range(4, KS):
                silu_up(v)
            for i in range(EARLY, TF):
                x2_copy(i)
            act.wait_ge(rt_dif, 1)
            act.activation(ex[:, :], dif[:, :], ACT.Exp).then_inc(rt_ex, 1)
            act.wait_ge(ld_we, 16 * 4 * E)
            act.wait_ge(at_g, 2 * B)
            act.wait_ge(mix_out[B - 2], 32)
            act.wait_ge(mix_out[B - 1], 32)
            for v in range(KS, len(UPS)):
                silu_up(v)
                if v >= SPLIT0:
                    high12(v - SPLIT0)
            act.wait_ge(s_h, len(UPS))
            act.wait_ge(rt_done, 1)
            act.wait_ge(w3_z, 1)
            for e in range(E):
                high3(e)

            def x_high(s, j):
                act.wait_ge(sl_tx, s + 1)
                act.activation(sl_xTh[:, j, :].rearrange("p (k c) -> p k c", k=KC), ps[:, 4 * j:4 * j + 2, 384:512],
                               ACT.Copy).then_inc(sl_xh, 1)

            def silu(s, j):
                act.wait_ge(sl_a, s + 1)
                act.activation(sl_s[:, j, :], ps[:, 4 * j, 0:H], ACT.Silu).then_inc(sl_si, 1)

            def h_high(s, j):
                act.wait_ge(sl_th, s + 1)
                act.activation(sl_hTh[:, j, :], ps[:, 4 * j + 2, 0:KH * P], ACT.Copy).then_inc(sl_hh, 1)

            def gated(s, j, first=False):
                act.wait_ge(sl_yp, s + 1)
                if not first:
                    act.wait_ge(sl_add, 16 * (s - 1))
                act.activation(sl_y[:, j, :], ps[:, 4 * j + 3, 0:C], ACT.Copy, scale=gate[:, bass.ds(s, 1)]).then_inc(sl_yr, 1)

            act.wait_ge(s_dn, 3)
            x_high(0, 0)
            x_high(1, 1)
            act.wait_ge(s_dn, TF)
            act.wait_ge(sl_g, 2)

            def act_body(s, j, first=False):
                h_high(s, j)
                x_high(s + 2, j)
                silu(s + 1, 1 - j)
                gated(s, j, first)

            silu(0, 0)
            act_body(0, 0, True)
            act_body(1, 1, True)
            with act.Fori(1, SLOTS // 2 - 1) as i:
                act_body(2 * i, 0)
                act_body(2 * i + 1, 1)
            act_body(SLOTS - 3, 0)
            h_high(SLOTS - 2, 1)
            silu(SLOTS - 1, 0)
            gated(SLOTS - 2, 1)
            h_high(SLOTS - 1, 0)
            gated(SLOTS - 1, 0)

        @block.vector
        def _(dve):
            for c in (0, 2):
                dve.wait_ge(ld_x[c], 32)
                dve.tensor_copy(by_patch(xrs, c), by_row(xst, c)).then_inc(xr_d, 1)
            dve.memset(mv[:, :, :], 0.0).then_inc(st_r, 1)
            dve.wait_ge(st_r, 1)
            dve.wait_ge(ld_tx, 16)
            for b in range(B):
                dve.bn_stats(st[0:NT, TI + b, :], tx[0:NT, b, :]).then_inc(st_r, 1)
            for b in range(B):
                dve.wait_ge(st_r, b + 2)
                dve.bn_aggr(mv[0:NT, TI + b, :], st[0:NT, TI + b, :]).then_inc(mv_r, 1)
            for f in range(KP):
                dve.wait_ge(x_t, f + 1)
                c, w0 = f // 2, (f % 2) * 4
                dve.tensor_copy(patchT[:, 2 * c:2 * c + 2, :].rearrange("p h (q w) -> p h q w", w=8)[:, :, :, w0:w0 + 4],
                                ps[:, 4 + f % 4, :].rearrange("p (w h q) -> p h q w", w=4, h=2)).then_inc(x_c, 1)
            dve.wait_ge(ld_b, 16 * BIASES)
            dve.tensor_tensor(posb[:, :], posb[:, :], tokb[:, :], ALU.add).then_inc(posb_r, 1)
            dve.wait_ge(posb_r, 1)
            dve.wait_ge(sd_r, 1)
            dve.reciprocal(rs2[:, TI:TA], rs[:, TI:TA]).then_inc(rs_r, 1)
            dve.wait_ge(rs_r, 1)
            for u in range(TI, TA):
                dve.tensor_scalar(xn[0:NT, u, :], tx[0:NT, u - TI, :], mv[0:NT, u, 0:1], rs2[0:NT, u:u + 1],
                                  ALU.subtract, ALU.mult).then_inc(xn_r, 1)
            def weight_low(f):
                dve.wait_ge(w_c, f + 1)
                dve.tensor_tensor(wl(f), ps[:, 4 + (f + 2) % 4, :].rearrange("p (a c) -> p a c", a=2), wTh[:, f, :, :],
                                  ALU.subtract).then_inc(w_l, 1)

            def xn_low(f):
                c0, w = turned(f)
                dve.wait_ge(xn_c, f + 1)
                dve.tensor_tensor(parts(xTl)[:, :, c0:c0 + w], ps[:, f % 4, :].rearrange("p (k c) -> p k c", k=KC)[:, :, 0:w],
                                  parts(xTh)[:, :, c0:c0 + w], ALU.subtract).then_inc(xn_l, 1)

            def split(i):
                c, w, m = P1[SPLITS[i]]
                cs = slice(m * T + c * CW, m * T + (c + 1) * CW)
                dve.wait_ge(p1_c, SPLITS[i] + 1)
                dve.tensor_copy((q1Th, k1Th)[w][:, cs], q1s[:, i % 4, :]).then_inc(p1_h, 1)
                dve.wait_ge(p1_h, i + 1)
                dve.tensor_tensor((q1Tl, k1Tl)[w][:, cs], q1s[:, i % 4, :], (q1Th, k1Th)[w][:, cs], ALU.subtract).then_inc(p1_l, 1)

            for f in range(4):
                weight_low(f)
            for i in range(TI):
                dve.wait_ge(emb, i + 1)
                dve.tensor_tensor(hI[:, i, :], ps[:, i, 0:C], posb[:, :], ALU.add).then_inc(hi_r, 1)
                dve.wait_ge(hi_r, i + 1)
                dve.bn_stats(st[:, i, :], hI[:, i, :]).then_inc(st_r, 1)
                dve.wait_ge(st_r, 2 + B + i)
                dve.bn_aggr(mv[:, i, :], st[:, i, :]).then_inc(mv_r, 1)
            for f in range(3):
                xn_low(f)
            weight_low(QW2)
            xn_low(3)
            weight_low(KW2)
            dve.wait_ge(w_t, 7)
            for x in (xTl, k1Tl, q1Tl):
                dve.memset(x[:, KC * T:XT].bitcast(F32), 0.0).then_inc(pads, 1)
            dve.wait_ge(sd_r, 2)
            dve.reciprocal(rs2[:, 0:TI], rs[:, 0:TI]).then_inc(rs_r, 1)
            dve.wait_ge(rs_r, 2)
            for u in range(TI):
                dve.tensor_scalar(xn[:, u, :], hI[:, u, :], mv[:, u, 0:1], rs2[:, u:u + 1],
                                  ALU.subtract, ALU.mult).then_inc(xn_r, 1)
            dve.wait_ge(h_out, 16 * (1 + B))
            split(0)
            xn_low(4)
            xn_low(5)
            for i in range(1, len(SPLITS)):
                split(i)

            def soft_in(v):
                r, _c = cols(tile_of(v // 3, v % 3))
                dve.wait_ge(sp, v + 1)
                if v >= 3:
                    dve.wait_ge(sp_q, v - 2)
                dve.tensor_tensor(spy[0:r, v % 3, :], ps[0:r, 4 + v % 2, :], qkb[0:r, :], ALU.add).then_inc(sp_y, 1)

            def soft_out(v):
                r, _c = cols(tile_of(v // 3, v % 3))
                dve.wait_ge(sp_l, v + 1)
                if v >= 6:
                    dve.wait_ge(at_a, 2 * (v // 3 - 1))
                dve.scalar_tensor_tensor(out=qk[0:r, (v // 3) % 2, v % 3, :], in0=spy[0:r, v % 3, :], scalar=0.0,
                                         in1=spa[0:r, v % 3, :], op0=ALU.max, op1=ALU.add).then_inc(sp_q, 1)

            def masked(b):
                j = b % 2
                dve.wait_ge(at_a, b + 1)
                if b >= 2:
                    dve.wait_ge(at_z, b - 1)
                dve.tensor_tensor(mm2[:, j, :], ps[:, j, 0:C], blocks[:, :, :].rearrange("p k c -> p (k c)"), ALU.mult).then_inc(at_m, 1)
                dve.wait_ge(at_m, b + 1)
                dve.tensor_tensor(mm2[:, j, :], mm2[:, j, :], ident2[:, :, :].rearrange("p k c -> p (k c)"), ALU.add).then_inc(at_m2, 1)

            def inverses(gp):
                for j in range(2):
                    dve.wait_ge(at_z, 2 * gp + j + 1)
                    dve.tensor_scalar(zs[:, j, :], ps[:, j, C:C + KC], float(C - 1), None, ALU.add).then_inc(at_zs, 1)
                dve.wait_ge(at_zs, 2 * gp + 2)
                if gp:
                    dve.wait_ge(at_zb, 2 * gp)
                dve.reciprocal(zr[:, :, :], zs[:, :, :]).then_inc(at_r, 1)

            def scaled(b):
                j = b % 2
                dve.wait_ge(at_zb, b + 1)
                if b >= 2:
                    dve.wait_ge(at_o, b - 1)
                dve.tensor_tensor(mm3[:, j, :], ps[:, j, C:2 * C], mm2[:, j, :], ALU.mult).then_inc(at_m3, 1)

            def gate_mix(b):
                j, r = b % 2, (b % 2) * NP
                dve.wait_ge(at_o, b + 1)
                if b == 0:
                    dve.wait_ge(pg_c, TA)
                if b >= 2:
                    dve.wait_ge(mix_out[b - 2], 32)
                dve.tensor_tensor(ogi[r:r + NP, j, :], ps[r:r + NP, 2 + j, 0:C], g[r:r + NP, b // 2, :], ALU.mult).then_inc(at_g, 1)
                dve.tensor_tensor(ogt[0:NT, j, :], ps[0:NT, 2 + j, C:2 * C], g[0:NT, TI + b, :], ALU.mult).then_inc(at_g, 1)

            def stream(k):
                dve.wait_ge(y_p, k + 1)
                for a, i in enumerate(GROUPS[k]):
                    n = rows_of(i)
                    dve.wait_ge(hb_r, i + 1)
                    dve.tensor_tensor(hb[0:n, i, :], ps[0:n, 7, a * C:(a + 1) * C], hb[0:n, i, :], ALU.add).then_inc(h2_r, 1)
                for i in GROUPS[k]:
                    n = rows_of(i)
                    dve.wait_ge(h2_r, i + 1)
                    dve.bn_stats(st[0:n, i, :], hb[0:n, i, :]).then_inc(st2, 1)
                for i in GROUPS[k]:
                    n = rows_of(i)
                    dve.wait_ge(st2, i + 1)
                    dve.bn_aggr(mv[0:n, i, :], st[0:n, i, :]).then_inc(mv2, 1)

            def normed(k, i0, i1):
                dve.wait_ge(sd2, k + 1)
                dve.reciprocal(rs2[:, i0:i1], rs[:, i0:i1]).then_inc(rs2_r, 1)
                dve.wait_ge(rs2_r, k + 1)
                for i in range(i0, i1):
                    n = rows_of(i)
                    dve.tensor_scalar(xn2[0:n, i, 0:C], hb[0:n, i, :], mv[0:n, i, 0:1], rs2[0:n, i:i + 1],
                                      ALU.subtract, ALU.mult).then_inc(n2, 1)

            for v in range(3):
                soft_in(v)
            for u in range(TA):
                r, _c = cols(u)
                dve.wait_ge(pg, u + 1)
                dve.tensor_tensor(g[0:r, u, :], ps[0:r, u % 4, 0:C], gb[0:r, :], ALU.add).then_inc(pg_b, 1)
                if u % 2 and u // 2 < 3:
                    soft_out(u // 2)
            for gp in range(TI):
                more = gp + 1 < TI
                v = 3 * gp + 3
                masked(2 * gp)
                masked(2 * gp + 1)
                if more:
                    soft_in(v)
                    soft_in(v + 1)
                inverses(gp)
                if more:
                    soft_in(v + 2)
                    soft_out(v)
                scaled(2 * gp)
                scaled(2 * gp + 1)
                if more:
                    soft_out(v + 1)
                if gp >= 1:
                    stream(gp - 1)
                if more:
                    soft_out(v + 2)
                gate_mix(2 * gp)
                gate_mix(2 * gp + 1)

            dve.wait_ge(at_o, B)
            dve.memset(lg[:, :, :], 0.0).then_inc(lg_z, 1)
            normed(0, 0, EARLY)

            def shared_h(v):
                m, c = UPS[v]
                r = P if m < KS - 1 else HS - m * P
                w = rows_in(chunk(c))
                dve.wait_ge(s_sil, v + 1)
                dve.tensor_tensor(hsT[0:r, c, m, 0:w], sil[0:r, v % 2, 0:w], ps[0:r, PAIR[v % 2] + 1, 0:w],
                                  ALU.mult).then_inc(s_h, 1)

            def low12(e):
                dve.wait_ge(we_h, e + 1)
                dve.tensor_tensor(w12l[:, e, :, :], w12[:, e, :, :], w12h[:, e, :, :], ALU.subtract).then_inc(we_l, 1)

            def low3(e):
                dve.wait_ge(we_h, E + e + 1)
                dve.tensor_tensor(w3l[:, e, :, :], w3[:, e, :, :], w3h[:, e, :, :], ALU.subtract).then_inc(we_l, 1)

            shared_h(0)
            shared_h(1)
            stream(TI - 1)
            shared_h(2)
            stream(TI)
            shared_h(3)
            normed(1, EARLY, TF)
            for v in range(4, KS):
                shared_h(v)
            dve.wait_ge(lg_z, 1)
            dve.wait_ge(r_l, TF)
            full = (TF - 1) * E
            dve.tensor_copy(lg[:, 0:TF - 1, :], ps[:, 4, 0:full].rearrange("p (t e) -> p t e", e=E)).then_inc(lg_r, 1)
            dve.tensor_copy(lg[0:LAST, TF - 1, :], ps[0:LAST, 4, full:full + E]).then_inc(lg_r, 1)
            dve.wait_ge(lg_r, 2)

            steps = [0]

            def then(ins, s=rt):
                steps[0] += 1
                ins.then_inc(rt, 1)
                dve.wait_ge(rt, steps[0])

            def wide(a):
                return a[:, :].unsqueeze(2).broadcast_to([P, TF, E])

            def per_tile(a):
                return a[:, :].unsqueeze(1).broadcast_to([P, TF, E])

            def best(l, mval, mx, oh):
                then(dve.tensor_reduce(mval[:, :], l[:, :, :], AX_X, ALU.max))
                then(dve.tensor_tensor(eq[:, :, :], l[:, :, :], wide(mval), ALU.is_equal))
                then(dve.tensor_tensor(eq[:, :, :], eq[:, :, :], per_tile(e_dn), ALU.mult))
                then(dve.tensor_reduce(mx[:, :], eq[:, :, :], AX_X, ALU.max))
                then(dve.tensor_tensor(oh[:, :, :], eq[:, :, :], wide(mx), ALU.is_equal))

            dve.wait_ge(k_ready, CONSTS)
            best(lg, m1, mx1, oh1)
            then(dve.scalar_tensor_tensor(out=lg2[:, :, :].rearrange("p t e -> p (t e)"),
                                          in0=oh1[:, :, :].rearrange("p t e -> p (t e)"), scalar=-BIG,
                                          in1=lg[:, :, :].rearrange("p t e -> p (t e)"), op0=ALU.mult, op1=ALU.add))
            best(lg2, m2, mx2, oh2)
            dve.tensor_tensor(both[:, :, :], oh1[:, :, :], oh2[:, :, :], ALU.add).then_inc(rt_both, 1)
            dve.tensor_tensor(dif[:, :], m2[:, :], m1[:, :], ALU.subtract).then_inc(rt_dif, 1)

            for v in range(KS, KS + 4):
                shared_h(v)
            dve.wait_ge(rt_ex, 1)
            then(dve.tensor_scalar(exs[:, :], ex[:, :], 1.0, None, ALU.add))
            then(dve.reciprocal(xn2[:, :, C + 1], exs[:, :]))
            then(dve.tensor_tensor(xn2[:, :, C + 2], ex[:, :], xn2[:, :, C + 1], ALU.mult))
            then(dve.tensor_scalar(xn2[:, :, C + 3], mx1[:, :], -1.0, float(E), ALU.mult, ALU.add))
            then(dve.tensor_copy(xn2[:, :, C], tok_no[:, :]))
            dve.wait_ge(rt_pre, 1)
            pre = ps[:, 4, RANKS:RANKS + (TF + 1) * E].rearrange("p (t e) -> p t e", e=E)
            then(dve.tensor_copy(cnt[:, :], pre[:, TF, :]))
            then(dve.tensor_tensor(cmpt[:, :, :], cnt[:, :].unsqueeze(2).broadcast_to([P, E, TF]),
                                   tile_at[:, :].unsqueeze(1).broadcast_to([P, E, TF]), ALU.is_gt))
            then(dve.tensor_reduce(ntl[:, :], cmpt[:, :, :], AX_X, ALU.add))
            then(dve.tensor_tensor(cume[:, :, :], e_lt[:, :, :], ntl[:, :].unsqueeze(1).broadcast_to([P, E, E]), ALU.mult))
            then(dve.tensor_reduce(base[:, :], cume[:, :, :], AX_X, ALU.add))
            then(dve.tensor_tensor(upto[:, :], base[:, :], ntl[:, :], ALU.add))
            then(dve.tensor_scalar(base[:, :], base[:, :], float(P), None, ALU.mult))
            then(dve.tensor_tensor(adr[:, :, :], pre[:, 0:TF, :], per_tile(base), ALU.add))
            then(dve.tensor_tensor(prd[:, 0, :, :], adr[:, :, :], oh1[:, :, :], ALU.mult))
            then(dve.tensor_tensor(prd[:, 1, :, :], adr[:, :, :], oh2[:, :, :], ALU.mult))
            then(dve.tensor_reduce(posf[:, :, :], prd[:, :, :, :], AX_X, ALU.add))
            then(dve.tensor_copy(posu[:, :, :], posf[:, :, :]))
            then(dve.tensor_tensor(cmps[:, :, :], upto[:, :].unsqueeze(1).broadcast_to([P, SLOTS, E]),
                                   slot_no[:, :].unsqueeze(2).broadcast_to([P, SLOTS, E]), ALU.is_le))
            then(dve.tensor_reduce(esl[:, :], cmps[:, :, :], AX_X, ALU.add))
            then(dve.tensor_scalar(esl[:, :], esl[:, :], float(E - 1), None, ALU.min))
            dve.tensor_copy(esu[:, :], esl[:, :]).then_inc(rt_done, 1)
            for v in range(KS + 4, len(UPS)):
                shared_h(v)
                low12(v - SPLIT0)
            for i in range(TF):
                n = rows_of(i)
                dve.wait_ge(s_dn, i + 1)
                dve.tensor_tensor(hb[0:n, i, :], ps[0:n, DOWN[i % 4], 0:C], hb[0:n, i, :], ALU.add).then_inc(s_o, 1)
                if i < E:
                    low3(i)

            def x_low(s, j):
                dve.wait_ge(sl_xh, s + 1)
                dve.tensor_tensor(sl_xTl[:, j, :].rearrange("p (k c) -> p k c", k=KC), ps[:, 4 * j:4 * j + 2, 384:512],
                                  sl_xTh[:, j, :].rearrange("p (k c) -> p k c", k=KC), ALU.subtract).then_inc(sl_xl, 1)

            x_low(0, 0)
            x_low(1, 1)
            dve.wait_ge(ld_tail, 16)
            dve.tensor_copy(idx[:, :], tail[:, :, 0]).then_inc(sl_g, 1)
            dve.tensor_tensor(dg[:, :], tail[:, :, 1], tail[:, :, 2], ALU.subtract).then_inc(sl_d, 1)
            dve.tensor_tensor(own[:, :], tail[:, :, 3], esl[:, :], ALU.is_equal).then_inc(sl_d, 1)
            dve.wait_ge(sl_d, 2)
            dve.tensor_tensor(dg[:, :], dg[:, :], own[:, :], ALU.mult).then_inc(sl_d, 1)
            dve.wait_ge(sl_d, 3)
            dve.tensor_tensor(gate[:, :], dg[:, :], tail[:, :, 2], ALU.add).then_inc(sl_g, 1)

            def h_low(s, j):
                dve.wait_ge(sl_hh, s + 1)
                dve.tensor_tensor(sl_hTl[:, j, :], ps[:, 4 * j + 2, 0:KH * P], sl_hTh[:, j, :], ALU.subtract).then_inc(sl_hl, 1)

            def h_prod(s, j):
                dve.wait_ge(sl_si, s + 1)
                dve.wait_ge(sl_b, s + 1)
                dve.tensor_tensor(sl_h[:, j, :], sl_s[:, j, :], ps[:, 4 * j + 1, 0:H], ALU.mult).then_inc(sl_hr, 1)

            def dve_body(s, j):
                h_low(s, j)
                x_low(s + 2, j)
                h_prod(s + 1, 1 - j)

            h_prod(0, 0)
            with dve.Fori(0, SLOTS // 2 - 1) as i:
                dve_body(2 * i, 0)
                dve_body(2 * i + 1, 1)
            dve_body(SLOTS - 3, 0)
            h_low(SLOTS - 2, 1)
            h_prod(SLOTS - 1, 0)
            h_low(SLOTS - 1, 0)

        @block.tensor
        def _(pe):
            pe.wait_ge(k_ready, CONSTS)
            pe.wait_ge(ld_wp, 16)
            for f in range(3):
                for kt in (2 * f, 2 * f + 1):
                    c0 = (kt % 2) * (PD // 2) + kt // 2
                    for k in range(KC):
                        ins = pe.transpose(ps[:, f, (kt % 2) * C + k * P:(kt % 2) * C + (k + 1) * P],
                                           wpn[:, k, c0:c0 + 3 * (P - 1) + 1:3], ident[:, :])
                ins.then_inc(wp_t, 1)
            pe.wait_ge(xr_d, 2)
            pe.wait_ge(xr_a, 1)
            for f in range(KP):
                if f >= 4:
                    pe.wait_ge(x_c, f - 3)
                for w in range(4):
                    c0 = ((f % 2) * 4 + w) * P
                    ins = pe.transpose(ps[:, 4 + f % 4, w * P:(w + 1) * P], xrs[:, f // 2, c0:c0 + P], ident[:, :])
                ins.then_inc(x_t, 1)
            def weight_turn(f):
                if f < 4:
                    pe.wait_ge(x_c, 3 + f)
                else:
                    pe.wait_ge(w_c, f - 3)
                    pe.wait_ge(w_l, f - 3)
                for k in range(KC):
                    for m in range(KC):
                        ins = pe.transpose(ps[:, 4 + (f + 2) % 4, k * C + m * P:k * C + (m + 1) * P],
                                           wnat[:, f, m, k * P:(k + 1) * P], ident[:, :])
                ins.then_inc(w_t, 1)

            pe.wait_ge(ld_wn, 16 * 8)
            for f in range(4):
                weight_turn(f)
            pe.wait_ge(x_c, KP)
            pe.wait_ge(wp_c, 3)
            for i in range(TI):
                for kt in range(KP):
                    ins = pe.matmul(ps[:, i, 0:C], patchT[:, kt, i * P:(i + 1) * P], wpT[:, kt, :],
                                    start=(kt == 0), stop=(kt == KP - 1))
                ins.then_inc(emb, 1)
            def xn_turn(f):
                r, u0, s = (NT, TI + 2 * f, 2 * f + 2) if f < 4 else (P, 2 * (f - 4), B + 2 * (f - 4) + 2)
                pe.wait_ge(xn_r, s)
                if f >= 4:
                    pe.wait_ge(xn_l, f - 3)
                else:
                    pe.wait_ge(hi_r, f + 1)
                for k in range(KC):
                    for j in range(2):
                        ins = pe.transpose(ps[:, f % 4, k * C + j * r:k * C + (j + 1) * r],
                                           xn[0:r, u0 + j, k * P:(k + 1) * P], ident[0:r, 0:r])
                ins.then_inc(xn_t, 1)

            for f in range(3):
                xn_turn(f)
            weight_turn(4)
            xn_turn(3)
            weight_turn(5)
            weight_turn(6)
            pe.wait_ge(pads, 6)
            for n, (c, w, m) in enumerate(P1):
                if n == 0:
                    pe.wait_ge(xn_l, 4)
                    pe.wait_ge(w_c, 7)
                if n < 4:
                    pe.wait_ge(w_l, min(n + 3, 6))
                if n == IMAGES_AT:
                    xn_turn(4)
                    xn_turn(5)
                if n == len(P1) // NCH:
                    pe.wait_ge(xn_l, 6)
                if n >= 4:
                    pe.wait_ge(p1_c, n - 3)
                for k in range(KC):
                    ms, cs = slice(m * P, (m + 1) * P), slice(k * T + c * CW, k * T + (c + 1) * CW)
                    passes = ((wTh[:, w, k, ms], xTh[:, cs]), (wTh[:, w, k, ms], xTl[:, cs]), (wl(w)[:, k, ms], xTh[:, cs]))
                    for a, (lhs, rhs) in enumerate(passes):
                        ins = pe.matmul(ps[:, 4 + n % 4, 0:CW], lhs, rhs, start=(k + a == 0), stop=(k == KC - 1 and a == 2))
                ins.then_inc(p1, 1)

            def token_major(out, src, cs, w):
                for k in range(KC):
                    c128 = slice(k * T + cs.start, k * T + cs.start + P)
                    passes = ((src[0], wTh[:, w, k, :]), (src[0], wl(w)[:, k, :]), (src[1], wTh[:, w, k, :]))
                    for a, (lhs, rhs) in enumerate(passes):
                        ins = pe.matmul(out, lhs[:, c128], rhs, start=(k + a == 0), stop=(k == KC - 1 and a == 2))
                return ins

            def layer2(v):
                cs = cols(tile_of(v // 3, v % 3))[1]
                if v >= 2:
                    pe.wait_ge(sp_y, v - 1)
                for n, (src, w) in enumerate((((q1Th, q1Tl), QW2), ((k1Th, k1Tl), KW2))):
                    ins = token_major(ps[:, 4 + v % 2, n * C:(n + 1) * C], src, cs, w)
                ins.then_inc(sp, 1)

            def gram(b):
                s, r = (b // 2) % 2, (b % 2) * NP
                pe.wait_ge(sp_q, 3 * (b // 2) + 3)
                if b >= 2:
                    pe.wait_ge(at_m3, b - 1)
                for m in range(KC):
                    qc, kc = slice(m * P, (m + 1) * P), slice(C + m * P, C + (m + 1) * P)
                    pe.matmul(ps[:, b % 2, qc], qk[r:r + NP, s, 0, kc], qk[r:r + NP, s, 0, qc], start=True, stop=False)
                    ins = pe.matmul(ps[:, b % 2, qc], qk[0:NT, s, 1 + b % 2, kc], qk[0:NT, s, 1 + b % 2, qc],
                                    start=False, stop=True)
                ins.then_inc(at_a, 1)

            def sums(b):
                pe.wait_ge(at_m2, b + 1)
                for m in range(KC):
                    ins = pe.matmul(ps[:, b % 2, C + m:C + m + 1], mm2[:, b % 2, m * P:(m + 1) * P], ones[:, 0:1],
                                    start=True, stop=True)
                ins.then_inc(at_z, 1)

            def spread(b):
                pe.wait_ge(at_r, b // 2 + 1)
                for m in range(KC):
                    ins = pe.matmul(ps[:, b % 2, C + m * P:C + (m + 1) * P], zr[:, b % 2, m:m + 1].broadcast_to([P, P]),
                                    ident[:, :], start=True, stop=True)
                ins.then_inc(at_zb, 1)

            def mixed(b):
                r = (b % 2) * NP
                pe.wait_ge(at_m3, b + 1)
                if b >= 2:
                    pe.wait_ge(at_g, 2 * (b - 1))
                for m in range(KC):
                    cs = slice(m * P, (m + 1) * P)
                    pe.matmul(ps[r:r + NP, 2 + b % 2, cs], vT[:, m, b * NP:(b + 1) * NP], mm3[:, b % 2, cs], start=True, stop=True)
                for m in range(KC):
                    cs = slice(m * P, (m + 1) * P)
                    ins = pe.matmul(ps[0:NT, 2 + b % 2, C + m * P:C + (m + 1) * P], vT[:, m, cols(TI + b)[1]],
                                    mm3[:, b % 2, cs], start=True, stop=True)
                ins.then_inc(at_o, 1)

            def project(k):
                for a, i in enumerate(GROUPS[k]):
                    n = rows_of(i)
                    pe.wait_ge(ld_xs[i], 16)
                    if k >= 1:
                        pe.wait_ge(xs_c, k)
                    for c in range(KC):
                        ins = pe.transpose(ps[:, 6, a * C + c * P:a * C + c * P + n], xs[0:n, i % XS, c * P:(c + 1) * P], ident[0:n, 0:n])
                    if n < P:
                        for c in range(KC):
                            ins = pe.transpose(ps[:, 6, c * P + n:(c + 1) * P], xs[0:P - n, i % XS, c * P:(c + 1) * P],
                                               ident[0:P - n, 0:P - n])
                ins.then_inc(xs_t, 1)
                pe.wait_ge(xs_c, k + 1)
                if k >= 1:
                    pe.wait_ge(h2_r, GROUPS[k][0])
                for a, i in enumerate(GROUPS[k]):
                    n = rows_of(i)
                    for c in range(KC):
                        ins = pe.matmul(ps[0:n, 7, a * C:(a + 1) * C], xsT[:, a, c * P:c * P + n], pwT[:, c, :],
                                        start=(c == 0), stop=(c == KC - 1))
                ins.then_inc(y_p, 1)

            def turn2(i):
                n = rows_of(i)
                pe.wait_ge(n2, i + 1)
                if i >= 2:
                    pe.wait_ge(n2_c, i - 1)
                for c in range(KC):
                    ins = pe.transpose(ps[:, TURN2[i % 2], c * P:c * P + n], xn2[0:n, i, c * P:(c + 1) * P], ident[0:n, 0:n])
                ins.then_inc(n2_t, 1)

            def route(i):
                n = rows_of(i)
                pe.wait_ge(n2_c, i + 1)
                for c in range(KC):
                    ins = pe.matmul(ps[0:n, 4, i * E:(i + 1) * E], x2T[:, c, i * P:i * P + n], wg[:, c, :],
                                    start=(c == 0), stop=(c == KC - 1))
                ins.then_inc(r_l, 1)

            pe.wait_ge(p1_c, len(P1))
            pe.wait_ge(p1_l, len(SPLITS))
            for v in range(3):
                layer2(v)
            for u in range(TA):
                if u >= 4:
                    pe.wait_ge(pg_b, u - 3)
                token_major(ps[:, u % 4, 0:C], (xTh, xTl), cols(u)[1], GW).then_inc(pg, 1)
            pe.wait_ge(pg_b, TA)
            for gp in range(TI):
                more = gp + 1 < TI
                v = 3 * gp + 3
                gram(2 * gp)
                gram(2 * gp + 1)
                if more:
                    layer2(v)
                    layer2(v + 1)
                sums(2 * gp)
                sums(2 * gp + 1)
                if more:
                    layer2(v + 2)
                spread(2 * gp)
                spread(2 * gp + 1)
                if gp >= 1:
                    project(gp - 1)
                mixed(2 * gp)
                mixed(2 * gp + 1)

            def shared_up(v):
                m, c = UPS[v]
                r = P if m < KS - 1 else HS - m * P
                cs = chunk(c)
                if v >= 2:
                    pe.wait_ge(s_h, v - 1)
                for n in range(2):
                    for k in range(KC):
                        ins = pe.matmul(ps[0:r, PAIR[v % 2] + n, 0:rows_in(cs)], ws12[:, k, n * HS + m * P:n * HS + m * P + r],
                                        x2T[:, k, cs], start=(k == 0), stop=(k == KC - 1))
                ins.then_inc(s_up, 1)

            pe.wait_ge(sp_y, 3 * TI)
            pe.wait_ge(xs_c, TI - 1)
            for i in range(EARLY + 1):
                if i < EARLY:
                    turn2(i)
                if i >= 1:
                    route(i - 1)
            pe.wait_ge(ld_ws, 16 * 4)
            pe.wait_ge(at_m3, B)
            pe.wait_ge(at_g, 2 * B)
            shared_up(0)
            shared_up(1)
            project(TI - 1)
            shared_up(2)
            project(TI)
            for v in range(3, KS):
                shared_up(v)
            for i in range(EARLY, TF):
                turn2(i)
            for i in range(EARLY, TF):
                route(i)
            for v in range(KS, KS + 3):
                shared_up(v)
            pe.wait_ge(rt_both, 1)
            full = (TF - 1) * E
            flat = both[:, :, :].rearrange("p t e -> p (t e)")
            pe.matmul(ps[:, 4, RANKS:RANKS + full], before[:, :], flat[:, 0:full], start=True, stop=False, skip_group_check=True)
            pe.matmul(ps[:, 4, RANKS + full:RANKS + full + E], before[0:LAST, :], flat[0:LAST, full:full + E], start=False, stop=False, skip_group_check=True)
            for t in range(TF):
                n = rows_of(t)
                ins = pe.matmul(ps[:, 4, RANKS + (t + 1) * E:RANKS + (TF + 1) * E], ones[0:n, :],
                                both[0:n, t, :].unsqueeze(1).broadcast_to([n, TF - t, E]),
                                start=False, stop=(t == TF - 1), skip_group_check=True)
            ins.then_inc(rt_pre, 1)
            for v in range(KS + 3, len(UPS)):
                shared_up(v)
            pe.wait_ge(rt_done, 1)
            for i in range(TF):
                n = rows_of(i)
                c, c0 = i * P // SW, i * P % SW
                if i % 3 == 0:
                    pe.wait_ge(s_h, (c + 1) * KS)
                if i >= 4:
                    pe.wait_ge(s_o, i - 3)
                for k in range(KS):
                    r = P if k < KS - 1 else HS - k * P
                    ins = pe.matmul(ps[0:n, DOWN[i % 4], 0:C], hsT[0:r, c, k, c0:c0 + n], ws3[0:r, k, :],
                                    start=(k == 0), stop=(k == KS - 1))
                ins.then_inc(s_dn, 1)

            def x_turn(s, j, i):
                pe.wait_ge(sl_ld[j], 16 * (i + 1))
                for k in range(KC):
                    ins = pe.transpose(ps[:, 4 * j + k, 384:512], sl_x[:, j, k * P:(k + 1) * P], ident[:, :])
                ins.then_inc(sl_tx, 1)

            def up(s, j, e):
                pe.wait_ge(sl_xl, s + 1)
                for n, done in ((0, sl_a), (1, sl_b)):
                    for k in range(KC):
                        at12 = bass.ds(e * (KC * 2 * H) + k * 2 * H + n * H, H)
                        for x, w in ((sl_xTh, w12hf), (sl_xTh, w12lf), (sl_xTl, w12hf)):
                            ins = pe.matmul(ps[:, 4 * j + n, 0:H], x[:, j, k * P:(k + 1) * P], w[:, at12],
                                            start=(k == 0 and w is w12hf and x is sl_xTh), stop=(k == KC - 1 and x is sl_xTl))
                    ins.then_inc(done, 1)

            def h_turn(s, j):
                pe.wait_ge(sl_hr, s + 1)
                for k in range(KH):
                    c0 = min(k * P, H - P)
                    ins = pe.transpose(ps[:, 4 * j + 2, k * P:(k + 1) * P], sl_h[:, j, c0:c0 + P], ident[:, :])
                ins.then_inc(sl_th, 1)

            def down(s, j, e, first=False):
                pe.wait_ge(sl_hl, s + 1)
                if not first:
                    pe.wait_ge(sl_yr, s - 1)
                for k in range(KH):
                    at3 = bass.ds(e * (KH * C) + k * C, C)
                    for h, w in ((sl_hTh, w3hf), (sl_hTh, w3lf), (sl_hTl, w3hf)):
                        ins = pe.matmul(ps[:, 4 * j + 3, 0:C], h[:, j, k * P:(k + 1) * P], w[:, at3],
                                        start=(k == 0 and w is w3hf and h is sl_hTh), stop=(k == KH - 1 and h is sl_hTl))
                ins.then_inc(sl_yp, 1)

            w12hf, w12lf = (w[:, :, :, :].rearrange("p e k h -> p (e k h)") for w in (w12h, w12l))
            w3hf, w3lf = (w[:, :, :, :].rearrange("p e k c -> p (e k c)") for w in (w3h, w3l))

            def expert(s):
                return pe.value_load(esu[0:1, bass.ds(s, 1)], min_val=0, max_val=E - 1)

            pe.wait_ge(s_h, len(UPS))
            x_turn(0, 0, 0)
            pe.wait_ge(s_o, TF)
            x_turn(1, 1, 0)
            pe.wait_ge(we_l, 2 * E)
            up(0, 0, expert(0))

            def pe_body(s, j, i, first=False, turn=True, more=True):
                e_next = expert(s + 1) if more else None
                h_turn(s, j)
                if turn:
                    x_turn(s + 2, j, i + 1)
                if more:
                    up(s + 1, 1 - j, e_next)
                down(s, j, expert(s), first)

            pe_body(0, 0, 0, True)
            pe_body(1, 1, 0, True)
            with pe.Fori(1, SLOTS // 2 - 1) as i:
                pe_body(2 * i, 0, i)
                pe_body(2 * i + 1, 1, i)
            i = SLOTS // 2 - 1
            pe_body(2 * i, 0, i)
            pe_body(2 * i + 1, 1, i, turn=False)
            pe_body(2 * i + 2, 0, i + 1, turn=False, more=False)


_INS = ['x', 'txt', 'L0_tok_Wp', 'L0_tok_b', 'L0_attn_q_w1', 'L0_attn_q_b1', 'L0_attn_q_w2', 'L0_attn_q_b2',
        'L0_attn_k_w1', 'L0_attn_k_b1', 'L0_attn_k_w2', 'L0_attn_k_b2', 'L0_attn_v_w', 'L0_attn_v_b',
        'L0_attn_g_w', 'L0_attn_g_b', 'L0_attn_p_w', 'L0_attn_p_b', 'L0_ffn_Wg', 'L0_ffn_W1', 'L0_ffn_W2',
        'L0_ffn_W3', 'L0_ffn_Ws1', 'L0_ffn_Ws2', 'L0_ffn_Ws3']


def position_table():
    import numpy as np
    side, quarter = IMG // PATCH, C // 4
    gh, gw = np.meshgrid(np.arange(side), np.arange(side), indexing="ij")
    factor = np.float32(10000.0) ** (np.arange(quarter, dtype=np.float32) / np.float32(quarter))
    h = gh.reshape(-1).astype(np.float32)[:, None] / factor
    w = gw.reshape(-1).astype(np.float32)[:, None] / factor
    return np.concatenate([np.sin(h), np.cos(h), np.sin(w), np.cos(w)], axis=-1).astype(np.float32)


def kernel(**inputs):
    import numpy as _np
    import concourse.bacc as _bacc
    from concourse import mybir as _mybir
    from concourse.bass_utils import run_bass_kernel_spmd as _run

    nc = _bacc.Bacc("TRN2", target_bir_lowering=False, num_devices=1)
    arrays, args = {}, []
    for name, a in [(n, inputs[n]) for n in _INS] + [("pos", position_table())]:
        a = _np.ascontiguousarray(a)
        arrays[f"in_{name}_dram"] = a
        args.append(nc.dram_tensor(f"in_{name}_dram", a.shape, _mybir.dt.from_np(a.dtype), kind="ExternalInput").ap())
    args.append(nc.dram_tensor("out_0_dram", (B, N, C), _mybir.dt.float32, kind="ExternalOutput").ap())
    fused_layer(nc, *args)
    r = _run(nc, [arrays], core_ids=[0])
    return r.results[0]["out_0_dram"]
```

```python
from contextlib import ExitStack

import concourse.bass as bass
from concourse import mybir

F32 = mybir.dt.float32
F32R = mybir.dt.float32r
U32 = mybir.dt.uint32
ALU = mybir.AluOpType
ACT = mybir.ActivationFunctionType
AX_X = mybir.AxisListType.X

P = 128
B, CH, IMG = 8, 3, 128
PATCH = 16
NP = (IMG // PATCH) ** 2
NT = 77
N = NP + NT
T = B * N
C = 256
KC = C // P
PD = CH * PATCH * PATCH
KP = PD // P
HEADS, HD = 16, 16
SCALE = float(HD) ** -0.5
EPS = 1e-5
E = 8
H = 352
HS = 704
KH = -(-H // P)
KS = -(-HS // P)
NCH = 3
CW = T // NCH
XT = KC * T + P - NT + 1
SW = 384
TI = B // 2
TA = TI + B
XS = 8
TF = -(-T // P)
LAST = T - (TF - 1) * P
SLOTS = (2 * T + E * (P - 1)) // P
ROW = C + 4
NOBODY = 4096.0
BIG = 3.0e38


def rows_of(i):
    return P if i < TF - 1 else LAST


def fused_layer(nc, x, txt, Wp, tok_b, q_w1, q_b1, q_w2, q_b2, k_w1, k_b1, k_w2, k_b2, v_w, v_b,
                g_w, g_b, p_w, p_b, Wg, W1, W2, W3, Ws1, Ws2, Ws3, pos, out):
    h_dram = nc.dram_tensor("h_dram", [T, C], F32, kind="Internal").ap()
    mix_dram = nc.dram_tensor("mix_dram", [B, HEADS * N * HD], F32, kind="Internal").ap()
    slot_dram = nc.dram_tensor("slot_dram", [SLOTS * P, ROW], F32, kind="Internal").ap()
    out2d = out.rearrange("b t c -> (b t) c")

    with ExitStack() as ctx:
        at = [-(-nc.sbuf_base // 32) * 32]

        def place(name, shape, dt=F32, where=None):
            size = 4
            for n in shape[1:]:
                size *= n
            size = -(-size // 32) * 32
            off = at[0] if where is None else where[0]
            t = nc.alloc_sbuf_tensor_at(name, shape, dt, offset=off)
            if where is None:
                at[0] += size
            else:
                where[0] += size
                assert where[0] <= where[1], (name, where)
            return t

        def sem(name):
            return ctx.enter_context(nc.semaphore(name))

        e0 = at[0]
        w12 = place("w12", [P, E, KC, 2 * H])
        w3 = place("w3", [P, E, KH, C])
        under = [e0, at[0]]
        xst = place("xst", [P, CH, PATCH * IMG // 2], where=under)
        xrs = place("xrs", [P, CH, PATCH * IMG // 2], where=under)
        wpn = place("wpn", [P, KC, PD], where=under)
        wpT = place("wpT", [P, KP, C], where=under)
        patchT = place("patchT", [P, KP, B * NP], where=under)
        wnat = place("wnat", [P, 7, KC, C], where=under)
        QW1, KW1, VW, GW, QW2, KW2 = range(6)
        w12l = nc.alloc_sbuf_tensor_at("w12l", [P, E, KC, 2 * H], F32R, offset=e0)
        w3l = nc.alloc_sbuf_tensor_at("w3l", [P, E, KH, C], F32R, offset=e0 + E * KC * 2 * H * 4)
        w30 = e0 + E * KC * 2 * H * 4
        over = [w30, at[0]]
        xTl = place("xTl", [P, XT], F32R, where=over)
        k1Tl = place("k1Tl", [P, XT], F32R, where=over)
        over[0] = max(over[0], under[0])
        wTl2 = place("wTl2", [P, 2, KC, C], F32R, where=over)
        a0 = at[0]
        xTh = place("xTh", [P, XT], F32R)
        q1Th = place("q1Th", [P, XT], F32R)
        k1Th = place("k1Th", [P, XT], F32R)
        vT = place("vT", [P, KC, T])
        over = [a0, at[0]]
        w3h = nc.alloc_sbuf_tensor_at("w3h", [P, E, KH, C], F32R, offset=a0)
        ws12l = nc.alloc_sbuf_tensor_at("ws12l", [P, 2, KC, KS * P], F32R, offset=a0)
        ws12 = place("ws12", [P, 2, KC, KS * P], where=over)
        x2Th = place("x2Th", [P, KC, TF * P], F32R, where=over)
        sil = place("sil", [P, 2, SW], where=over)
        lg = place("lg", [P, TF, E], where=over)
        lg2 = place("lg2", [P, TF, E], where=over)
        eq = place("eq", [P, TF, E], where=over)
        oh1 = place("oh1", [P, TF, E], where=over)
        oh2 = place("oh2", [P, TF, E], where=over)
        both = place("both", [P, TF, E], where=over)
        assert over[0] >= a0 + E * KH * C * 4
        xn2 = place("xn2", [P, TF, ROW], where=over)
        m1 = place("m1", [P, TF], where=over)
        m2 = place("m2", [P, TF], where=over)
        mx1 = place("mx1", [P, TF], where=over)
        mx2 = place("mx2", [P, TF], where=over)
        dif = place("dif", [P, TF], where=over)
        ex = place("ex", [P, TF], where=over)
        exs = place("exs", [P, TF], where=over)
        cnt = place("cnt", [P, E], where=over)
        cmpt = place("cmpt", [P, E, TF], where=over)
        ntl = place("ntl", [P, E], where=over)
        cume = place("cume", [P, E, E], where=over)
        base = place("base", [P, E], where=over)
        g0 = at[0]
        g = place("g", [P, TA, C])
        qk = place("qk", [P, 2, 3, 2 * C])
        spy = place("spy", [P, 3, 2 * C])
        q1s = place("q1s", [P, 4, CW], where=[at[0], at[0] + 3 * 2 * C * 4])
        spa = place("spa", [P, 3, 2 * C])
        l0 = at[0]
        wTl1 = nc.alloc_sbuf_tensor_at("wTl1", [P, 4, KC, C], F32R, offset=l0)
        mm2 = place("mm2", [P, 2, C])
        zs = place("zs", [P, 2, KC])
        zr = place("zr", [P, 2, KC])
        mm3 = place("mm3", [P, 2, C])
        ogi = place("ogi", [P, 2, C])
        ogt = place("ogt", [P, 2, C])
        assert l0 + 4 * KC * C * 4 <= at[0]
        over = [g0, at[0]]
        w12h = place("w12h", [P, E, KC, 2 * H], F32R, where=over)
        lgT = place("lgT", [P, T], where=[g0 + 3 * KC * 2 * H * 4, g0 + 4 * KC * 2 * H * 4])
        over = [g0 + E // 2 * KC * 2 * H * 4, at[0]]
        x2Tl = place("x2Tl", [P, KC, TF * P], F32R, where=over)
        ws12h = place("ws12h", [P, 2, KC, KS * P], F32R, where=over)
        assert over[0] <= g0 + E * KC * 2 * H * 4
        n0 = at[0]
        xn = place("xn", [P, TA, C])
        hI = place("hI", [P, TI, C])
        tx = place("tx", [P, B, C])
        over = [n0, at[0]]
        ws3 = place("ws3", [P, KS, C], where=over)
        hb = place("hb", [P, TF, C], where=over)
        hs0 = over[0]
        at[0] += 32
        q1Tl = nc.alloc_sbuf_tensor_at("q1Tl", [P, XT], F32R, offset=hs0)
        assert hs0 + XT * 4 <= at[0]
        w0 = at[0]
        wTh = place("wTh", [P, 6, KC, C], F32R)
        pwT = place("pwT", [P, KC, C])
        xs = place("xs", [P, XS, C], where=[w0, w0 + 4 * KC * C * 4])
        qkb = place("qkb", [P, 2 * C])
        posb = place("posb", [P, C])
        tokb = place("tokb", [P, C])
        hsT = place("hsT", [P, NCH, KS, SW], where=[hs0, at[0]])
        assert hs0 + KS * SW * 4 <= w0
        over = [hs0, at[0]]
        sl_xTh = place("sl_xTh", [P, 2, C], F32R, where=over)
        sl_xTl = place("sl_xTl", [P, 2, C], F32R, where=over)
        assert over[0] <= hs0 + KS * SW * 4
        sl_s = place("sl_s", [P, 2, H], where=over)
        sl_h = place("sl_h", [P, 2, H], where=over)
        sl_hTh = place("sl_hTh", [P, 2, KH * P], F32R, where=over)
        sl_hTl = place("sl_hTl", [P, 2, KH * P], F32R, where=over)
        sl_y = place("sl_y", [P, 2, C], where=over)
        sl_x = place("sl_x", [P, 2, C])
        xsT = place("xsT", [P, 2, C])
        ident = place("ident", [P, P])
        ones = place("ones", [P, P])
        before = place("before", [P, P])
        blocks = place("blocks", [P, KC, P])
        ident2 = place("ident2", [P, KC, P])
        gb = place("gb", [P, C])
        pb = place("pb", [P, C])
        cb = place("cb", [P, 3, KC])
        eps = place("eps", [P, 1])
        empty = place("empty", [P, ROW])
        st = place("st", [P, TA, 6])
        mv = place("mv", [P, TA, 2])
        rs = place("rs", [P, TA])
        rs2 = place("rs2", [P, TA])
        e_dn = place("e_dn", [P, E])
        e_lt = place("e_lt", [P, E, E])
        tile_at = place("tile_at", [P, TF])
        slot_no = place("slot_no", [P, SLOTS])
        tok_no = place("tok_no", [P, TF])
        tail = place("tail", [P, SLOTS, ROW - C])
        dg = place("dg", [P, SLOTS])
        own = place("own", [P, SLOTS])
        gate = place("gate", [P, SLOTS])
        idx = place("idx", [P, SLOTS], U32)
        cmps = place("cmps", [P, SLOTS, E])
        adr = place("adr", [P, TF, E])
        prd = place("prd", [P, 2, TF, E])
        posf = place("posf", [P, 2, TF])
        posu = place("posu", [P, 2, TF], U32)
        upto = place("upto", [P, E])
        esl = place("esl", [P, SLOTS])
        esu = place("esu", [P, SLOTS], U32)
        assert at[0] <= nc.sbuf_usable_end, at[0]

        ps = ctx.enter_context(nc.psum_tensor("ps", [P, 8, 512], F32))

        ld_wp, ld_tx, ld_wn = sem("ld_wp"), sem("ld_tx"), sem("ld_wn")
        ld_x = [sem(f"ld_x{c}") for c in range(CH)]
        ld_pos, ld_b, ld_ws, ld_we = sem("ld_pos"), sem("ld_b"), sem("ld_ws"), sem("ld_we")
        ld_xs = [sem(f"ld_xs{i}") for i in range(TF)]
        ld_hb = sem("ld_hb")
        ld_tail = sem("ld_tail")
        h_out, slot_zero = sem("h_out"), sem("slot_zero")
        mix_out = [sem(f"mix_out{b}") for b in range(B)]
        slot_out, out_init = sem("slot_out"), sem("out_init")
        sl_ld = [sem(f"sl_ld{i}") for i in range(2)]
        sl_add = sem("sl_add")
        k_set, k_ready, k_empty, w3_z = sem("k_set"), sem("k_ready"), sem("k_empty"), sem("w3_z")
        wp_t, wp_c, x_t, x_c, x_ca = sem("wp_t"), sem("wp_c"), sem("x_t"), sem("x_c"), sem("x_ca")
        xr_a, xr_d = sem("xr_a"), sem("xr_d")
        posb_r, emb, hi_r = sem("posb_r"), sem("emb"), sem("hi_r")
        w_t, w_c, w_l = sem("w_t"), sem("w_c"), sem("w_l")
        st_r, mv_r, sd_r, rs_r, xn_p, xn_r, xn_t, xn_c, xn_l, pads = (
            sem(n) for n in ("st_r", "mv_r", "sd_r", "rs_r", "xn_p", "xn_r", "xn_t", "xn_c", "xn_l", "pads"))
        p1, p1_c, p1_h, p1_l, pg, pg_b, pg_c = (sem(n) for n in ("p1", "p1_c", "p1_h", "p1_l", "pg", "pg_b", "pg_c"))
        sp, sp_y, sp_a, sp_e, sp_l, sp_q = (sem(n) for n in ("sp", "sp_y", "sp_a", "sp_e", "sp_l", "sp_q"))
        at_a, at_m, at_m2, at_z, at_zs, at_r, at_zb, at_m3, at_o, at_g = (
            sem(n) for n in ("at_a", "at_m", "at_m2", "at_z", "at_zs", "at_r", "at_zb", "at_m3", "at_o", "at_g"))
        hb_r, xs_t, xs_c, y_p, h2_r, st2, mv2, sd2, rs2_r, n2, n2_t, n2_c, n2_l, r_l, lg_r, lg_z = (
            sem(n) for n in ("hb_r", "xs_t", "xs_c", "y_p", "h2_r", "st2", "mv2", "sd2", "rs2_r", "n2",
                             "n2_t", "n2_c", "n2_l", "r_l", "lg_r", "lg_z"))
        rt, rt_both, rt_pre, rt_dif, rt_pos, rt_ex, rt_done = (
            sem(n) for n in ("rt", "rt_both", "rt_pre", "rt_dif", "rt_pos", "rt_ex", "rt_done"))
        we_h, we_l, we_p, ws_h, ws_l, ws_z, lg_t = (
            sem(n) for n in ("we_h", "we_l", "we_p", "ws_h", "ws_l", "ws_z", "lg_t"))
        s_up, s_sil, s_h, s_dn, s_o = (sem(n) for n in ("s_up", "s_sil", "s_h", "s_dn", "s_o"))
        sl_tx, sl_xh, sl_xl, sl_a, sl_b, sl_si, sl_hr, sl_th, sl_hh, sl_hl, sl_yp, sl_yr, sl_d, sl_g = (
            sem(n) for n in ("sl_tx", "sl_xh", "sl_xl", "sl_a", "sl_b", "sl_si", "sl_hr", "sl_th", "sl_hh", "sl_hl",
                             "sl_yp", "sl_yr", "sl_d", "sl_g"))

        block = ctx.enter_context(nc.Block())

        def cols(u):
            if u < TI:
                return P, slice(u * P, (u + 1) * P)
            return NT, slice(B * NP + (u - TI) * NT, B * NP + (u - TI + 1) * NT)

        def tile_of(gp, j):
            return gp if j == 0 else TI + 2 * gp + j - 1

        def last_batch(i):
            return (i * P + rows_of(i) - 1) // N

        def by_row(t, c):
            return t[:, c, :].rearrange("p (r w k) -> p w r k", w=8, k=PATCH)

        def by_patch(t, c):
            return t[:, c, :].rearrange("p (w r k) -> p w r k", w=8, k=PATCH)

        CONSTS = 11
        P1 = [(c, w, m) for c in range(NCH - 1, -1, -1) for w in range(3) for m in range(KC)]
        IMAGES_AT = 3
        SPLITS = [n for n, (_c, w, _m) in enumerate(P1) if w < 2]
        XORDER = (0, 1, 4, 5, 2, 3)
        DVE_TEXTS = 4
        BIASES = 7
        PAIR = (0, 2)
        UPS = [(m, 0) for m in (KS - 1, *range(KS - 1))] + [(KS - 1, 1), (KS - 1, 2)]
        UPS += [(m, c) for c in (1, 2) for m in range(KS - 1)]
        LOGITS = (0, KS, KS + 1)
        CHUNK_DONE = (KS, 2 * KS + 1, 3 * KS)
        GROUPS = [(2 * k, 2 * k + 1) for k in range(TF // 2)] + [(TF - 1,)]
        TURN2 = (4, 5)
        RANKS = P
        G_FIRST = 2
        POOL12, POOL3 = (0, 1, 2, 3), (4, 5, 6, 7)
        EARLY = 2 * (TI - 1)
        DOWN = (6, 7, 4, 5)

        def patches(q):
            c, w0 = XORDER[q] // 2, (XORDER[q] % 2) * 4
            return (patchT[:, 2 * c:2 * c + 2, :].rearrange("p h (q w) -> p h q w", w=8)[:, :, :, w0:w0 + 4],
                    ps[:, 4 + q % 4, :].rearrange("p (w h q) -> p h q w", w=4, h=2))

        def chunk(c):
            return slice(c * SW, min((c + 1) * SW, T))

        def hidden(m):
            return min(P, HS - m * P), slice(m * P, (m + 1) * P)

        def wl(w):
            return wTl1[:, w, :, :] if w < QW2 else wTl2[:, w - QW2, :, :]

        def turned(f):
            w = 2 * NT if f < 4 else 2 * P
            c0 = B * NP + f * w if f < 4 else (f - 4) * w
            return c0, w

        def parts(x):
            return x[:, 0:KC * T].rearrange("p (k t) -> p k t", k=KC)

        def rows_in(s):
            return s.stop - s.start

        def load_rows(q, i, mix_rows):
            n = rows_of(i)
            for b in range((i * P) // N, last_batch(i) + 1):
                q.wait_ge(mix_out[b], 32)
            if i >= XS:
                q.wait_ge(xs_t, i - XS + 1)
            q.dma_start(xs[0:n, i % XS, :], mix_rows[i * P:i * P + n, :]).then_inc(ld_xs[i], 16)

        def load_x(q, hf):
            for c in (0, 2, 1):
                q.dma_start(xst[hf * 64:(hf + 1) * 64, c, :],
                            x[:, c].rearrange("b (n h r) w -> h b n (r w)", h=2, r=PATCH // 2)[hf]).then_inc(ld_x[c], 16)

        @block.sync
        def _(sp_):
            load_x(sp_, 0)
            sp_.dma_start(tx[0:NT, :, :], txt.rearrange("b t c -> t b c")).then_inc(ld_tx, 16)
            for n, w in enumerate((q_w1, k_w1, v_w, g_w, q_w2, k_w2, p_w)):
                sp_.dma_start(wnat[:, n, :, :], w.rearrange("(k p) c -> p k c", p=P)).then_inc(ld_wn, 16)
            hv = h_dram.rearrange("(b t) c -> b t c", t=N)
            sp_.dma_start(hv[:, NP:N, :].rearrange("b t c -> b (t c)"), txt.rearrange("b t c -> b (t c)")).then_inc(h_out, 16)
            for i in range(TI):
                sp_.wait_ge(hi_r, i + 1)
                for j in range(2):
                    sp_.dma_start(hv[2 * i + j, 0:NP, :], hI[j * NP:(j + 1) * NP, i, :]).then_inc(h_out, 16)
            sp_.wait_ge(xn_t, 6)
            sp_.wait_ge(h_out, 16 * (1 + B))
            full = HS // P
            sp_.dma_start(ws3[:, 0:full, :], Ws3[0:full * P, :].rearrange("(k p) c -> p k c", p=P)).then_inc(ld_ws, 16)
            sp_.dma_start(ws3[0:HS - full * P, full, :], Ws3[full * P:HS, :]).then_inc(ld_ws, 16)
            sp_.wait_ge(xn_t, 6)
            sp_.dma_start(hb[:, 0:TF - 1, :], h_dram[0:(TF - 1) * P, :].rearrange("(i p) c -> p i c", p=P)).then_inc(ld_hb, 16)
            sp_.dma_start(hb[0:LAST, TF - 1, :], h_dram[(TF - 1) * P:T, :]).then_inc(ld_hb, 16)
            sp_.wait_ge(emb, TI)
            sp_.wait_ge(w_t, 7)
            for e in range(E):
                sp_.dma_start(w12[:, e, :, 0:H], W1[e].rearrange("(k p) h -> p k h", p=P)).then_inc(ld_we, 16)
                sp_.dma_start(w12[:, e, :, H:2 * H], W2[e].rearrange("(k p) h -> p k h", p=P)).then_inc(ld_we, 16)
            mix_rows = mix_dram.rearrange("b (t c) -> (b t) c", c=C)
            loaded = 0
            for b in range(B):
                v = mix_dram[b].rearrange("(h d n) -> d h n", h=HEADS, n=HD)
                r = (b % 2) * NP
                if b == B - 4:
                    sp_.wait_ge(sp, 3 * TI)
                    for n, w in enumerate((Ws1, Ws2)):
                        sp_.dma_start(ws12[:, n, :, 0:HS], w.rearrange("(k p) h -> p k h", p=P)).then_inc(ld_ws, 16)
                    sp_.dma_start(ws12[:, 0, :, HS:HS + E], Wg.rearrange("(k p) e -> p k e", p=P)).then_inc(ld_ws, 16)
                sp_.wait_ge(at_g, 2 * b + 2)
                sp_.dma_start(v[0:NP], ogi[r:r + NP, b % 2, :].rearrange("p (h n) -> p h n", n=HD)).then_inc(mix_out[b], 16)
                sp_.dma_start(v[NP:N], ogt[0:NT, b % 2, :].rearrange("p (h n) -> p h n", n=HD)).then_inc(mix_out[b], 16)
                while b % 2 and loaded < TF and last_batch(loaded) <= b:
                    load_rows(sp_, loaded, mix_rows)
                    loaded += 1
            full = H // P
            for e in range(E):
                sp_.dma_start(w3[:, e, 0:full, :], W3[e, 0:full * P, :].rearrange("(k p) c -> p k c", p=P)).then_inc(ld_we, 16)
                sp_.dma_start(w3[KH * P - H:P, e, full, :], W3[e, full * P:H, :]).then_inc(ld_we, 16)
            for i in range(TF):
                sp_.wait_ge(s_o, i + 1)
                sp_.dma_start(out2d[i * P:i * P + rows_of(i), :], hb[0:rows_of(i), i, :]).then_inc(out_init, 16)
                if i == 4:
                    sp_.wait_ge(slot_out, 2 * TF * 16)
                    for s in range(2):
                        sp_.dma_start(sl_x[:, s, :], slot_dram[s * P:(s + 1) * P, 0:C]).then_inc(sl_ld[s], 16)
                    sp_.dma_start(tail[:, :, :], slot_dram[:, C:ROW].rearrange("(s p) c -> p s c", p=P)).then_inc(ld_tail, 16)

            def slot_load(s, j):
                sp_.wait_ge(sl_tx, s - 1)
                sp_.dma_start(sl_x[:, j, :], slot_dram[bass.ds(s * P, P), 0:C]).then_inc(sl_ld[j], 16)

            with sp_.Fori(1, SLOTS // 2) as i:
                slot_load(2 * i, 0)
                slot_load(2 * i + 1, 1)
            slot_load(SLOTS - 1, 0)
            sp_.wait_ge(out_init, TF * 16)
            sp_.wait_ge(sl_add, SLOTS * 16)

        @block.gpsimd
        def _(pool):
            pool.memset(ident[:, :], 0.0).then_inc(k_set, 1)
            pool.memset(ident2[:, :, :], 0.0).then_inc(k_set, 1)
            pool.memset(blocks[:, :, :], SCALE).then_inc(k_set, 1)
            pool.memset(before[:, :], 1.0).then_inc(k_set, 1)
            pool.memset(e_lt[:, :, :], 1.0).then_inc(k_set, 1)
            pool.memset(empty[:, :], 0.0).then_inc(k_set, 1)
            pool.memset(ones[:, :], 1.0).then_inc(k_ready, 1)
            pool.memset(eps[:, :], EPS).then_inc(k_ready, 1)
            pool.wait_ge(k_set, 6)
            pool.affine_select(out=ident[:, :], in_=ident[:, :], compare_op=ALU.not_equal, fill=1.0, base=0,
                               pattern=[[-1, P]], channel_multiplier=1).then_inc(k_ready, 1)
            pool.affine_select(out=ident2[:, :, :], in_=ident2[:, :, :], compare_op=ALU.not_equal, fill=1.0, base=0,
                               pattern=[[0, KC], [-1, P]], channel_multiplier=1).then_inc(k_ready, 1)
            pool.affine_select(out=before[:, :], in_=before[:, :], compare_op=ALU.is_gt, fill=0.0, base=0,
                               pattern=[[1, P]], channel_multiplier=-1).then_inc(k_ready, 1)
            pool.affine_select(out=e_lt[:, :, :], in_=e_lt[:, :, :], compare_op=ALU.is_gt, fill=0.0, base=0,
                               pattern=[[1, E], [-1, E]], channel_multiplier=0).then_inc(k_ready, 1)
            bl = blocks[:, :, :].rearrange("p k (b n) -> p (k b) n", n=HD)
            pool.affine_select(out=bl, in_=bl, compare_op=ALU.is_ge, fill=0.0, base=0,
                               pattern=[[0, KC], [-HD, P // HD], [0, HD]], channel_multiplier=1).then_inc(k_set, 1)
            pool.wait_ge(k_set, 7)
            pool.affine_select(out=bl, in_=bl, compare_op=ALU.is_ge, fill=0.0, base=HD - 1,
                               pattern=[[0, KC], [HD, P // HD], [0, HD]], channel_multiplier=-1).then_inc(k_ready, 1)
            for x in (xTh, q1Th, k1Th):
                pool.memset(x[:, KC * T:XT].bitcast(F32), 0.0).then_inc(pads, 1)
            io = dict(allow_small_or_imprecise_dtypes=True)
            pool.iota(e_dn[:, :], pattern=[[-1, E]], base=E, channel_multiplier=0, **io).then_inc(k_ready, 1)
            pool.iota(tile_at[:, :], pattern=[[P, TF]], base=0, channel_multiplier=0, **io).then_inc(k_ready, 1)
            pool.iota(slot_no[:, :], pattern=[[1, SLOTS]], base=0, channel_multiplier=0, **io).then_inc(k_ready, 1)
            pool.iota(tok_no[:, :], pattern=[[P, TF]], base=0, channel_multiplier=1, **io).then_inc(k_ready, 1)
            row = lambda a: a.partition_broadcast(P)
            for j in range(2):
                pool.dma_start(posb[j * NP:(j + 1) * NP, :], pos).then_inc(ld_pos, 16)
            pool.dma_start(tokb[:, :], row(tok_b)).then_inc(ld_pos, 16)
            for n, w in enumerate((q_b1, k_b1, v_b)):
                pool.dma_start(cb[:, n, :], w.rearrange("(k p) -> p k", p=P), allow_slow_non_contiguous=True).then_inc(ld_b, 16)
            pool.dma_start(gb[:, :], row(g_b)).then_inc(ld_b, 16)
            pool.dma_start(qkb[:, 0:C], row(q_b2)).then_inc(ld_b, 16)
            pool.dma_start(qkb[:, C:2 * C], row(k_b2)).then_inc(ld_b, 16)
            pool.dma_start(pb[:, :], row(p_b)).then_inc(ld_b, 16)
            pool.wait_ge(rs_r, 1)
            for u in range(TI + DVE_TEXTS, TA):
                pool.tensor_scalar(xn[0:NT, u, :], tx[0:NT, u - TI, :], mv[0:NT, u, 0:1], rs2[0:NT, u:u + 1],
                                   ALU.subtract, ALU.mult).then_inc(xn_p, 1)
            pool.memset(empty[:, C:C + 1], NOBODY).then_inc(k_empty, 1)
            pool.wait_ge(k_empty, 1)
            pool.wait_ge(ld_we, 16 * 2 * E)
            pool.dma_start(slot_dram.rearrange("(s p) c -> p s c", p=P),
                           empty[:, :].unsqueeze(1).broadcast_to([P, SLOTS, ROW])).then_inc(slot_zero, 16)
            pool.wait_ge(ld_hb, 32)
            pool.wait_ge(ld_b, 16 * BIASES)
            for i in range(TF):
                n = rows_of(i)
                pool.tensor_tensor(hb[0:n, i, :], hb[0:n, i, :], pb[0:n, :], ALU.add).then_inc(hb_r, 1)
            pool.wait_ge(sp, 3 * TI)
            pool.memset(ws12[:, 0, :, HS + E:KS * P], 0.0).then_inc(ws_z, 1)
            pool.memset(ws12[:, 1, :, HS:KS * P], 0.0).then_inc(ws_z, 1)
            pool.memset(w3[0:KH * P - H, :, KH - 1, :], 0.0).then_inc(w3_z, 1)
            def low(x, xl, xh, e, before):
                pool.wait_ge(we_h, before + 1)
                pool.tensor_tensor(xl[:, e, :, :], x[:, e, :, :], xh[:, e, :, :], ALU.subtract).then_inc(we_p, 1)

            for e in POOL12:
                low(w12, w12l, w12h, e, e)
            pool.wait_ge(slot_zero, 16)
            pool.wait_ge(rt_pos, 1)
            for i in range(TF):
                n = rows_of(i)
                for j in range(2):
                    pool.indirect_dma_start(
                        out=slot_dram, out_offset=bass.IndirectOffsetOnAxis(ap=posu[0:n, j, i:i + 1], axis=0),
                        in_=xn2[0:n, i, :], in_offset=None).then_inc(slot_out, 16)

            for e in POOL3:
                low(w3, w3l, w3h, e, E + e)
            pool.wait_ge(out_init, TF * 16)
            pool.wait_ge(sl_g, 2)
            for s in range(SLOTS):
                pool.wait_ge(sl_yr, s + 1)
                if s:
                    pool.wait_ge(sl_add, 16 * s)
                pool.indirect_dma_start(
                    out=out2d, out_offset=bass.IndirectOffsetOnAxis(ap=idx[:, s:s + 1], axis=0),
                    in_=sl_y[:, s % 2, :], in_offset=None, bounds_check=T - 1, oob_is_err=False,
                    compute_op=ALU.add).then_inc(sl_add, 16)
            pool.wait_ge(sl_add, SLOTS * 16)

        @block.scalar
        def _(act):
            act.dma_start(wpn[:, :, :], Wp.rearrange("(k p) d -> p k d", p=P)).then_inc(ld_wp, 16)
            load_x(act, 1)

            for f in range(3):
                act.wait_ge(wp_t, f + 1)
                act.activation(wpT[:, 2 * f:2 * f + 2, :], ps[:, f, :].rearrange("p (a c) -> p a c", a=2), ACT.Copy).then_inc(wp_c, 1)
            act.wait_ge(ld_x[1], 32)
            act.activation(by_patch(xrs, 1), by_row(xst, 1), ACT.Copy).then_inc(xr_a, 1)
            for q in range(4, KP):
                act.wait_ge(x_t, q + 1)
                act.activation(*patches(q), ACT.Copy).then_inc(x_ca, 1)
            act.wait_ge(k_ready, CONSTS)
            act.wait_ge(mv_r, B)
            act.activation(rs[:, TI:TA], mv[:, TI:TA, 1], ACT.Sqrt, bias=eps[:, 0:1]).then_inc(sd_r, 1)
            def weight_copy(f):
                act.wait_ge(w_t, f + 1)
                act.activation(wTh[:, f, :, :] if f < 6 else pwT[:, :, :],
                               ps[:, 4 + (f + 2) % 4, :].rearrange("p (a c) -> p a c", a=2), ACT.Copy).then_inc(w_c, 1)

            def xn_copy(f):
                act.wait_ge(xn_t, f + 1)
                c0, w = turned(f)
                act.activation(parts(xTh)[:, :, c0:c0 + w], ps[:, f % 4, :].rearrange("p (k c) -> p k c", k=KC)[:, :, 0:w],
                               ACT.Copy).then_inc(xn_c, 1)

            for f in range(4):
                weight_copy(f)
            xn_copy(0)
            xn_copy(1)
            weight_copy(4)
            weight_copy(5)
            xn_copy(2)
            weight_copy(6)
            xn_copy(3)
            act.wait_ge(mv_r, TA)
            act.activation(rs[:, 0:TI], mv[:, 0:TI, 1], ACT.Sqrt, bias=eps[:, 0:1]).then_inc(sd_r, 1)

            def soft(v):
                r, _c = cols(tile_of(v // 3, v % 3))
                act.wait_ge(sp_y, v + 1)
                if v >= 3:
                    act.wait_ge(sp_q, v - 2)
                act.activation(spa[0:r, v % 3, :], spy[0:r, v % 3, :], ACT.Abs).then_inc(sp_a, 1)
                act.wait_ge(sp_a, v + 1)
                act.activation(spa[0:r, v % 3, :], spa[0:r, v % 3, :], ACT.Exp, scale=-1.0).then_inc(sp_e, 1)
                act.wait_ge(sp_e, v + 1)
                act.activation(spa[0:r, v % 3, :], spa[0:r, v % 3, :], ACT.Ln, bias=1.0).then_inc(sp_l, 1)

            def mix_copy(k):
                act.wait_ge(xs_t, k + 1)
                if k >= 1:
                    act.wait_ge(y_p, k)
                n = len(GROUPS[k])
                act.activation(xsT[:, 0:n, :], ps[:, 6, 0:n * C].rearrange("p (a c) -> p a c", c=C), ACT.Copy).then_inc(xs_c, 1)

            for n, (c, w, m) in enumerate(P1):
                if n == 0:
                    act.wait_ge(ld_b, 16 * BIASES)
                if n == IMAGES_AT:
                    xn_copy(4)
                    xn_copy(5)
                act.wait_ge(p1, n + 1)
                if w < 2:
                    i = SPLITS.index(n)
                    if i >= 4:
                        act.wait_ge(p1_l, i - 3)
                    y = q1s[:, i % 4, :]
                else:
                    y = vT[:, m, c * CW:(c + 1) * CW]
                act.activation(y, ps[:, 4 + n % 4, 0:CW], ACT.Gelu, bias=cb[:, w, m:m + 1]).then_inc(p1_c, 1)
            act.preload_act_table_set("natural_log_exp_and_others")
            for v in range(3):
                soft(v)
            for u in range(TA):
                act.wait_ge(pg_b, u + 1)
                r, _c = cols(u)
                act.activation(g[0:r, u, :], g[0:r, u, :], ACT.Gelu).then_inc(pg_c, 1)

            act.preload_act_table_set("natural_log_exp_and_others")
            for gp in range(TI):
                more = gp + 1 < TI
                if more:
                    soft(3 * gp + 3)
                    soft(3 * gp + 4)
                if gp >= 1:
                    mix_copy(gp - 1)
                if more:
                    soft(3 * gp + 5)

            def deviations(i0, i1):
                act.wait_ge(mv2, i1)
                act.activation(rs[:, i0:i1], mv[:, i0:i1, 1], ACT.Sqrt, bias=eps[:, 0:1]).then_inc(sd2, 1)

            def x2_copy(i):
                n = rows_of(i)
                act.wait_ge(n2_t, i + 1)
                act.activation(x2Th[:, :, i * P:i * P + n], ps[:, TURN2[i % 2], 0:C].rearrange("p (k c) -> p k c", k=KC)[:, :, 0:n],
                               ACT.Copy).then_inc(n2_c, 1)

            def shared_high(n):
                act.activation(ws12h[:, n, :, :], ws12[:, n, :, :], ACT.Copy).then_inc(ws_h, 1)

            def silu_up(v):
                r = hidden(UPS[v][0])[0]
                w = rows_in(chunk(UPS[v][1]))
                act.wait_ge(s_up, v + 1)
                if v >= 2:
                    act.wait_ge(s_h, v - 1)
                act.activation(sil[0:r, v % 2, 0:w], ps[0:r, PAIR[v % 2], 0:w], ACT.Silu).then_inc(s_sil, 1)

            def high12(e):
                act.activation(w12h[:, e, :, :], w12[:, e, :, :], ACT.Copy).then_inc(we_h, 1)

            def high3(e):
                act.activation(w3h[:, e, :, :], w3[:, e, :, :], ACT.Copy).then_inc(we_h, 1)

            act.wait_ge(ld_ws, 16 * 5)
            act.wait_ge(ws_z, 2)
            act.wait_ge(at_m3, B)
            shared_high(0)
            deviations(0, EARLY)
            act.wait_ge(at_o, B)
            act.wait_ge(mix_out[B - 2], 32)
            act.wait_ge(mix_out[B - 1], 32)
            shared_high(1)
            mix_copy(TI - 1)
            for i in range(4):
                x2_copy(i)
            mix_copy(TI)
            deviations(EARLY, TF)
            silu_up(0)
            for i in range(4, EARLY):
                x2_copy(i)
            for v in range(1, 4):
                silu_up(v)
                x2_copy(EARLY + v - 1)
            act.wait_ge(ld_we, 16 * 4 * E)
            act.wait_ge(at_g, 2 * B)
            silu_up(4)
            high12(0)
            silu_up(5)
            high12(1)
            silu_up(KS)
            for v in range(KS + 1, len(UPS)):
                silu_up(v)
                if v == KS + 1:
                    high12(2)
                if v == KS + 3:
                    act.wait_ge(rt_dif, 1)
                    act.activation(ex[:, :], dif[:, :], ACT.Exp).then_inc(rt_ex, 1)
                if v == KS + 5:
                    act.wait_ge(lg_r, 2)
                    high12(3)
            act.wait_ge(s_h, len(UPS))
            for e in range(E // 2, E):
                high12(e)
            act.wait_ge(rt_done, 1)
            act.wait_ge(w3_z, 1)
            for e in range(E):
                high3(e)

            def x_high(s, j):
                act.wait_ge(sl_tx, s + 1)
                act.activation(sl_xTh[:, j, :].rearrange("p (k c) -> p k c", k=KC), ps[:, 4 * j:4 * j + 2, 384:512],
                               ACT.Copy).then_inc(sl_xh, 1)

            def silu(s, j):
                act.wait_ge(sl_a, s + 1)
                act.activation(sl_s[:, j, :], ps[:, 4 * j, 0:H], ACT.Silu).then_inc(sl_si, 1)

            def h_high(s, j):
                act.wait_ge(sl_th, s + 1)
                act.activation(sl_hTh[:, j, :], ps[:, 4 * j + 2, 0:KH * P], ACT.Copy).then_inc(sl_hh, 1)

            def gated(s, j, first=False):
                act.wait_ge(sl_yp, s + 1)
                if not first:
                    act.wait_ge(sl_add, 16 * (s - 1))
                act.activation(sl_y[:, j, :], ps[:, 4 * j + 3, 0:C], ACT.Copy, scale=gate[:, bass.ds(s, 1)]).then_inc(sl_yr, 1)

            act.wait_ge(s_dn, 3)
            x_high(0, 0)
            x_high(1, 1)
            act.wait_ge(s_dn, TF)
            act.wait_ge(sl_g, 2)

            def act_body(s, j, first=False):
                h_high(s, j)
                x_high(s + 2, j)
                silu(s + 1, 1 - j)
                gated(s, j, first)

            silu(0, 0)
            act_body(0, 0, True)
            act_body(1, 1, True)
            with act.Fori(1, SLOTS // 2 - 1) as i:
                act_body(2 * i, 0)
                act_body(2 * i + 1, 1)
            act_body(SLOTS - 3, 0)
            h_high(SLOTS - 2, 1)
            silu(SLOTS - 1, 0)
            gated(SLOTS - 2, 1)
            h_high(SLOTS - 1, 0)
            gated(SLOTS - 1, 0)

        @block.vector
        def _(dve):
            for c in (0, 2):
                dve.wait_ge(ld_x[c], 32)
                dve.tensor_copy(by_patch(xrs, c), by_row(xst, c)).then_inc(xr_d, 1)
            for q in range(4):
                dve.wait_ge(x_t, q + 1)
                dve.tensor_copy(*patches(q)).then_inc(x_c, 1)
            dve.memset(mv[:, :, :], 0.0).then_inc(st_r, 1)
            dve.wait_ge(st_r, 1)
            dve.wait_ge(ld_tx, 16)
            for b in range(B):
                dve.bn_stats(st[0:NT, TI + b, :], tx[0:NT, b, :]).then_inc(st_r, 1)
            for b in range(B):
                dve.wait_ge(st_r, b + 2)
                dve.bn_aggr(mv[0:NT, TI + b, :], st[0:NT, TI + b, :]).then_inc(mv_r, 1)
            dve.wait_ge(ld_pos, 16 * 3)
            dve.tensor_tensor(posb[:, :], posb[:, :], tokb[:, :], ALU.add).then_inc(posb_r, 1)
            dve.wait_ge(posb_r, 1)
            dve.wait_ge(sd_r, 1)
            dve.reciprocal(rs2[:, TI:TA], rs[:, TI:TA]).then_inc(rs_r, 1)
            dve.wait_ge(rs_r, 1)
            for u in range(TI, TI + DVE_TEXTS):
                dve.tensor_scalar(xn[0:NT, u, :], tx[0:NT, u - TI, :], mv[0:NT, u, 0:1], rs2[0:NT, u:u + 1],
                                  ALU.subtract, ALU.mult).then_inc(xn_r, 1)

            def weight_low(f):
                dve.wait_ge(w_c, f + 1)
                dve.tensor_tensor(wl(f), ps[:, 4 + (f + 2) % 4, :].rearrange("p (a c) -> p a c", a=2), wTh[:, f, :, :],
                                  ALU.subtract).then_inc(w_l, 1)

            def xn_low(f):
                c0, w = turned(f)
                dve.wait_ge(xn_c, f + 1)
                dve.tensor_tensor(parts(xTl)[:, :, c0:c0 + w], ps[:, f % 4, :].rearrange("p (k c) -> p k c", k=KC)[:, :, 0:w],
                                  parts(xTh)[:, :, c0:c0 + w], ALU.subtract).then_inc(xn_l, 1)

            def split(i):
                c, w, m = P1[SPLITS[i]]
                cs = slice(m * T + c * CW, m * T + (c + 1) * CW)
                dve.wait_ge(p1_c, SPLITS[i] + 1)
                dve.tensor_copy((q1Th, k1Th)[w][:, cs], q1s[:, i % 4, :]).then_inc(p1_h, 1)
                dve.wait_ge(p1_h, i + 1)
                dve.tensor_tensor((q1Tl, k1Tl)[w][:, cs], q1s[:, i % 4, :], (q1Th, k1Th)[w][:, cs], ALU.subtract).then_inc(p1_l, 1)

            for i in range(TI):
                dve.wait_ge(emb, i + 1)
                dve.tensor_tensor(hI[:, i, :], ps[:, i, 0:C], posb[:, :], ALU.add).then_inc(hi_r, 1)
                dve.wait_ge(hi_r, i + 1)
                dve.bn_stats(st[:, i, :], hI[:, i, :]).then_inc(st_r, 1)
                dve.wait_ge(st_r, 2 + B + i)
                dve.bn_aggr(mv[:, i, :], st[:, i, :]).then_inc(mv_r, 1)
                if i == 1:
                    for f in range(4):
                        weight_low(f)
                if i == 2:
                    xn_low(0)
                    xn_low(1)
                    weight_low(QW2)
                    weight_low(KW2)
            xn_low(2)
            xn_low(3)
            dve.wait_ge(w_t, 7)
            for x in (xTl, k1Tl, q1Tl):
                dve.memset(x[:, KC * T:XT].bitcast(F32), 0.0).then_inc(pads, 1)
            dve.wait_ge(sd_r, 2)
            dve.reciprocal(rs2[:, 0:TI], rs[:, 0:TI]).then_inc(rs_r, 1)
            dve.wait_ge(rs_r, 2)
            for u in range(TI):
                dve.tensor_scalar(xn[:, u, :], hI[:, u, :], mv[:, u, 0:1], rs2[:, u:u + 1],
                                  ALU.subtract, ALU.mult).then_inc(xn_r, 1)
            dve.wait_ge(h_out, 16 * (1 + B))
            split(0)
            xn_low(4)
            xn_low(5)
            for i in range(1, len(SPLITS)):
                split(i)

            dve.wait_ge(ld_b, 16 * BIASES)

            def soft_in(v):
                r, _c = cols(tile_of(v // 3, v % 3))
                dve.wait_ge(sp, v + 1)
                if v >= 3:
                    dve.wait_ge(sp_q, v - 2)
                dve.tensor_tensor(spy[0:r, v % 3, :], ps[0:r, 4 + v % 2, :], qkb[0:r, :], ALU.add).then_inc(sp_y, 1)

            def soft_out(v):
                r, _c = cols(tile_of(v // 3, v % 3))
                dve.wait_ge(sp_l, v + 1)
                if v >= 6:
                    dve.wait_ge(at_a, 2 * (v // 3 - 1))
                dve.scalar_tensor_tensor(out=qk[0:r, (v // 3) % 2, v % 3, :], in0=spy[0:r, v % 3, :], scalar=0.0,
                                         in1=spa[0:r, v % 3, :], op0=ALU.max, op1=ALU.add).then_inc(sp_q, 1)

            def masked(b):
                j = b % 2
                dve.wait_ge(at_a, b + 1)
                if b >= 2:
                    dve.wait_ge(at_z, b - 1)
                dve.tensor_tensor(mm2[:, j, :], ps[:, j, 0:C], blocks[:, :, :].rearrange("p k c -> p (k c)"), ALU.mult).then_inc(at_m, 1)
                dve.wait_ge(at_m, b + 1)
                dve.tensor_tensor(mm2[:, j, :], mm2[:, j, :], ident2[:, :, :].rearrange("p k c -> p (k c)"), ALU.add).then_inc(at_m2, 1)

            def inverses(gp):
                for j in range(2):
                    dve.wait_ge(at_z, 2 * gp + j + 1)
                    dve.tensor_scalar(zs[:, j, :], ps[:, j, C:C + KC], float(C - 1), None, ALU.add).then_inc(at_zs, 1)
                dve.wait_ge(at_zs, 2 * gp + 2)
                if gp:
                    dve.wait_ge(at_zb, 2 * gp)
                dve.reciprocal(zr[:, :, :], zs[:, :, :]).then_inc(at_r, 1)

            def scaled(b):
                j = b % 2
                dve.wait_ge(at_zb, b + 1)
                if b >= 2:
                    dve.wait_ge(at_o, b - 1)
                dve.tensor_tensor(mm3[:, j, :], ps[:, j, C:2 * C], mm2[:, j, :], ALU.mult).then_inc(at_m3, 1)

            def gate_mix(b):
                j, r = b % 2, (b % 2) * NP
                dve.wait_ge(at_o, b + 1)
                if b == 0:
                    dve.wait_ge(pg_c, TA)
                if b >= 2:
                    dve.wait_ge(mix_out[b - 2], 32)
                dve.tensor_tensor(ogi[r:r + NP, j, :], ps[r:r + NP, 2 + j, 0:C], g[r:r + NP, b // 2, :], ALU.mult).then_inc(at_g, 1)
                dve.tensor_tensor(ogt[0:NT, j, :], ps[0:NT, 2 + j, C:2 * C], g[0:NT, TI + b, :], ALU.mult).then_inc(at_g, 1)

            def shared_low(n):
                dve.wait_ge(ws_h, n + 1)
                dve.tensor_tensor(ws12l[:, n, :, :], ws12[:, n, :, :], ws12h[:, n, :, :], ALU.subtract).then_inc(ws_l, 1)

            def stream(k):
                dve.wait_ge(y_p, k + 1)
                for a, i in enumerate(GROUPS[k]):
                    n = rows_of(i)
                    dve.wait_ge(hb_r, i + 1)
                    dve.tensor_tensor(hb[0:n, i, :], ps[0:n, 7, a * C:(a + 1) * C], hb[0:n, i, :], ALU.add).then_inc(h2_r, 1)
                for i in GROUPS[k]:
                    n = rows_of(i)
                    dve.wait_ge(h2_r, i + 1)
                    dve.bn_stats(st[0:n, i, :], hb[0:n, i, :]).then_inc(st2, 1)
                for i in GROUPS[k]:
                    n = rows_of(i)
                    dve.wait_ge(st2, i + 1)
                    dve.bn_aggr(mv[0:n, i, :], st[0:n, i, :]).then_inc(mv2, 1)

            def normed(k, i0, i1):
                dve.wait_ge(sd2, k + 1)
                dve.reciprocal(rs2[:, i0:i1], rs[:, i0:i1]).then_inc(rs2_r, 1)
                dve.wait_ge(rs2_r, k + 1)
                for i in range(i0, i1):
                    n = rows_of(i)
                    dve.tensor_scalar(xn2[0:n, i, 0:C], hb[0:n, i, :], mv[0:n, i, 0:1], rs2[0:n, i:i + 1],
                                      ALU.subtract, ALU.mult).then_inc(n2, 1)

            for u in range(TA):
                r, _c = cols(u)
                if u == G_FIRST:
                    for v in range(3):
                        soft_in(v)
                dve.wait_ge(pg, u + 1)
                dve.tensor_tensor(g[0:r, u, :], ps[0:r, u % 4, 0:C], gb[0:r, :], ALU.add).then_inc(pg_b, 1)
                if u % 2 == 0 and 1 <= u // 2 <= 3:
                    soft_out(u // 2 - 1)
            for gp in range(TI):
                more = gp + 1 < TI
                v = 3 * gp + 3
                masked(2 * gp)
                masked(2 * gp + 1)
                if more:
                    soft_in(v)
                    soft_in(v + 1)
                inverses(gp)
                if more:
                    soft_in(v + 2)
                    soft_out(v)
                scaled(2 * gp)
                scaled(2 * gp + 1)
                if more:
                    soft_out(v + 1)
                    soft_out(v + 2)
                    if gp >= 1:
                        stream(gp - 1)
                gate_mix(2 * gp)
                gate_mix(2 * gp + 1)
            stream(TI - 2)

            dve.wait_ge(at_o, B)
            dve.memset(lg[:, :, :], 0.0).then_inc(lg_z, 1)
            for x in (x2Th, x2Tl):
                dve.memset(x[:, :, T:TF * P].bitcast(F32), 0.0).then_inc(pads, 1)
            normed(0, 0, EARLY)

            def x2_low(i):
                n = rows_of(i)
                dve.wait_ge(n2_c, i + 1)
                dve.tensor_tensor(x2Tl[:, :, i * P:i * P + n], ps[:, TURN2[i % 2], 0:C].rearrange("p (k c) -> p k c", k=KC)[:, :, 0:n],
                                  x2Th[:, :, i * P:i * P + n], ALU.subtract).then_inc(n2_l, 1)

            shared_low(0)
            x2_low(0)
            x2_low(1)
            shared_low(1)
            stream(TI - 1)
            x2_low(2)
            x2_low(3)
            stream(TI)
            normed(1, EARLY, TF)

            def shared_h(v):
                m, c = UPS[v]
                r = hidden(m)[0]
                w = rows_in(chunk(c))
                if v in LOGITS:
                    dve.wait_ge(s_up, v + 1)
                    dve.tensor_copy(lgT[HS % P:HS % P + E, chunk(c)], ps[HS % P:HS % P + E, PAIR[v % 2], 0:w]).then_inc(lg_t, 1)
                dve.wait_ge(s_sil, v + 1)
                dve.tensor_tensor(hsT[0:r, c, m, 0:w], sil[0:r, v % 2, 0:w], ps[0:r, PAIR[v % 2] + 1, 0:w],
                                  ALU.mult).then_inc(s_h, 1)

            def low12(e):
                dve.wait_ge(we_h, e + 1)
                dve.tensor_tensor(w12l[:, e, :, :], w12[:, e, :, :], w12h[:, e, :, :], ALU.subtract).then_inc(we_l, 1)

            def low3(e):
                dve.wait_ge(we_h, E + e + 1)
                dve.tensor_tensor(w3l[:, e, :, :], w3[:, e, :, :], w3h[:, e, :, :], ALU.subtract).then_inc(we_l, 1)

            shared_h(0)
            for i in range(4, EARLY):
                x2_low(i)
            for v in range(1, KS + 1):
                shared_h(v)
                if EARLY + v - 1 < TF:
                    x2_low(EARLY + v - 1)
            shared_h(KS + 1)
            dve.wait_ge(lg_z, 1)
            dve.wait_ge(r_l, TF)
            full = (TF - 1) * E
            dve.tensor_copy(lg[:, 0:TF - 1, :], ps[:, 4, 0:full].rearrange("p (t e) -> p t e", e=E)).then_inc(lg_r, 1)
            dve.tensor_copy(lg[0:LAST, TF - 1, :], ps[0:LAST, 4, full:full + E]).then_inc(lg_r, 1)
            dve.wait_ge(lg_r, 2)

            steps = [0]

            def then(ins, s=rt):
                steps[0] += 1
                ins.then_inc(rt, 1)
                dve.wait_ge(rt, steps[0])

            def wide(a):
                return a[:, :].unsqueeze(2).broadcast_to([P, TF, E])

            def per_tile(a):
                return a[:, :].unsqueeze(1).broadcast_to([P, TF, E])

            def best(l, mval, mx, oh):
                then(dve.tensor_reduce(mval[:, :], l[:, :, :], AX_X, ALU.max))
                then(dve.tensor_tensor(eq[:, :, :], l[:, :, :], wide(mval), ALU.is_equal))
                then(dve.tensor_tensor(eq[:, :, :], eq[:, :, :], per_tile(e_dn), ALU.mult))
                then(dve.tensor_reduce(mx[:, :], eq[:, :, :], AX_X, ALU.max))
                then(dve.tensor_tensor(oh[:, :, :], eq[:, :, :], wide(mx), ALU.is_equal))

            dve.wait_ge(k_ready, CONSTS)
            best(lg, m1, mx1, oh1)
            then(dve.scalar_tensor_tensor(out=lg2[:, :, :].rearrange("p t e -> p (t e)"),
                                          in0=oh1[:, :, :].rearrange("p t e -> p (t e)"), scalar=-BIG,
                                          in1=lg[:, :, :].rearrange("p t e -> p (t e)"), op0=ALU.mult, op1=ALU.add))
            shared_h(KS + 2)
            best(lg2, m2, mx2, oh2)
            dve.tensor_tensor(both[:, :, :], oh1[:, :, :], oh2[:, :, :], ALU.add).then_inc(rt_both, 1)
            dve.tensor_tensor(dif[:, :], m2[:, :], m1[:, :], ALU.subtract).then_inc(rt_dif, 1)

            shared_h(KS + 3)
            dve.wait_ge(rt_ex, 1)
            then(dve.tensor_scalar(exs[:, :], ex[:, :], 1.0, None, ALU.add))
            then(dve.reciprocal(xn2[:, :, C + 1], exs[:, :]))
            then(dve.tensor_tensor(xn2[:, :, C + 2], ex[:, :], xn2[:, :, C + 1], ALU.mult))
            then(dve.tensor_scalar(xn2[:, :, C + 3], mx1[:, :], -1.0, float(E), ALU.mult, ALU.add))
            then(dve.tensor_copy(xn2[:, :, C], tok_no[:, :]))
            shared_h(KS + 4)
            dve.wait_ge(rt_pre, 1)
            pre = ps[:, 4, RANKS:RANKS + (TF + 1) * E].rearrange("p (t e) -> p t e", e=E)
            then(dve.tensor_copy(cnt[:, :], pre[:, TF, :]))
            then(dve.tensor_tensor(cmpt[:, :, :], cnt[:, :].unsqueeze(2).broadcast_to([P, E, TF]),
                                   tile_at[:, :].unsqueeze(1).broadcast_to([P, E, TF]), ALU.is_gt))
            then(dve.tensor_reduce(ntl[:, :], cmpt[:, :, :], AX_X, ALU.add))
            shared_h(KS + 5)
            then(dve.tensor_tensor(cume[:, :, :], e_lt[:, :, :], ntl[:, :].unsqueeze(1).broadcast_to([P, E, E]), ALU.mult))
            then(dve.tensor_reduce(base[:, :], cume[:, :, :], AX_X, ALU.add))
            then(dve.tensor_tensor(upto[:, :], base[:, :], ntl[:, :], ALU.add))
            then(dve.tensor_scalar(base[:, :], base[:, :], float(P), None, ALU.mult))
            then(dve.tensor_tensor(adr[:, :, :], pre[:, 0:TF, :], per_tile(base), ALU.add))
            shared_h(KS + 6)
            then(dve.tensor_tensor(prd[:, 0, :, :], adr[:, :, :], oh1[:, :, :], ALU.mult))
            then(dve.tensor_tensor(prd[:, 1, :, :], adr[:, :, :], oh2[:, :, :], ALU.mult))
            then(dve.tensor_reduce(posf[:, :, :], prd[:, :, :, :], AX_X, ALU.add))
            dve.tensor_copy(posu[:, :, :], posf[:, :, :]).then_inc(rt_pos, 1)
            shared_h(KS + 7)
            then(dve.tensor_tensor(cmps[:, :, :], upto[:, :].unsqueeze(1).broadcast_to([P, SLOTS, E]),
                                   slot_no[:, :].unsqueeze(2).broadcast_to([P, SLOTS, E]), ALU.is_le))
            then(dve.tensor_reduce(esl[:, :], cmps[:, :, :], AX_X, ALU.add))
            then(dve.tensor_scalar(esl[:, :], esl[:, :], float(E - 1), None, ALU.min))
            dve.tensor_copy(esu[:, :], esl[:, :]).then_inc(rt_done, 1)
            for v in range(KS + 8, len(UPS)):
                shared_h(v)
            def x_low(s, j):
                dve.wait_ge(sl_xh, s + 1)
                dve.tensor_tensor(sl_xTl[:, j, :].rearrange("p (k c) -> p k c", k=KC), ps[:, 4 * j:4 * j + 2, 384:512],
                                  sl_xTh[:, j, :].rearrange("p (k c) -> p k c", k=KC), ALU.subtract).then_inc(sl_xl, 1)

            def gates():
                dve.wait_ge(ld_tail, 16)
                dve.tensor_copy(idx[:, :], tail[:, :, 0]).then_inc(sl_g, 1)
                dve.tensor_tensor(dg[:, :], tail[:, :, 1], tail[:, :, 2], ALU.subtract).then_inc(sl_d, 1)
                dve.tensor_tensor(own[:, :], tail[:, :, 3], esl[:, :], ALU.is_equal).then_inc(sl_d, 1)
                dve.wait_ge(sl_d, 2)
                dve.tensor_tensor(dg[:, :], dg[:, :], own[:, :], ALU.mult).then_inc(sl_d, 1)
                dve.wait_ge(sl_d, 3)
                dve.tensor_tensor(gate[:, :], dg[:, :], tail[:, :, 2], ALU.add).then_inc(sl_g, 1)

            lows = [(low12, e) for e in range(E // 2, E)] + [(low3, e) for e in range(E) if e not in POOL3]
            for i in range(TF):
                if i == TF - 1:
                    x_low(0, 0)
                    gates()
                n = rows_of(i)
                dve.wait_ge(s_dn, i + 1)
                dve.tensor_tensor(hb[0:n, i, :], ps[0:n, DOWN[i % 4], 0:C], hb[0:n, i, :], ALU.add).then_inc(s_o, 1)
                for low, e in lows[i * len(lows) // (TF - 1):(i + 1) * len(lows) // (TF - 1)]:
                    low(e)

            x_low(1, 1)

            def h_low(s, j):
                dve.wait_ge(sl_hh, s + 1)
                dve.tensor_tensor(sl_hTl[:, j, :], ps[:, 4 * j + 2, 0:KH * P], sl_hTh[:, j, :], ALU.subtract).then_inc(sl_hl, 1)

            def h_prod(s, j):
                dve.wait_ge(sl_si, s + 1)
                dve.wait_ge(sl_b, s + 1)
                dve.tensor_tensor(sl_h[:, j, :], sl_s[:, j, :], ps[:, 4 * j + 1, 0:H], ALU.mult).then_inc(sl_hr, 1)

            def dve_body(s, j):
                h_low(s, j)
                x_low(s + 2, j)
                h_prod(s + 1, 1 - j)

            h_prod(0, 0)
            with dve.Fori(0, SLOTS // 2 - 1) as i:
                dve_body(2 * i, 0)
                dve_body(2 * i + 1, 1)
            dve_body(SLOTS - 3, 0)
            h_low(SLOTS - 2, 1)
            h_prod(SLOTS - 1, 0)
            h_low(SLOTS - 1, 0)

        @block.tensor
        def _(pe):
            pe.wait_ge(k_ready, CONSTS)
            pe.wait_ge(ld_wp, 16)
            for f in range(3):
                for kt in (2 * f, 2 * f + 1):
                    c0 = (kt % 2) * (PD // 2) + kt // 2
                    for k in range(KC):
                        ins = pe.transpose(ps[:, f, (kt % 2) * C + k * P:(kt % 2) * C + (k + 1) * P],
                                           wpn[:, k, c0:c0 + 3 * (P - 1) + 1:3], ident[:, :])
                ins.then_inc(wp_t, 1)
            for q, f in enumerate(XORDER):
                if q % 2 == 0:
                    pe.wait_ge(*((xr_d, 1), (xr_d, 2), (xr_a, 1))[q // 2])
                if q >= 4:
                    pe.wait_ge(x_c, q - 3)
                for w in range(4):
                    c0 = ((f % 2) * 4 + w) * P
                    ins = pe.transpose(ps[:, 4 + q % 4, w * P:(w + 1) * P], xrs[:, f // 2, c0:c0 + P], ident[:, :])
                ins.then_inc(x_t, 1)
            def weight_turn(f):
                if f >= 4:
                    pe.wait_ge(w_c, f - 3)
                    pe.wait_ge(w_l, f - 3)
                for k in range(KC):
                    for m in range(KC):
                        ins = pe.transpose(ps[:, 4 + (f + 2) % 4, k * C + m * P:k * C + (m + 1) * P],
                                           wnat[:, f, m, k * P:(k + 1) * P], ident[:, :])
                ins.then_inc(w_t, 1)

            def xn_turn(f):
                r, u0 = (NT, TI + 2 * f) if f < 4 else (P, 2 * (f - 4))
                if f >= 4:
                    pe.wait_ge(xn_r, DVE_TEXTS + 2 * (f - 4) + 2)
                    pe.wait_ge(xn_l, f - 3)
                else:
                    if 2 * f < DVE_TEXTS:
                        pe.wait_ge(xn_r, 2 * f + 2)
                    else:
                        pe.wait_ge(xn_p, 2 * f + 2 - DVE_TEXTS)
                    pe.wait_ge(hi_r, f + 1)
                for k in range(KC):
                    for j in range(2):
                        ins = pe.transpose(ps[:, f % 4, k * C + j * r:k * C + (j + 1) * r],
                                           xn[0:r, u0 + j, k * P:(k + 1) * P], ident[0:r, 0:r])
                ins.then_inc(xn_t, 1)

            pe.wait_ge(x_c, 4)
            pe.wait_ge(x_ca, KP - 4)
            pe.wait_ge(wp_c, 3)
            for i in range(TI):
                for kt in range(KP):
                    ins = pe.matmul(ps[:, i, 0:C], patchT[:, kt, i * P:(i + 1) * P], wpT[:, kt, :],
                                    start=(kt == 0), stop=(kt == KP - 1))
                ins.then_inc(emb, 1)
                if i == 1:
                    pe.wait_ge(ld_wn, 16 * 7)
                    for f in range(4):
                        weight_turn(f)
                if i == 2:
                    xn_turn(0)
                    xn_turn(1)
                    weight_turn(4)
                    weight_turn(5)
            xn_turn(2)
            weight_turn(6)
            xn_turn(3)
            pe.wait_ge(pads, 6)
            for n, (c, w, m) in enumerate(P1):
                if n == 0:
                    pe.wait_ge(xn_l, 4)
                    pe.wait_ge(w_c, 7)
                if n < 4:
                    pe.wait_ge(w_l, min(n + 3, 6))
                if n == IMAGES_AT:
                    xn_turn(4)
                    xn_turn(5)
                if n == len(P1) // NCH:
                    pe.wait_ge(xn_l, 6)
                if n >= 4:
                    pe.wait_ge(p1_c, n - 3)
                for k in range(KC):
                    ms, cs = slice(m * P, (m + 1) * P), slice(k * T + c * CW, k * T + (c + 1) * CW)
                    passes = ((wTh[:, w, k, ms], xTh[:, cs]), (wTh[:, w, k, ms], xTl[:, cs]), (wl(w)[:, k, ms], xTh[:, cs]))
                    for a, (lhs, rhs) in enumerate(passes):
                        ins = pe.matmul(ps[:, 4 + n % 4, 0:CW], lhs, rhs, start=(k + a == 0), stop=(k == KC - 1 and a == 2))
                ins.then_inc(p1, 1)

            def token_major(out, src, cs, w):
                for k in range(KC):
                    c128 = slice(k * T + cs.start, k * T + cs.start + P)
                    passes = ((src[0], wTh[:, w, k, :]), (src[0], wl(w)[:, k, :]), (src[1], wTh[:, w, k, :]))
                    for a, (lhs, rhs) in enumerate(passes):
                        ins = pe.matmul(out, lhs[:, c128], rhs, start=(k + a == 0), stop=(k == KC - 1 and a == 2))
                return ins

            def layer2(v):
                cs = cols(tile_of(v // 3, v % 3))[1]
                if v >= 2:
                    pe.wait_ge(sp_y, v - 1)
                for n, (src, w) in enumerate((((q1Th, q1Tl), QW2), ((k1Th, k1Tl), KW2))):
                    ins = token_major(ps[:, 4 + v % 2, n * C:(n + 1) * C], src, cs, w)
                ins.then_inc(sp, 1)

            def gram(b):
                s, r = (b // 2) % 2, (b % 2) * NP
                pe.wait_ge(sp_q, 3 * (b // 2) + 3)
                if b >= 2:
                    pe.wait_ge(at_m3, b - 1)
                for m in range(KC):
                    qc, kc = slice(m * P, (m + 1) * P), slice(C + m * P, C + (m + 1) * P)
                    pe.matmul(ps[:, b % 2, qc], qk[r:r + NP, s, 0, kc], qk[r:r + NP, s, 0, qc], start=True, stop=False)
                    ins = pe.matmul(ps[:, b % 2, qc], qk[0:NT, s, 1 + b % 2, kc], qk[0:NT, s, 1 + b % 2, qc],
                                    start=False, stop=True)
                ins.then_inc(at_a, 1)

            def sums(b):
                pe.wait_ge(at_m2, b + 1)
                for m in range(KC):
                    ins = pe.matmul(ps[:, b % 2, C + m:C + m + 1], mm2[:, b % 2, m * P:(m + 1) * P], ones[:, 0:1],
                                    start=True, stop=True)
                ins.then_inc(at_z, 1)

            def spread(b):
                pe.wait_ge(at_r, b // 2 + 1)
                for m in range(KC):
                    ins = pe.matmul(ps[:, b % 2, C + m * P:C + (m + 1) * P], zr[:, b % 2, m:m + 1].broadcast_to([P, P]),
                                    ident[:, :], start=True, stop=True)
                ins.then_inc(at_zb, 1)

            def mixed(b):
                r = (b % 2) * NP
                if b == 0:
                    pe.wait_ge(pg_b, TA)
                pe.wait_ge(at_m3, b + 1)
                if b >= 2:
                    pe.wait_ge(at_g, 2 * (b - 1))
                for m in range(KC):
                    cs = slice(m * P, (m + 1) * P)
                    pe.matmul(ps[r:r + NP, 2 + b % 2, cs], vT[:, m, b * NP:(b + 1) * NP], mm3[:, b % 2, cs], start=True, stop=True)
                for m in range(KC):
                    cs = slice(m * P, (m + 1) * P)
                    ins = pe.matmul(ps[0:NT, 2 + b % 2, C + m * P:C + (m + 1) * P], vT[:, m, cols(TI + b)[1]],
                                    mm3[:, b % 2, cs], start=True, stop=True)
                ins.then_inc(at_o, 1)

            def mix_turn(k):
                for a, i in enumerate(GROUPS[k]):
                    n = rows_of(i)
                    pe.wait_ge(ld_xs[i], 16)
                    if k >= 1:
                        pe.wait_ge(xs_c, k)
                    for c in range(KC):
                        ins = pe.transpose(ps[:, 6, a * C + c * P:a * C + c * P + n], xs[0:n, i % XS, c * P:(c + 1) * P], ident[0:n, 0:n])
                    if n < P:
                        for c in range(KC):
                            ins = pe.transpose(ps[:, 6, c * P + n:(c + 1) * P], xs[0:P - n, i % XS, c * P:(c + 1) * P],
                                               ident[0:P - n, 0:P - n])
                ins.then_inc(xs_t, 1)

            def project(k):
                pe.wait_ge(xs_c, k + 1)
                if k >= 1:
                    pe.wait_ge(h2_r, GROUPS[k][0])
                for a, i in enumerate(GROUPS[k]):
                    n = rows_of(i)
                    for c in range(KC):
                        ins = pe.matmul(ps[0:n, 7, a * C:(a + 1) * C], xsT[:, a, c * P:c * P + n], pwT[:, c, :],
                                        start=(c == 0), stop=(c == KC - 1))
                ins.then_inc(y_p, 1)

            def turn2(i):
                n = rows_of(i)
                pe.wait_ge(n2, i + 1)
                if i >= 2:
                    pe.wait_ge(n2_l, i - 1)
                for c in range(KC):
                    ins = pe.transpose(ps[:, TURN2[i % 2], c * P:c * P + n], xn2[0:n, i, c * P:(c + 1) * P], ident[0:n, 0:n])
                ins.then_inc(n2_t, 1)

            def logits(i):
                n, u0 = rows_of(i), HS % P
                pe.wait_ge(lg_t, i * P // SW + 1)
                ins = pe.transpose(ps[0:n, 4, i * E:(i + 1) * E], lgT[u0:u0 + E, i * P:i * P + n], ident[u0:u0 + E, u0:u0 + E])
                ins.then_inc(r_l, 1)

            for u in range(TA):
                if u == G_FIRST:
                    pe.wait_ge(p1_c, len(P1))
                    pe.wait_ge(p1_l, len(SPLITS))
                    for v in range(3):
                        layer2(v)
                if u >= 4:
                    pe.wait_ge(pg_b, u - 3)
                token_major(ps[:, u % 4, 0:C], (xTh, xTl), cols(u)[1], GW).then_inc(pg, 1)
            pe.wait_ge(pg_b, TA - 2)
            for gp in range(TI):
                more = gp + 1 < TI
                v = 3 * gp + 3
                gram(2 * gp)
                gram(2 * gp + 1)
                if more:
                    layer2(v)
                    layer2(v + 1)
                sums(2 * gp)
                sums(2 * gp + 1)
                if more:
                    layer2(v + 2)
                if gp >= 1 and more:
                    mix_turn(gp - 1)
                spread(2 * gp)
                spread(2 * gp + 1)
                if gp >= 1 and more:
                    project(gp - 1)
                mixed(2 * gp)
                mixed(2 * gp + 1)

            def shared_up(v):
                m, c = UPS[v]
                ms, cs = hidden(m)[1], chunk(c)
                pe.wait_ge(n2_l, min(3 * (c + 1), TF))
                if v >= 2:
                    pe.wait_ge(s_h, v - 1)
                for n in range(2):
                    if v == 0:
                        pe.wait_ge(ws_l, n + 1)
                    for k in range(KC):
                        passes = ((ws12h, x2Th), (ws12h, x2Tl), (ws12l, x2Th))
                        for a, (lhs, rhs) in enumerate(passes):
                            ins = pe.matmul(ps[:, PAIR[v % 2] + n, 0:rows_in(cs)], lhs[:, n, k, ms], rhs[:, k, cs],
                                            start=(k + a == 0), stop=(k == KC - 1 and a == 2))
                ins.then_inc(s_up, 1)

            pe.wait_ge(sp_y, 3 * TI)
            mix_turn(TI - 2)
            project(TI - 2)
            mix_turn(TI - 1)
            turn2(0)
            turn2(1)
            project(TI - 1)
            turn2(2)
            turn2(3)
            mix_turn(TI)
            project(TI)
            pe.wait_ge(pads, 8)
            pe.wait_ge(at_m3, B)
            pe.wait_ge(at_g, 2 * B)
            shared_up(0)
            for i in range(4, EARLY):
                turn2(i)
            for v in range(1, KS + 1):
                shared_up(v)
                if EARLY + v - 1 < TF:
                    turn2(EARLY + v - 1)
            shared_up(KS + 1)
            shared_up(KS + 2)
            for i in range(TF):
                logits(i)
            for v in range(KS + 3, KS + 5):
                shared_up(v)
            pe.wait_ge(rt_both, 1)
            full = (TF - 1) * E
            flat = both[:, :, :].rearrange("p t e -> p (t e)")
            pe.matmul(ps[:, 4, RANKS:RANKS + full], before[:, :], flat[:, 0:full], start=True, stop=False, skip_group_check=True)
            pe.matmul(ps[:, 4, RANKS + full:RANKS + full + E], before[0:LAST, :], flat[0:LAST, full:full + E], start=False, stop=False, skip_group_check=True)
            for t in range(TF):
                n = rows_of(t)
                ins = pe.matmul(ps[:, 4, RANKS + (t + 1) * E:RANKS + (TF + 1) * E], ones[0:n, :],
                                both[0:n, t, :].unsqueeze(1).broadcast_to([n, TF - t, E]),
                                start=False, stop=(t == TF - 1), skip_group_check=True)
            ins.then_inc(rt_pre, 1)
            for v in range(KS + 5, len(UPS)):
                shared_up(v)
            def x_turn(s, j, i):
                pe.wait_ge(sl_ld[j], 16 * (i + 1))
                for k in range(KC):
                    ins = pe.transpose(ps[:, 4 * j + k, 384:512], sl_x[:, j, k * P:(k + 1) * P], ident[:, :])
                ins.then_inc(sl_tx, 1)

            def expert(s):
                return pe.value_load(esu[0:1, bass.ds(s, 1)], min_val=0, max_val=E - 1)

            pe.wait_ge(rt_done, 1)
            first_expert = expert(0)
            for i in range(TF):
                n = rows_of(i)
                c, c0 = i * P // SW, i * P % SW
                if i % 3 == 0:
                    pe.wait_ge(s_h, CHUNK_DONE[c])
                if i >= 4:
                    pe.wait_ge(s_o, i - 3)
                for k in range(KS):
                    r = hidden(k)[0]
                    ins = pe.matmul(ps[0:n, DOWN[i % 4], 0:C], hsT[0:r, c, k, c0:c0 + n], ws3[0:r, k, :],
                                    start=(k == 0), stop=(k == KS - 1))
                ins.then_inc(s_dn, 1)
                if i == TF - 2:
                    x_turn(0, 0, 0)

            def up(s, j, e):
                pe.wait_ge(sl_xl, s + 1)
                for n, done in ((0, sl_a), (1, sl_b)):
                    for k in range(KC):
                        at12 = bass.ds(e * (KC * 2 * H) + k * 2 * H + n * H, H)
                        for x, w in ((sl_xTh, w12hf), (sl_xTh, w12lf), (sl_xTl, w12hf)):
                            ins = pe.matmul(ps[:, 4 * j + n, 0:H], x[:, j, k * P:(k + 1) * P], w[:, at12],
                                            start=(k == 0 and w is w12hf and x is sl_xTh), stop=(k == KC - 1 and x is sl_xTl))
                    ins.then_inc(done, 1)

            def h_turn(s, j):
                pe.wait_ge(sl_hr, s + 1)
                for k in range(KH):
                    c0 = min(k * P, H - P)
                    ins = pe.transpose(ps[:, 4 * j + 2, k * P:(k + 1) * P], sl_h[:, j, c0:c0 + P], ident[:, :])
                ins.then_inc(sl_th, 1)

            def down(s, j, e, first=False):
                pe.wait_ge(sl_hl, s + 1)
                if not first:
                    pe.wait_ge(sl_yr, s - 1)
                for k in range(KH):
                    at3 = bass.ds(e * (KH * C) + k * C, C)
                    for h, w in ((sl_hTh, w3hf), (sl_hTh, w3lf), (sl_hTl, w3hf)):
                        ins = pe.matmul(ps[:, 4 * j + 3, 0:C], h[:, j, k * P:(k + 1) * P], w[:, at3],
                                        start=(k == 0 and w is w3hf and h is sl_hTh), stop=(k == KH - 1 and h is sl_hTl))
                ins.then_inc(sl_yp, 1)

            w12hf, w12lf = (w[:, :, :, :].rearrange("p e k h -> p (e k h)") for w in (w12h, w12l))
            w3hf, w3lf = (w[:, :, :, :].rearrange("p e k c -> p (e k c)") for w in (w3h, w3l))

            pe.wait_ge(we_l, 2 * E - len(POOL12) - len(POOL3))
            pe.wait_ge(we_p, len(POOL12) + len(POOL3))
            pe.wait_ge(s_o, TF - 1)
            x_turn(1, 1, 0)
            up(0, 0, first_expert)
            pe.wait_ge(s_o, TF)

            def pe_body(s, j, i, first=False, turn=True, more=True):
                e_next = expert(s + 1) if more else None
                h_turn(s, j)
                if turn:
                    x_turn(s + 2, j, i + 1)
                if more:
                    up(s + 1, 1 - j, e_next)
                down(s, j, expert(s), first)

            pe_body(0, 0, 0, True)
            pe_body(1, 1, 0, True)
            assert (SLOTS // 2 - 2) % 2 == 0
            with pe.Fori(0, (SLOTS // 2 - 2) // 2) as i:
                for k in range(2):
                    pe_body(4 * i + 2 * k + 2, 0, 2 * i + k + 1)
                    pe_body(4 * i + 2 * k + 3, 1, 2 * i + k + 1)
            i = SLOTS // 2 - 1
            pe_body(2 * i, 0, i)
            pe_body(2 * i + 1, 1, i, turn=False)
            pe_body(2 * i + 2, 0, i + 1, turn=False, more=False)


_INS = ['x', 'txt', 'L0_tok_Wp', 'L0_tok_b', 'L0_attn_q_w1', 'L0_attn_q_b1', 'L0_attn_q_w2', 'L0_attn_q_b2',
        'L0_attn_k_w1', 'L0_attn_k_b1', 'L0_attn_k_w2', 'L0_attn_k_b2', 'L0_attn_v_w', 'L0_attn_v_b',
        'L0_attn_g_w', 'L0_attn_g_b', 'L0_attn_p_w', 'L0_attn_p_b', 'L0_ffn_Wg', 'L0_ffn_W1', 'L0_ffn_W2',
        'L0_ffn_W3', 'L0_ffn_Ws1', 'L0_ffn_Ws2', 'L0_ffn_Ws3']


def position_table():
    import numpy as np
    side, quarter = IMG // PATCH, C // 4
    gh, gw = np.meshgrid(np.arange(side), np.arange(side), indexing="ij")
    factor = np.float32(10000.0) ** (np.arange(quarter, dtype=np.float32) / np.float32(quarter))
    h = gh.reshape(-1).astype(np.float32)[:, None] / factor
    w = gw.reshape(-1).astype(np.float32)[:, None] / factor
    return np.concatenate([np.sin(h), np.cos(h), np.sin(w), np.cos(w)], axis=-1).astype(np.float32)


def kernel(**inputs):
    import numpy as _np
    import concourse.bacc as _bacc
    from concourse import mybir as _mybir
    from concourse.bass_utils import run_bass_kernel_spmd as _run

    nc = _bacc.Bacc("TRN2", target_bir_lowering=False, num_devices=1)
    arrays, args = {}, []
    for name, a in [(n, inputs[n]) for n in _INS] + [("pos", position_table())]:
        a = _np.ascontiguousarray(a)
        arrays[f"in_{name}_dram"] = a
        args.append(nc.dram_tensor(f"in_{name}_dram", a.shape, _mybir.dt.from_np(a.dtype), kind="ExternalInput").ap())
    args.append(nc.dram_tensor("out_0_dram", (B, N, C), _mybir.dt.float32, kind="ExternalOutput").ap())
    fused_layer(nc, *args)
    r = _run(nc, [arrays], core_ids=[0])
    return r.results[0]["out_0_dram"]
```
